# Optimizing a Trainium2 kernel written in Bass

```python
import numpy as np
import jax
import jax.numpy as jnp

def _softmax(x, axis=-1):
    return jax.nn.softmax(x, axis=axis)

def _gelu(x):
    return jax.nn.gelu(x, approximate=True)

def _silu(x):
    return jax.nn.silu(x)

def _sigmoid(x):
    return jax.nn.sigmoid(x)

def _layernorm(x, axis=-1, eps=1e-05):
    m = jnp.mean(x, axis=axis, keepdims=True)
    v = jnp.var(x, axis=axis, keepdims=True)
    return (x - m) / jnp.sqrt(v + eps)

def _scatter_add(tgt, idx, src, axis=0):
    return tgt.at[idx].add(src)

def _segment_sum(src, seg, n):
    return jax.ops.segment_sum(src, seg, n)
kernel_name = 'mk_flamingo_gated_d2_seqx_r2_8e8914'

def setup_inputs(seed: int=0):
    np.random.seed(seed)
    _w = jnp.asarray

    def _rec_inputs():
        import jax
        import jax.numpy as jnp
        _rk = jax.random.key(seed)
        x = -0.0002928 + 1 * jax.random.normal(jax.random.fold_in(_rk, 1), (2, 2048, 512), jnp.float32)
        _lenS = 2048 - jax.random.randint(jax.random.fold_in(_rk, 7), (2,), 0, max(1, 2048 // 4) + 1, jnp.int32)
        _lenS2 = 154 - jax.random.randint(jax.random.fold_in(_rk, 8), (2,), 0, max(1, 154 // 4) + 1, jnp.int32)
        _ctx_1024P = jax.random.normal(jax.random.fold_in(_rk, 11), (2, 16, 512), jnp.float32)
        _ctx_1024c = jax.random.dirichlet(jax.random.fold_in(_rk, 511), 0.3 * jnp.ones((16,), jnp.float32), (2, 154))
        _ctx_1024t = jnp.einsum('bsk,bkd->bsd', _ctx_1024c, _ctx_1024P)
        _ctx_1024t = _ctx_1024t * jax.lax.rsqrt(jnp.mean(jnp.square(_ctx_1024t)) + 1e-12) * 0.953939
        ctx_1024 = -1.39393e-06 + 0.999914 * (_ctx_1024t + 0.3 * jax.random.normal(jax.random.fold_in(_rk, 611), (2, 154, 512), jnp.float32))
        _validS = jnp.arange(2048)[None, :] < _lenS[:, None]
        _validS2 = jnp.arange(154)[None, :] < _lenS2[:, None]
        _causal = jnp.tril(jnp.ones((2048, 2048), dtype=bool))
        mask_Bx1xSxS2_ik1 = jnp.where(jnp.broadcast_to(_validS2[:, None, None, :], (2, 1, 2048, 154)), 1, 0).astype(jnp.int32)
        _g = jax.random.normal(jax.random.fold_in(_rk, 9001), (2, 2), jnp.float32)
        _g = jnp.sign(_g) * jnp.maximum(jnp.abs(_g), 1.0) + (_g == 0) * 1.0
        g_xattn = _g[0]
        g_ffn = _g[1]
        return (x, ctx_1024, mask_Bx1xSxS2_ik1, g_xattn, g_ffn)
    x, ctx_1024, mask_Bx1xSxS2_ik1, g_xattn, g_ffn = _rec_inputs()

    def _L0_xattn_setup():
        import jax, jax.numpy as jnp
        import numpy as np
        DIM = 512
        HEADS = 16
        HEAD_DIM = DIM // HEADS
        key = jax.random.key(seed)
        ks = jax.random.split(key, 12)
        B, Tq, Tk = (2, 1024, 1024)
        inp = {'query': jax.random.normal(ks[0], (B, Tq, DIM), jnp.float32), 'key': jax.random.normal(ks[1], (B, Tk, DIM), jnp.float32), 'value': jax.random.normal(ks[2], (B, Tk, DIM), jnp.float32), 'mask': jax.random.randint(ks[3], (B, 1, Tq, Tk), 0, 2, jnp.int32), 'wq': jax.random.uniform(ks[4], (DIM, DIM), jnp.float32, -1.0, 1.0) * np.sqrt(6.0 / (2 * DIM)), 'wk': jax.random.uniform(ks[5], (DIM, DIM), jnp.float32, -1.0, 1.0) * np.sqrt(6.0 / (2 * DIM)), 'wv': jax.random.uniform(ks[6], (DIM, DIM), jnp.float32, -1.0, 1.0) * np.sqrt(6.0 / (2 * DIM)), 'wo': jax.random.uniform(ks[7], (DIM, DIM), jnp.float32, -1.0, 1.0) * np.sqrt(6.0 / (2 * DIM)), 'bq': jnp.zeros((DIM,), jnp.float32), 'bk': jnp.zeros((DIM,), jnp.float32), 'bv': jnp.zeros((DIM,), jnp.float32), 'bo': jnp.zeros((DIM,), jnp.float32)}
        return inp
    _L0_xattn_all = _L0_xattn_setup()
    _L0_xattn_in = {k: v for k, v in _L0_xattn_all.items() if k in ('wq', 'wk', 'wv', 'wo', 'bq', 'bk', 'bv', 'bo')}
    del _L0_xattn_all

    def _L0_ffn_setup():
        import jax, jax.numpy as jnp
        import numpy as np
        TOP_K = 8
        CAPACITY = 256

        def _silu(x):
            return x * jax.nn.sigmoid(x)
        key = jax.random.key(seed)
        ks = jax.random.split(key, 7)
        B, S, H, E, I, Is = (2, 512, 512, 64, 256, 1024)
        s = 0.05
        return {'hidden_states': jax.random.normal(ks[0], (B, S, H), jnp.float32), 'gate_w': jax.random.normal(ks[1], (H, E), jnp.float32) * s, 'shared_gate_w': jax.random.normal(ks[2], (H, 1), jnp.float32) * s, 'shared_gate_up_w': jax.random.normal(ks[3], (H, 2 * Is), jnp.float32) * s, 'shared_down_w': jax.random.normal(ks[4], (Is, H), jnp.float32) * s, 'expert_gate_up_w': jax.random.normal(ks[5], (E, H, 2 * I), jnp.float32) * s, 'expert_down_w': jax.random.normal(ks[6], (E, I, H), jnp.float32) * s}
    _L0_ffn_all = _L0_ffn_setup()
    _L0_ffn_in = {k: v for k, v in _L0_ffn_all.items() if k in ('gate_w', 'shared_gate_w', 'shared_gate_up_w', 'shared_down_w', 'expert_gate_up_w', 'expert_down_w')}
    del _L0_ffn_all

    def _L1_xattn_setup():
        import jax, jax.numpy as jnp
        import numpy as np
        D_MODEL = 512
        NUM_HEADS = 16
        DEPTH = D_MODEL // NUM_HEADS
        key = jax.random.key(seed)
        ks = jax.random.split(key, 6)
        B, S = (2, 1024)
        scale = 1.0 / np.sqrt(D_MODEL)
        return {'q': jax.random.normal(ks[0], (B, S, D_MODEL), jnp.float32), 'k': jax.random.normal(ks[1], (B, S, D_MODEL), jnp.float32), 'v': jax.random.normal(ks[2], (B, S, D_MODEL), jnp.float32), 'wq': jax.random.normal(ks[3], (D_MODEL, D_MODEL), jnp.float32) * scale, 'wk': jax.random.normal(ks[4], (D_MODEL, D_MODEL), jnp.float32) * scale, 'wv': jax.random.normal(ks[5], (D_MODEL, D_MODEL), jnp.float32) * scale}
    _L1_xattn_all = _L1_xattn_setup()
    _L1_xattn_in = {k: v for k, v in _L1_xattn_all.items() if k in ('wq', 'wk', 'wv')}
    del _L1_xattn_all

    def _L1_ffn_setup():
        import jax, jax.numpy as jnp
        import numpy as np
        B, T, D, R, KEXP = (4, 2048, 512, 64, 8)
        RH = max(D, 32)
        SCALE = 0.02

        def _fused_branch(Q_side, K_side, V, W, U, b, router_w1, router_b1, router_w2, router_b2, expert_bias):
            xV = jnp.einsum('btd,kdr->btkr', Q_side, V)
            yW = jnp.einsum('btd,kdr->btkr', K_side, W)
            cum_yW = jnp.cumsum(yW, axis=1)
            prod = xV * cum_yW
            h = jax.nn.gelu(Q_side @ router_w1.T + router_b1, approximate=False)
            logits = h @ router_w2.T + router_b2 + expert_bias
            weights = jax.nn.softmax(logits, axis=-1)
            out = jnp.einsum('btkr,kdr->btd', prod * weights[..., None], U)
            out = out + weights @ b
            n_valid = jnp.arange(1, Q_side.shape[1] + 1, dtype=Q_side.dtype)
            return out / n_valid[None, :, None]
        key = jax.random.key(seed)
        ks = jax.random.split(key, 20)
        x = jax.random.normal(ks[0], (B, T, D), dtype=jnp.float32)
        W_Q = jax.random.normal(ks[1], (D, D), dtype=jnp.float32) * (1.0 / np.sqrt(D))
        W_K = jax.random.normal(ks[2], (D, D), dtype=jnp.float32) * (1.0 / np.sqrt(D))
        W_O = jax.random.normal(ks[3], (D, D), dtype=jnp.float32) * (1.0 / np.sqrt(D))
        W_inv = jnp.eye(D, dtype=jnp.float32) + 0.01 * jax.random.normal(ks[4], (D, D), dtype=jnp.float32)
        V_fwd = jax.random.normal(ks[5], (KEXP, D, R), dtype=jnp.float32) * SCALE
        W_fwd = jax.random.normal(ks[6], (KEXP, D, R), dtype=jnp.float32) * SCALE
        U_fwd = jax.random.normal(ks[7], (KEXP, D, R), dtype=jnp.float32) * SCALE
        b_fwd = jnp.zeros((KEXP, D), dtype=jnp.float32)
        V_inv = jax.random.normal(ks[8], (KEXP, D, R), dtype=jnp.float32) * SCALE
        W_inv_exp = jax.random.normal(ks[9], (KEXP, D, R), dtype=jnp.float32) * SCALE
        U_inv = jax.random.normal(ks[10], (KEXP, D, R), dtype=jnp.float32) * SCALE
        b_inv = jnp.zeros((KEXP, D), dtype=jnp.float32)
        router_w1 = jax.random.normal(ks[11], (RH, D), dtype=jnp.float32) * (1.0 / np.sqrt(D))
        router_b1 = jnp.zeros((RH,), dtype=jnp.float32)
        router_w2 = jax.random.normal(ks[12], (KEXP, RH), dtype=jnp.float32) * (1.0 / np.sqrt(RH))
        router_b2 = jnp.zeros((KEXP,), dtype=jnp.float32)
        alpha_bi = jnp.asarray(0.5, dtype=jnp.float32)
        expert_bias = jnp.zeros((KEXP,), dtype=jnp.float32)
        return dict(x=x, W_Q=W_Q, W_K=W_K, W_O=W_O, W_inv=W_inv, V_fwd=V_fwd, W_fwd=W_fwd, U_fwd=U_fwd, b_fwd=b_fwd, V_inv=V_inv, W_inv_exp=W_inv_exp, U_inv=U_inv, b_inv=b_inv, router_w1=router_w1, router_b1=router_b1, router_w2=router_w2, router_b2=router_b2, alpha_bi=alpha_bi, expert_bias=expert_bias)
    _L1_ffn_all = _L1_ffn_setup()
    _L1_ffn_in = {k: v for k, v in _L1_ffn_all.items() if k in ('W_Q', 'W_K', 'W_O', 'W_inv', 'V_fwd', 'W_fwd', 'U_fwd', 'b_fwd', 'V_inv', 'W_inv_exp', 'U_inv', 'b_inv', 'router_w1', 'router_b1', 'router_w2', 'router_b2', 'alpha_bi', 'expert_bias')}
    del _L1_ffn_all
    return {'x': x, 'ctx_1024': ctx_1024, 'mask_Bx1xSxS2_ik1': mask_Bx1xSxS2_ik1, 'g_xattn': g_xattn, 'g_ffn': g_ffn, 'L0_xattn_wq': _L0_xattn_in['wq'], 'L0_xattn_wk': _L0_xattn_in['wk'], 'L0_xattn_wv': _L0_xattn_in['wv'], 'L0_xattn_wo': _L0_xattn_in['wo'], 'L0_xattn_bq': _L0_xattn_in['bq'], 'L0_xattn_bk': _L0_xattn_in['bk'], 'L0_xattn_bv': _L0_xattn_in['bv'], 'L0_xattn_bo': _L0_xattn_in['bo'], 'L0_ffn_gate_w': _L0_ffn_in['gate_w'], 'L0_ffn_shared_gate_w': _L0_ffn_in['shared_gate_w'], 'L0_ffn_shared_gate_up_w': _L0_ffn_in['shared_gate_up_w'], 'L0_ffn_shared_down_w': _L0_ffn_in['shared_down_w'], 'L0_ffn_expert_gate_up_w': _L0_ffn_in['expert_gate_up_w'], 'L0_ffn_expert_down_w': _L0_ffn_in['expert_down_w'], 'L1_xattn_wq': _L1_xattn_in['wq'], 'L1_xattn_wk': _L1_xattn_in['wk'], 'L1_xattn_wv': _L1_xattn_in['wv'], 'L1_ffn_W_Q': _L1_ffn_in['W_Q'], 'L1_ffn_W_K': _L1_ffn_in['W_K'], 'L1_ffn_W_O': _L1_ffn_in['W_O'], 'L1_ffn_W_inv': _L1_ffn_in['W_inv'], 'L1_ffn_V_fwd': _L1_ffn_in['V_fwd'], 'L1_ffn_W_fwd': _L1_ffn_in['W_fwd'], 'L1_ffn_U_fwd': _L1_ffn_in['U_fwd'], 'L1_ffn_b_fwd': _L1_ffn_in['b_fwd'], 'L1_ffn_V_inv': _L1_ffn_in['V_inv'], 'L1_ffn_W_inv_exp': _L1_ffn_in['W_inv_exp'], 'L1_ffn_U_inv': _L1_ffn_in['U_inv'], 'L1_ffn_b_inv': _L1_ffn_in['b_inv'], 'L1_ffn_router_w1': _L1_ffn_in['router_w1'], 'L1_ffn_router_b1': _L1_ffn_in['router_b1'], 'L1_ffn_router_w2': _L1_ffn_in['router_w2'], 'L1_ffn_router_b2': _L1_ffn_in['router_b2'], 'L1_ffn_alpha_bi': _L1_ffn_in['alpha_bi'], 'L1_ffn_expert_bias': _L1_ffn_in['expert_bias']}

def reference(x, ctx_1024, mask_Bx1xSxS2_ik1, g_xattn, g_ffn, L0_xattn_wq, L0_xattn_wk, L0_xattn_wv, L0_xattn_wo, L0_xattn_bq, L0_xattn_bk, L0_xattn_bv, L0_xattn_bo, L0_ffn_gate_w, L0_ffn_shared_gate_w, L0_ffn_shared_gate_up_w, L0_ffn_shared_down_w, L0_ffn_expert_gate_up_w, L0_ffn_expert_down_w, L1_xattn_wq, L1_xattn_wk, L1_xattn_wv, L1_ffn_W_Q, L1_ffn_W_K, L1_ffn_W_O, L1_ffn_W_inv, L1_ffn_V_fwd, L1_ffn_W_fwd, L1_ffn_U_fwd, L1_ffn_b_fwd, L1_ffn_V_inv, L1_ffn_W_inv_exp, L1_ffn_U_inv, L1_ffn_b_inv, L1_ffn_router_w1, L1_ffn_router_b1, L1_ffn_router_w2, L1_ffn_router_b2, L1_ffn_alpha_bi, L1_ffn_expert_bias):
    import jax
    import jax.numpy as jnp

    def _L0_xattn_ref(query, key, value, mask, wq, wk, wv, wo, bq, bk, bv, bo):
        import jax, jax.numpy as jnp
        import numpy as np
        DIM = 512
        HEADS = 16
        HEAD_DIM = DIM // HEADS
        B, Tq, C = query.shape
        Tk = key.shape[1]
        scale = 1.0 / np.sqrt(HEAD_DIM)
        q = (query @ wq.T + bq).reshape(B, Tq, HEADS, HEAD_DIM).transpose(0, 2, 1, 3)
        k = (key @ wk.T + bk).reshape(B, Tk, HEADS, HEAD_DIM).transpose(0, 2, 1, 3)
        v = (value @ wv.T + bv).reshape(B, Tk, HEADS, HEAD_DIM).transpose(0, 2, 1, 3)
        scores = jnp.einsum('bhqd,bhkd->bhqk', q, k) * scale
        scores = jnp.clip(scores, -100.0, 100.0)
        scores = jnp.where(mask == 0, -jnp.inf, scores)
        attn = jax.nn.softmax(scores, axis=-1)
        out = jnp.einsum('bhqk,bhkd->bhqd', attn, v)
        out = out.transpose(0, 2, 1, 3).reshape(B, Tq, HEADS * HEAD_DIM)
        return out @ wo.T + bo

    def _L0_ffn_ref(hidden_states, gate_w, shared_gate_w, shared_gate_up_w, shared_down_w, expert_gate_up_w, expert_down_w):
        import jax, jax.numpy as jnp
        import numpy as np
        TOP_K = 8
        CAPACITY = 256

        def _silu(x):
            return x * jax.nn.sigmoid(x)
        B, S, H = hidden_states.shape
        x = hidden_states.reshape(-1, H)
        T = x.shape[0]
        E = gate_w.shape[1]
        Is = shared_gate_up_w.shape[1] // 2
        I = expert_gate_up_w.shape[2] // 2
        gu = x @ shared_gate_up_w
        shared = _silu(gu[:, :Is]) * gu[:, Is:] @ shared_down_w
        shared = shared * jax.nn.sigmoid(x @ shared_gate_w)
        logits = x @ gate_w
        probs = jax.nn.softmax(logits.astype(jnp.float32), axis=-1)
        w, idx = jax.lax.top_k(probs, TOP_K)
        w = (w / jnp.sum(w, axis=-1, keepdims=True)).astype(x.dtype)
        e_flat = idx.reshape(-1)
        w_flat = w.reshape(-1)
        A = e_flat.shape[0]
        tok = jnp.arange(A) // TOP_K
        onehot = jax.nn.one_hot(e_flat, E, dtype=jnp.int32)
        pos = jnp.take_along_axis(jnp.cumsum(onehot, axis=0) - 1, e_flat[:, None], axis=1)[:, 0]
        slot = jnp.minimum(pos, CAPACITY)
        buf = jnp.zeros((E, CAPACITY + 1, H), x.dtype).at[e_flat, slot].set(x[tok])
        gu_e = jnp.einsum('ech,ehf->ecf', buf, expert_gate_up_w)
        act = _silu(gu_e[..., :I]) * gu_e[..., I:]
        out_e = jnp.einsum('eci,eih->ech', act, expert_down_w)
        y = out_e[e_flat, slot] * w_flat[:, None]
        y = jnp.where((pos < CAPACITY)[:, None], y, jnp.zeros_like(y))
        y = y.reshape(T, TOP_K, H).sum(axis=1)
        return (y + shared).reshape(B, S, H)

    def _L1_xattn_ref(q, k, v, wq, wk, wv):
        import jax, jax.numpy as jnp
        import numpy as np
        D_MODEL = 512
        NUM_HEADS = 16
        DEPTH = D_MODEL // NUM_HEADS
        B, S, _ = q.shape

        def split(x):
            return x.reshape(B, -1, NUM_HEADS, DEPTH).transpose(0, 2, 1, 3)
        Q = split(q @ wq.T)
        K = split(k @ wk.T)
        V = split(v @ wv.T)
        scores = jnp.einsum('bhqd,bhkd->bhqk', Q, K) / np.sqrt(DEPTH).astype(np.float32)
        attn = jax.nn.softmax(scores, axis=-1)
        out = jnp.einsum('bhqk,bhkd->bhqd', attn, V)
        return out.transpose(0, 2, 1, 3).reshape(B, S, D_MODEL)

    def _L1_ffn_ref(x, W_Q, W_K, W_O, W_inv, V_fwd, W_fwd, U_fwd, b_fwd, V_inv, W_inv_exp, U_inv, b_inv, router_w1, router_b1, router_w2, router_b2, alpha_bi, expert_bias):
        import jax, jax.numpy as jnp
        import numpy as np
        B, T, D, R, KEXP = (4, 2048, 512, 64, 8)
        RH = max(D, 32)
        SCALE = 0.02

        def _fused_branch(Q_side, K_side, V, W, U, b, router_w1, router_b1, router_w2, router_b2, expert_bias):
            xV = jnp.einsum('btd,kdr->btkr', Q_side, V)
            yW = jnp.einsum('btd,kdr->btkr', K_side, W)
            cum_yW = jnp.cumsum(yW, axis=1)
            prod = xV * cum_yW
            h = jax.nn.gelu(Q_side @ router_w1.T + router_b1, approximate=False)
            logits = h @ router_w2.T + router_b2 + expert_bias
            weights = jax.nn.softmax(logits, axis=-1)
            out = jnp.einsum('btkr,kdr->btd', prod * weights[..., None], U)
            out = out + weights @ b
            n_valid = jnp.arange(1, Q_side.shape[1] + 1, dtype=Q_side.dtype)
            return out / n_valid[None, :, None]
        Q = x @ W_Q.T
        K = x @ W_K.T
        invQ = Q @ W_inv.T
        invK = K @ W_inv.T
        fwd = _fused_branch(Q, K, V_fwd, W_fwd, U_fwd, b_fwd, router_w1, router_b1, router_w2, router_b2, expert_bias)
        inv = _fused_branch(invQ, invK, W_inv_exp, V_inv, U_inv, b_inv, router_w1, router_b1, router_w2, router_b2, expert_bias)
        out = fwd + alpha_bi * inv
        return out @ W_O.T
    x = x + jnp.tanh(g_xattn[0]) * _L0_xattn_ref(_layernorm(x, axis=-1), ctx_1024, ctx_1024, mask_Bx1xSxS2_ik1, L0_xattn_wq, L0_xattn_wk, L0_xattn_wv, L0_xattn_wo, L0_xattn_bq, L0_xattn_bk, L0_xattn_bv, L0_xattn_bo)
    x = x + jnp.tanh(g_ffn[0]) * _L0_ffn_ref(_layernorm(x, axis=-1), L0_ffn_gate_w, L0_ffn_shared_gate_w, L0_ffn_shared_gate_up_w, L0_ffn_shared_down_w, L0_ffn_expert_gate_up_w, L0_ffn_expert_down_w)
    x = x + jnp.tanh(g_xattn[1]) * _L1_xattn_ref(_layernorm(x, axis=-1), ctx_1024, ctx_1024, L1_xattn_wq, L1_xattn_wk, L1_xattn_wv)
    x = x + jnp.tanh(g_ffn[1]) * _L1_ffn_ref(_layernorm(x, axis=-1), L1_ffn_W_Q, L1_ffn_W_K, L1_ffn_W_O, L1_ffn_W_inv, L1_ffn_V_fwd, L1_ffn_W_fwd, L1_ffn_U_fwd, L1_ffn_b_fwd, L1_ffn_V_inv, L1_ffn_W_inv_exp, L1_ffn_U_inv, L1_ffn_b_inv, L1_ffn_router_w1, L1_ffn_router_b1, L1_ffn_router_w2, L1_ffn_router_b2, L1_ffn_alpha_bi, L1_ffn_expert_bias)
    return x

_drawn_inputs = setup_inputs


def setup_inputs(seed=0):
    import zlib

    import numpy as np

    out = dict(_drawn_inputs(seed))
    spreads = {'g_ffn': (-1.0, 0.2),
     'L0_xattn_bq': (0.0, 0.1),
     'L0_xattn_bk': (0.0, 0.1),
     'L0_xattn_bv': (0.0, 0.1),
     'L0_xattn_bo': (0.0, 0.1),
     'L1_ffn_b_fwd': (0.0, 0.1),
     'L1_ffn_b_inv': (0.0, 0.1),
     'L1_ffn_router_b1': (0.0, 0.1),
     'L1_ffn_router_b2': (0.0, 0.1),
     'L1_ffn_expert_bias': (0.0, 0.1)}
    factors = {}
    for name, (base, spread) in spreads.items():
        noise = np.random.default_rng([zlib.crc32(name.encode()), seed]).standard_normal(out[name].shape)
        drawn = base * np.exp(spread * noise) if base else spread * noise
        out[name] = jnp.asarray(drawn.astype(out[name].dtype))
    for name, factor in factors.items():
        out[name] = (out[name] * factor).astype(out[name].dtype)
    return out
```

```python
from contextlib import ExitStack

import concourse.bass as bass
from concourse import mybir

F32, F16, BF16 = mybir.dt.float32, mybir.dt.float16, mybir.dt.bfloat16
U32 = mybir.dt.uint32
ALU, ACT = mybir.AluOpType, mybir.ActivationFunctionType
AX = mybir.AxisListType

P = 128
D = 512
KT = D // P
BATCH, SEQ, CTX = 2, 2048, 154
T = BATCH * SEQ
BLK = 512
TPB = BLK // P
NBB = SEQ // BLK
HEADS, HD = 16, 32
HH = HEADS // 2
REM = CTX - P
HG = P // HD
E, TOPK, CAP = 64, 8, 256
SLOTS = E * CAP
EI = 256
IS = 1024
FB = IS // P
RH, KE, RR = 512, 8, 64
KR = KE * RR
WS = 256.0
EPS = 1e-5
BIG = 65536.0
EPL = 8


class Engine:

    def __init__(self, eng, sem):
        self.eng, self.sem, self.n = eng, sem, 0

    def mark(self, ins):
        ins.then_inc(self.sem, 1)
        self.n += 1
        return (self.sem, self.n)

    def need(self, *tokens):
        for sem, value in tokens:
            self.eng.wait_ge(sem, value)


class Port:

    def __init__(self, sem):
        self.sem, self.n = sem, 0

    def mark(self, ins):
        ins.then_inc(self.sem, 16)
        self.n += 16
        return (self.sem, self.n)


class SoftPort:

    def __init__(self, sem, per_turn):
        self.sem, self.per_turn, self.n, self.base = sem, per_turn, 0, 0

    def turn(self, g):
        self.base = g * self.per_turn

    def mark(self, ins):
        ins.then_inc(self.sem, 16)
        self.n += 16
        return (self.sem, self.base + self.n)


class Ring:

    def __init__(self, bufs):
        self.bufs = bufs
        self.reset()

    def reset(self):
        self.free, self.was, self.at = [()] * len(self.bufs), [()] * len(self.bufs), 0

    def take(self):
        i = self.at % len(self.bufs)
        self.at += 1
        free = self.free[i]
        assert free is not None, "taken before its last user gave it back"
        self.was[i], self.free[i] = free, None
        return self.bufs[i], i, free

    def give(self, i, *tokens):
        self.free[i] = tokens


class Core:
    def __init__(self, nc, ctx):
        self.nc, self.ctx = nc, ctx
        self.sems, self.ports, self.soft = [], [], []
        self.engines = []
        for name, engine in (("tensor", nc.tensor), ("scalar", nc.scalar), ("vector", nc.vector),
                             ("gpsimd", nc.gpsimd), ("sync", nc.sync)):
            sem = ctx.enter_context(nc.semaphore(f"s_{name}"))
            self.engines.append(Engine(engine, sem))
            self.sems.append(sem)
        self.pe, self.act, self.vec, self.pool, self.sp = self.engines
        self.idle = ctx.enter_context(nc.sbuf_tensor("idle", [P, 2], F32))
        nc.gpsimd.memset(self.idle[:, :], 0.0)

    def port(self, name):
        sem = self.ctx.enter_context(self.nc.semaphore(name))
        self.sems.append(sem)
        self.ports.append(Port(sem))
        return self.ports[-1]

    def soft_port(self, name, per_turn):
        self.soft.append(SoftPort(self.ctx.enter_context(self.nc.semaphore(name)), per_turn))
        return self.soft[-1]

    def meet(self):
        for p in self.ports:
            if p.n:
                self.sp.need((p.sem, p.n))
        for p in self.soft:
            if p.n:
                assert p.n == p.per_turn
                self.pool.need((p.sem, p.base + p.n))
        if any(p.n for p in self.soft):
            self.nc.gpsimd.tensor_tensor(self.idle[:, 0:1], self.idle[:, 1:2], self.idle[:, 1:2], ALU.add)
        self.nc.all_engine_barrier()
        for sem in self.sems:
            self.nc.sync.sem_clear(sem)
        self.nc.all_engine_barrier()
        for e in self.engines:
            e.n = 0
        for p in self.ports + self.soft:
            p.n = 0


def split3(c, out, lhs, rhs, ks, start=True, stop=True):
    n = len(ks)
    for i, k in enumerate(ks):
        for j, (a, b) in enumerate(((0, 0), (0, 1), (1, 0))):
            mm = c.nc.tensor.matmul(out, lhs(a, k), rhs(b, k), start=start and i == 0 and j == 0,
                                    stop=stop and i == n - 1 and j == 2)
    return mm


def load_split(c, stage, port, dst, src, after=()):
    c.sp.need(*after)
    got = port.mark(c.nc.sync.dma_start(stage, src))
    c.act.need(got)
    hi = c.act.mark(c.nc.scalar.activation(dst(0), stage, ACT.Copy, scale=WS))
    c.vec.need(hi, got)
    return (c.vec.mark(c.nc.vector.scalar_tensor_tensor(dst(1), stage, WS, dst(0), ALU.mult, ALU.subtract)),)


class NormBuffers:

    def __init__(self, c, ctx, tag, banks):
        nc = c.nc
        sb = lambda n, s, d: ctx.enter_context(nc.sbuf_tensor(f"{tag}_{n}", s, d))
        self.x = Ring([sb(f"x{i}", [P, TPB, D], F32) for i in range(3)])
        self.z = sb("z", [P, TPB, D], F32)
        self.zs = sb("zs", [P, TPB, 2, D], F16)
        self.zT = Ring([sb(f"zT{i}", [P, 2, KT, BLK], F16) for i in range(2)])
        self.stats = sb("stats", [P, TPB, 6], F32)
        self.mv = sb("mv", [P, TPB, 2], F32)
        self.sd = sb("sd", [P, TPB], F32)
        self.rstd = sb("rstd", [P, TPB], F32)
        self.px = [c.port(f"{tag}_x{i}") for i in range(3)]
        self.banks = banks
        self.reset()

    def reset(self):
        self.z_free = self.zs_free = ()
        for r in (self.x, self.zT):
            r.reset()


def load_tokens(c, nb, src, row):
    x, i, free = nb.x.take()
    c.sp.need(*free)
    got = nb.px[i].mark(c.nc.sync.dma_start(
        x[:, :, :], src[bass.ds(row, BLK), :].rearrange("(t p) d -> p t d", p=P)))
    return x, i, got


def normalise(c, K, nb, x, got):
    nc, z, zs = c.nc, nb.z, nb.zs
    c.vec.need(got)
    for t in range(TPB):
        tok = c.vec.mark(nc.vector.bn_stats(nb.stats[:, t, :], x[:, t, :]))
    c.vec.need(tok)
    for t in range(TPB):
        tok = c.vec.mark(nc.vector.bn_aggr(nb.mv[:, t, :], nb.stats[:, t, :]))
    c.act.need(tok)
    sd = c.act.mark(nc.scalar.activation(nb.sd[:, :], nb.mv[:, :, 1], ACT.Sqrt, bias=K.eps[:, 0:1]))
    c.vec.need(sd)
    rs = c.vec.mark(nc.vector.reciprocal(nb.rstd[:, :], nb.sd[:, :]))
    c.vec.need(rs, *nb.z_free)
    normed = [c.vec.mark(nc.vector.tensor_scalar(z[:, t, :], x[:, t, :], nb.mv[:, t, 0:1],
                                                 nb.rstd[:, t:t + 1], ALU.subtract, ALU.mult))
              for t in range(TPB)]
    nb.x_done = normed[-1]
    c.act.need(*nb.zs_free)
    c.pool.need(*nb.zs_free)
    lows = []
    for t in range(TPB):
        c.act.need(normed[t])
        hi = c.act.mark(nc.scalar.copy(zs[:, t, 0, :], z[:, t, :]))
        c.pool.need(hi)
        lows.append(c.pool.mark(nc.gpsimd.tensor_tensor(zs[:, t, 1, :], z[:, t, :], zs[:, t, 0, :],
                                                        ALU.subtract)))
    nb.z_free = (lows[-1],)
    zT, zi, free = nb.zT.take()
    c.act.need(*free)
    c.vec.need(*nb.zT.was[zi])
    done = []
    for t in range(TPB):
        bank, bi, free = nb.banks.take()
        c.pe.need(*free)
        turned = bank[:, :].bitcast(F16).rearrange("p (h k n) -> p h k n", h=2, k=KT)
        c.pe.need(lows[t])
        for h in range(2):
            for k in range(KT):
                mm = nc.tensor.transpose(turned[:, h, k, :], zs[:, t, h, k * P:(k + 1) * P], K.id16[:, :])
        tp = c.pe.mark(mm)
        e = c.act if t % 2 == 0 else c.vec
        e.need(tp)
        dst = zT[:, :, :, t * P:(t + 1) * P]
        out = e.mark(nc.scalar.copy(dst, turned) if t % 2 == 0 else nc.vector.tensor_copy(dst, turned))
        nb.banks.give(bi, out)
        done.append(out)
    nb.zs_free = (tp,)
    return zT, zi, done, lows


def place(h):
    return (h % HG) * (HH // HG) + h // HG


class Consts:
    pass


def constants(c, ctx, I):
    nc, K = c.nc, Consts()
    sb = lambda n, s, d: ctx.enter_context(nc.sbuf_tensor(n, s, d))
    K.id32, K.id16, K.eps = sb("id32", [P, P], F32), sb("id16", [P, P], F16), sb("eps", [P, 1], F32)
    K.gates, K.tg, K.tgw = sb("gates", [P, 4], F32), sb("tg", [P, 4], F32), sb("tgw", [P, 4], F32)
    pg = c.port("gates_in")
    tok = c.pool.mark(nc.gpsimd.memset(K.id32[:, :], 0.0))
    c.pool.need(tok)
    tok = c.pool.mark(nc.gpsimd.affine_select(out=K.id32[:, :], in_=K.id32[:, :], compare_op=ALU.not_equal,
                                              fill=1.0, base=0, pattern=[[-1, P]], channel_multiplier=1))
    c.vec.need(tok)
    c.vec.mark(nc.vector.tensor_copy(K.id16[:, :], K.id32[:, :]))
    c.vec.mark(nc.vector.memset(K.eps[:, :], EPS))
    for i, g in enumerate((I["g_xattn"], I["g_ffn"])):
        got = pg.mark(nc.sync.dma_start(K.gates[:, 2 * i:2 * i + 2],
                                        g.rearrange("(a n) -> a n", a=1).broadcast_to([P, 2])))
        c.sp.need(got)
    c.act.need(got)
    tok = c.act.mark(nc.scalar.activation(K.tg[:, :], K.gates[:, :], ACT.Tanh))
    c.vec.need(tok)
    c.vec.mark(nc.vector.tensor_scalar(K.tgw[:, :], K.tg[:, :], 1.0 / WS, None, ALU.mult))
    c.meet()
    return K


def attention(c, K, I, layer, src, dst, R=None, oute=None):
    nc = c.nc
    L0 = layer == 0
    with ExitStack() as ctx:
        sb = lambda n, s, d: ctx.enter_context(nc.sbuf_tensor(f"at{layer}_{n}", s, d))
        port = lambda n: c.port(f"at{layer}_{n}")
        gen = Ring([ctx.enter_context(nc.psum_tensor(f"at{layer}_g{i}", [P, 512], F32)) for i in range(2)])
        trp = Ring([ctx.enter_context(nc.psum_tensor(f"at{layer}_t{i}", [P, 512], F32)) for i in range(2)])
        S = ctx.enter_context(nc.psum_tensor(f"at{layer}_S", [P, HH, 256], F32))
        nrm = NormBuffers(c, ctx, f"at{layer}", gen)
        wq = sb("wq", [P, 2, KT, D], F16)
        wk, wv = sb("wk", [P, KT, D], F32), sb("wv", [P, KT, D], F32)
        kctx = sb("kctx", [P, KT, CTX], F32)
        rctx = sb("rctx", [P, KT, P], F32)
        KTn = sb("KT", [P, KT, CTX], F32)
        V = sb("V", [P, HEADS, P], F32)
        VR = sb("VR", [P, KT, P], F32)
        qT = Ring([sb(f"qT{i}", [P, KT, BLK], F32) for i in range(2)])
        s = Ring([sb(f"s{i}", [P, HH, CTX], F32) for i in range(2)])
        prob = Ring([sb(f"p{i}", [P, HH * (P + HD)], F32) for i in range(2)])
        pT = Ring([sb(f"pT{i}", [P, HH + 2, BLK], F32) for i in range(2 - (not L0))])
        mx, sm, rs = (Ring([sb(f"{n}{i}", [P, HH], F32) for i in range(2)]) for n in ("mx", "sm", "rs"))
        pw, pk, pv, pc, pr = (port(n) for n in ("wq", "wk", "wv", "kctx", "rctx"))
        pst = [port(f"st{i}") for i in range(3)]
        wk_d, wv_d, wq_d = (I[f"L{layer}_xattn_{n}"].rearrange("(k p) m -> p k m", p=P) for n in ("wkT", "wvT", "wqT"))
        stage = qT.bufs[0]
        load_split(c, stage[:, :, :], pw, lambda h: wq[:, h, :, :], wq_d)
        pk.mark(nc.sync.dma_start(wk[:, :, :], wk_d))
        pv.mark(nc.sync.dma_start(wv[:, :, :], wv_d))
        if L0:
            wo = sb("wo", [P, 2, KT, D], F16)
            oT = Ring([sb(f"oT{i}", [P, 2, KT, BLK], F16) for i in range(1)])
            bq, bqs, bk = sb("bq", [P, KT], F32), sb("bqs", [P, KT], F32), sb("bk", [P, KT], F32)
            bv, bo, tbo = sb("bv", [P, D], F32), sb("bo", [P, D], F32), sb("tbo", [P, D], F32)
            limi = [sb(f"mi{i}", [P, TPB, CTX], mybir.dt.int32) for i in range(1)]
            lim = Ring([sb(f"lim{i}", [P, TPB, CTX], F32) for i in range(2)])
            pb, pm = port("bias"), port("mask")
            stage1 = qT.bufs[1]
            load_split(c, stage1[:, :, :], port("wo"), lambda h: wo[:, h, :, :],
                       I["L0_xattn_woT"].rearrange("(k p) m -> p k m", p=P))
            with nc.allow_non_contiguous_dma(reason="biases by head dim, once"):
                for dstb, n in ((bq, "bq"), (bk, "bk")):
                    got = pb.mark(nc.sync.dma_start(dstb[:, :], I[f"L0_xattn_{n}"].rearrange("(k p) -> p k", p=P)))
            for dstb, n in ((bv, "bv"), (bo, "bo")):
                got = pb.mark(nc.sync.dma_start(dstb[:, :], I[f"L0_xattn_{n}"].rearrange("(a n) -> a n", a=1)
                                                .broadcast_to([P, D])))
            c.vec.need(got)
            c.vec.mark(nc.vector.tensor_scalar(bqs[:, :], bq[:, :], HD ** -0.5, None, ALU.mult))
            c.vec.mark(nc.vector.tensor_scalar(tbo[:, :], bo[:, :], K.tg[:, 0:1], None, ALU.mult))
        else:
            oF = Ring([sb(f"oF{i}", [P, KT, BLK], F32) for i in range(1)])
        c.vec.mark(nc.vector.memset(V[:, :, :], 0.0))
        c.vec.mark(nc.vector.memset(VR[:, :, :], 0.0))
        for b in prob.bufs:
            c.pool.mark(nc.gpsimd.memset(b[:, :], 0.0))
        if not L0:
            rb = ReturnBuffers(c, ctx)
        c.meet()

        with nc.Fori(0, BATCH) as g:
            for r in (gen, trp, qT, s, prob, pT, mx, sm, rs, *((oT, lim) if L0 else (oF,))):
                r.reset()
            nrm.reset()
            if not L0:
                rb.turn(g)
            gotc = pc.mark(nc.sync.dma_start(kctx[:, :, :], I["ctxT"][bass.ds(g, 1), :, :]
                                             .rearrange("a (k p) n -> p (a k) n", p=P)))
            gotr = pr.mark(nc.sync.dma_start(rctx[:, :, :], I["ctxR"][bass.ds(g, 1), :, :]
                                             .rearrange("a (k p) n -> p (a k) n", p=P)))
            blocks = {}

            def load(b):
                row = g * SEQ + b * BLK
                x, xi, got = load_tokens(c, nrm, src, row)
                m = None
                if L0:
                    l, li, free = lim.take()
                    c.vec.need(*free)
                    c.sp.need(*load.mask_free)
                    gm = pm.mark(nc.sync.dma_start(limi[0][:, :, :], I["mask"][bass.ds(row, BLK), :]
                                                   .rearrange("(t p) n -> p t n", p=P)))
                    c.vec.need(gm, *lim.was[li])
                    a = c.vec.mark(nc.vector.tensor_scalar(l[:, :, :], limi[0][:, :, :], 0.0, None, ALU.not_equal))
                    load.mask_free = (a,)
                    c.vec.need(a)
                    a = c.vec.mark(nc.vector.tensor_scalar(l[:, :, :], l[:, :, :], 1e30, -1e30, ALU.mult, ALU.add))
                    c.vec.need(a)
                    a = c.vec.mark(nc.vector.tensor_scalar(l[:, :, :], l[:, :, :], 100.0, None, ALU.add))
                    m = (l, li, a)
                blocks[b] = dict(x=x, xi=xi, got=got, m=m, row=row, tile=g * (SEQ // P) + b * TPB)

            load.mask_free = ()

            def project(b):
                w = blocks[b]
                if not L0:
                    w["got"] = add_returns(c, R, rb, oute, w["x"], w["got"], w["tile"])
                w["zT"], zi, done, lows = normalise(c, K, nrm, w["x"], w["got"])
                if L0:
                    c.pool.need(nrm.x_done)
                    for t in range(TPB):
                        w["x_ready"] = c.pool.mark(nc.gpsimd.tensor_tensor(w["x"][:, t, :], w["x"][:, t, :],
                                                                           tbo[:, :], ALU.add))
                else:
                    w["x_ready"] = nrm.x_done
                q, qi, free = qT.take()
                c.act.need(*free)
                c.pe.need(*done)
                for m in range(KT):
                    bank, bi, free = gen.take()
                    c.pe.need(*free)
                    mm = split3(c, bank[:, :], lambda h, k: wq[:, h, k, m * P:(m + 1) * P],
                                lambda h, k: w["zT"][:, h, k, :], range(KT))
                    tok = c.pe.mark(mm)
                    c.act.need(tok)
                    sc = HD ** -0.5 / WS
                    if L0:
                        out = c.act.mark(nc.scalar.activation(q[:, m, :], bank[:, :], ACT.Identity,
                                                              bias=bqs[:, m:m + 1], scale=sc))
                    else:
                        out = c.act.mark(nc.scalar.activation(q[:, m, :], bank[:, :], ACT.Copy, scale=sc))
                    gen.give(bi, out)
                nrm.zT.give(zi, tok)
                w["q"], w["qi"], w["q_ready"] = q, qi, out

            score_free = [()]

            def scores(b, u, t):
                w = blocks[b]
                c.pe.need(w["q_ready"], *score_free[0])
                for h in range(HH):
                    o, m = HD * (h % HG), 2 * u + h // HG
                    mm = nc.tensor.matmul(S[:, place(h), 0:CTX], w["q"][o:o + HD, m, t * P:(t + 1) * P],
                                          KTn[o:o + HD, m, :], start=True, stop=True)
                tok = c.pe.mark(mm)
                w["q_used"] = tok
                sb_, si, free = s.take()
                c.vec.need(*free)
                mxb, mi, free = mx.take()
                c.vec.need(*free)
                smb, smi, free = sm.take()
                c.vec.need(*free)
                rsb, ri, free = rs.take()
                c.vec.need(*free)
                c.vec.need(tok)
                if L0:
                    l, li, lt = w["m"]
                    c.vec.need(lt)
                    a = c.vec.mark(nc.vector.scalar_tensor_tensor(
                        sb_[:, :, :], S[:, :, 0:CTX], -100.0,
                        l[:, t:t + 1, :].broadcast_to([P, HH, CTX]), ALU.max, ALU.min))
                    score_free[0] = (a,)
                    if (u, t) == (1, TPB - 1):
                        lim.give(li, a)
                    c.vec.need(a)
                    top = c.vec.mark(nc.vector.tensor_reduce(mxb[:, :], sb_[:, :, :], AX.X, ALU.max))
                    c.pool.need(top)
                    sub = c.pool.mark(nc.gpsimd.tensor_tensor(
                        sb_[:, :, :], sb_[:, :, :], mxb[:, :, None].broadcast_to([P, HH, CTX]), ALU.subtract))
                else:
                    top = c.vec.mark(nc.vector.tensor_reduce(mxb[:, :], S[:, :, 0:CTX], AX.X, ALU.max))
                    c.vec.need(top)
                    sub = c.vec.mark(nc.vector.tensor_tensor(
                        sb_[:, :, :], S[:, :, 0:CTX], mxb[:, :, None].broadcast_to([P, HH, CTX]), ALU.subtract))
                    score_free[0] = (sub,)
                mx.give(mi, sub)
                c.act.need(sub)
                ex = c.act.mark(nc.scalar.activation(sb_[:, :, :], sb_[:, :, :], ACT.Exp))
                return dict(s=sb_, si=si, sm=smb, smi=smi, rs=rsb, ri=ri, ex=ex)

            def probabilities(v):
                sb_, smb, rsb = v["s"], v["sm"], v["rs"]
                pb_, v["pi"], free = prob.take()
                c.pool.need(*free)
                v["p"] = pb_
                c.vec.need(v["ex"])
                a = c.vec.mark(nc.vector.tensor_reduce(smb[:, :], sb_[:, :, :], AX.X, ALU.add))
                c.vec.need(a)
                r = c.vec.mark(nc.vector.reciprocal(rsb[:, :], smb[:, :]))
                sm.give(v["smi"], r)
                c.pool.need(r)
                main = pb_[:, 0:HH * P].rearrange("p (h n) -> p h n", h=HH)
                rem = pb_[:, HH * P:].rearrange("p (j r n) -> p r j n", r=HG, n=HD)
                srem = sb_[:, :, P:CTX].rearrange("p (r j) n -> p r j n", r=HG)
                rrem = rsb[:, :].rearrange("p (r j) -> p r j", r=HG)[:, :, :, None]
                nc.gpsimd.tensor_tensor(main, sb_[:, :, 0:P], rsb[:, :, None].broadcast_to([P, HH, P]), ALU.mult)
                tok = c.pool.mark(nc.gpsimd.tensor_tensor(rem[:, :, :, 0:REM], srem,
                                                          rrem.broadcast_to([P, HG, HH // HG, REM]), ALU.mult))
                s.give(v["si"], tok)
                rs.give(v["ri"], tok)
                v["p_ready"] = tok

            def turn(v, ptb, t):
                c.pe.need(v["p_ready"])
                outs = []
                for j0 in range(0, HH + 2, 4):
                    n = min(4, HH + 2 - j0)
                    bank, bi, free = trp.take()
                    c.pe.need(*free)
                    for j in range(n):
                        mm = nc.tensor.transpose(bank[:, j * P:(j + 1) * P],
                                                 v["p"][:, (j0 + j) * P:(j0 + j + 1) * P], K.id32[:, :])
                    tok = c.pe.mark(mm)
                    e = c.vec if j0 == 8 else c.act
                    e.need(tok, *pT_free[0])
                    dst_ = ptb[:, j0:j0 + n, t * P:(t + 1) * P]
                    srcb = bank[:, 0:n * P].rearrange("p (j n) -> p j n", j=n)
                    out = e.mark(nc.vector.tensor_copy(dst_, srcb) if j0 == 8 else nc.scalar.copy(dst_, srcb))
                    trp.give(bi, out)
                    outs.append(out)
                prob.give(v["pi"], tok)
                return outs

            pT_free = [()]

            def values(b, u, ptb, pti, ready):
                w = blocks[b]
                c.pe.need(*ready)
                if u == 0:
                    w["o"], w["oi"], free = (oT if L0 else oF).take()
                    c.act.need(*free)
                    c.vec.need(*(oT if L0 else oF).was[w["oi"]])
                    w["o_ready"] = []
                for gi in range(2):
                    grp = 2 * u + gi
                    bank, bi, free = gen.take()
                    c.pe.need(*free)
                    for j in range(HG):
                        nc.tensor.matmul(bank[:, :], V[:, grp * HG + j, :],
                                         ptb[:, place(gi * HG + j), :],
                                         start=(j == 0), stop=False)
                    tok = c.pe.mark(nc.tensor.matmul(bank[:, :], VR[:, grp, :], ptb[:, HH + gi, :],
                                                     start=False, stop=True))
                    c.act.need(tok)
                    if L0:
                        hi = c.act.mark(nc.scalar.copy(w["o"][:, 0, grp, :], bank[:, :]))
                        c.vec.need(hi)
                        out = c.vec.mark(nc.vector.tensor_tensor(w["o"][:, 1, grp, :], bank[:, :],
                                                                 w["o"][:, 0, grp, :], ALU.subtract))
                    else:
                        out = c.act.mark(nc.scalar.copy(w["o"][:, grp, :], bank[:, :]))
                    gen.give(bi, out)
                    w["o_ready"].append(out)
                pT.give(pti, tok)

            def finish(b):
                w = blocks[b]
                x, xi = w["x"], w["xi"]
                c.pe.need(*w["o_ready"])
                for t in range(TPB):
                    bank, bi, free = gen.take()
                    c.pe.need(*free)
                    if L0:
                        mm = split3(c, bank[:, :], lambda h, k: w["o"][:, h, k, t * P:(t + 1) * P],
                                    lambda h, k: wo[:, h, k, :], range(KT))
                    else:
                        for k in range(KT):
                            mm = nc.tensor.transpose(bank[:, k * P:(k + 1) * P],
                                                     w["o"][:, k, t * P:(t + 1) * P], K.id32[:, :])
                    tok = c.pe.mark(mm)
                    c.vec.need(tok, w["x_ready"])
                    out = c.vec.mark(nc.vector.scalar_tensor_tensor(
                        x[:, t, :], bank[:, :], K.tgw[:, 0:1] if L0 else K.tg[:, 1:2], x[:, t, :],
                        ALU.mult, ALU.add))
                    gen.give(bi, out)
                (oT if L0 else oF).give(w["oi"], tok)
                qT.give(w["qi"], w["q_used"])
                c.sp.need(out)
                st = pst[xi].mark(nc.sync.dma_start(
                    dst[bass.ds(w["row"], BLK), :].rearrange("(t p) d -> p t d", p=P), x[:, :, :]))
                nrm.x.give(xi, st)

            load(0)
            c.pe.need(gotc, gotr)
            kv = []
            for m in range(KT):
                bank, bi, free = gen.take()
                c.pe.need(*free)
                for k in range(KT):
                    mm = nc.tensor.matmul(bank[:, 0:CTX], wk[:, k, m * P:(m + 1) * P], kctx[:, k, :],
                                          start=(k == 0), stop=(k == KT - 1))
                tok = c.pe.mark(mm)
                c.vec.need(tok)
                if L0:
                    out = c.vec.mark(nc.vector.tensor_scalar(KTn[:, m, :], bank[:, 0:CTX], bk[:, m:m + 1],
                                                             None, ALU.add))
                else:
                    out = c.vec.mark(nc.vector.tensor_copy(KTn[:, m, :], bank[:, 0:CTX]))
                gen.give(bi, out)
            for rem in range(2):
                bank, bi, free = gen.take()
                c.pe.need(*free)
                for k in range(KT):
                    mm = nc.tensor.matmul(bank[:, :], rctx[:, k, :] if rem else kctx[:, k, 0:P], wv[:, k, :],
                                          start=(k == 0), stop=(k == KT - 1))
                tok = c.pe.mark(mm)
                c.vec.need(tok)
                for h in range(HG):
                    rows = slice(HD * h, HD * h + HD) if rem else slice(0, P)
                    o = (VR[rows, :, HD * h:HD * h + HD] if rem else
                         V[:, :, :].rearrange("p (g h) n -> p g h n", h=HG)[:, :, h, HD * h:HD * h + HD])
                    i_ = bank[:, :].rearrange("p (g h n) -> p g h n", g=KT, h=HG)[rows, :, h, :]
                    if L0:
                        b_ = bv[:, :].rearrange("p (g h n) -> p g h n", g=KT, h=HG)[rows, :, h, :]
                        out = c.vec.mark(nc.vector.tensor_tensor(o, i_, b_, ALU.add))
                    else:
                        out = c.vec.mark(nc.vector.tensor_copy(o, i_))
                gen.give(bi, out)
            c.pe.need(out)
            project(0)
            units = [(b, u, t) for b in range(NBB) for u in range(2) for t in range(TPB)]
            pend = []

            def end_unit(v, b, u, t):
                if t == 0:
                    end_unit.pt, end_unit.pti, free = pT.take()
                    c.act.need(*free)
                    pT_free[0] = pT.was[end_unit.pti]
                    end_unit.ready = []
                end_unit.ready += turn(v, end_unit.pt, t)
                if t == TPB - 1:
                    values(b, u, end_unit.pt, end_unit.pti, end_unit.ready)
                    if u == 1:
                        finish(b)

            for n, (b, u, t) in enumerate(units):
                if (u, t) == (0, 0) and b + 1 < NBB:
                    load(b + 1)
                v = scores(b, u, t)
                pend.append((v, b, u, t))
                if (u, t) == (0, 2) and b + 1 < NBB:
                    project(b + 1)
                if len(pend) > 1:
                    probabilities(pend[-2][0])
                if len(pend) > 2 or (len(pend) == 2 and n > 1):
                    end_unit(*pend.pop(0))
            probabilities(pend[-1][0])
            for p_ in pend:
                end_unit(*p_)
            c.meet()


class Routing:

    def __init__(self, nc, ctx):
        sb = lambda n, s, d: ctx.enter_context(nc.sbuf_tensor(n, s, d))
        self.slots = sb("slots", [P, T // P, TOPK], U32)
        self.weights = sb("weights", [P, T // P, TOPK], F32)


def shared_and_route(c, K, I, R, src, dst, zrows, ids):
    nc = c.nc
    with ExitStack() as ctx:
        sb = lambda n, s, d: ctx.enter_context(nc.sbuf_tensor(f"sh_{n}", s, d))
        port = lambda n: c.port(f"sh_{n}")
        ps = lambda n, s: ctx.enter_context(nc.psum_tensor(f"sh_{n}", s, F32))
        gen = Ring([ps(f"g{i}", [P, 512]) for i in range(3)])
        gu = Ring([ps(f"gu{i}", [P, 2, 512]) for i in range(2)])
        LG = ps("LG", [P, TPB, E + 1])
        nrm = NormBuffers(c, ctx, "sh", gen)
        wgu, wdn = sb("wgu", [P, 2, KT, 2 * IS], F16), sb("wdn", [P, 2, FB, D], F16)
        wgt = sb("wgt", [P, 2, KT, E + 1], F16)
        actT = sb("actT", [P, 2, FB, BLK], F16)
        act32 = Ring([sb(f"a{i}", [P, BLK], F32) for i in range(2)])
        silu = Ring([sb(f"si{i}", [P, BLK], F32) for i in range(2)])
        stage = nrm.x.bufs
        pw, pst, pz, psc = port("w"), [port(f"st{i}") for i in range(3)], port("z"), [c.soft_port(f"sh_sc{i}", 16 * TPB * TOPK * NBB // 2) for i in range(2)]
        tri, ones = sb("tri", [P, P], BF16), sb("ones", [P, P], BF16)
        one32 = sb("one32", [P, P], F32)
        iexp, iexpi = sb("iexp", [P, E], F32), sb("iexpi", [P, E], mybir.dt.int32)
        tokf, toki = sb("tokf", [P, TPB], F32), sb("toki", [P, TPB], mybir.dt.int32)
        tokb = Ring([sb(f"tk{i}", [P, TPB], F32) for i in range(2)])
        count, countb, sum4 = sb("count", [P, E], F32), sb("countb", [P, E], BF16), sb("sum4", [P, E], F32)
        ex, rep = sb("ex", [P, TPB, E], F32), sb("rep", [P, TPB, E], F32)
        M = sb("M", [P, TPB, E], BF16)
        top, idx, idxf = sb("top", [P, TPB, TOPK], F32), sb("idx", [P, TPB, TOPK], U32), sb("idxf", [P, TPB, TOPK], F32)
        mx, sm, rs = sb("mx", [P, TPB], F32), sb("sm", [P, TPB], F32), sb("rs", [P, TPB], F32)
        w8, slot, far = sb("w8", [P, TPB, TOPK], F32), sb("slot", [P, TPB, E], F32), sb("far", [P, TPB, E], F32)
        eq, slotk = sb("eq", [P, TPB, TOPK, E], F32), sb("slotk", [P, TPB, TOPK], F32)
        kept = sb("kept", [P, TPB, TOPK], F32)
        slotu = Ring([sb(f"su{i}", [P, TPB, TOPK], U32) for i in range(2)])
        sg = sb("sg", [P, TPB], F32)

        wgu_d = I["L0_ffn_shared_gate_up_w"].rearrange("(k p) n -> p k n", p=P)
        wdn_d = I["L0_ffn_shared_down_w"].rearrange("(k p) n -> p k n", p=P)
        last = ()
        for n in range(4):
            st = stage[n % 2]
            last = load_split(c, st[:, :, :], pw, lambda h: wgu[:, h, :, n * 512:(n + 1) * 512],
                              wgu_d[:, :, n * 512:(n + 1) * 512], after=last)
        for n in range(2):
            last = load_split(c, stage[n][:, :, :], pw, lambda h: wdn[:, h, 4 * n:4 * n + 4, :],
                              wdn_d[:, 4 * n:4 * n + 4, :], after=last)
        load_split(c, stage[0][:, :, 0:E + 1], pw, lambda h: wgt[:, h, :, :],
                   I["gates65"].rearrange("(k p) n -> p k n", p=P), after=last)
        a = c.pool.mark(nc.gpsimd.memset(one32[:, :], 1.0))
        c.pool.need(a)
        a = c.pool.mark(nc.gpsimd.affine_select(out=one32[:, :], in_=one32[:, :], compare_op=ALU.is_gt, fill=0.0,
                                                base=0, pattern=[[1, P]], channel_multiplier=-1))
        b = c.pool.mark(nc.gpsimd.iota(iexpi[:, :], pattern=[[CAP, E]], base=0, channel_multiplier=0))
        b = c.pool.mark(nc.gpsimd.iota(toki[:, :], pattern=[[P, TPB]], base=0, channel_multiplier=1))
        c.vec.need(a, b)
        c.vec.mark(nc.vector.tensor_copy(tri[:, :], one32[:, :]))
        c.vec.mark(nc.vector.memset(ones[:, :], 1.0))
        c.vec.mark(nc.vector.tensor_copy(iexp[:, :], iexpi[:, :]))
        c.vec.mark(nc.vector.tensor_copy(tokf[:, :], toki[:, :]))
        c.vec.mark(nc.vector.memset(count[:, :], 0.0))
        c.vec.mark(nc.vector.memset(countb[:, :], 0.0))
        z = c.vec.mark(nc.vector.memset(eq[:, :, :, :], 0.0))
        c.sp.need(z)
        pz.mark(nc.sync.dma_start(ids.rearrange("(p n) a -> p (n a)", p=P), eq[:, 0, 0:2, :].rearrange("p a b -> p (a b)")))
        c.meet()

        with nc.Fori(0, BATCH) as g:
            for r in (gen, gu, act32, silu, tokb, slotu):
                r.reset()
            nrm.reset()
            for q in psc:
                q.turn(g)
            blocks, held = {}, dict(route=(), scat=(), actT=(), LG=(), pos=())

            def load(b):
                row = g * SEQ + b * BLK
                x, xi, got = load_tokens(c, nrm, src, row)
                blocks[b] = dict(x=x, xi=xi, got=got, row=row)

            def project(b):
                w = blocks[b]
                w["zT"], w["zi"], w["done"], lows = normalise(c, K, nrm, w["x"], w["got"])
                c.sp.need(*lows)
                zst = pz.mark(nc.sync.dma_start(
                    zrows[bass.ds(w["row"], BLK), :].rearrange("(t p) d -> p t d", p=P),
                    nrm.zs[:, :, :, :].rearrange("p t h d -> p t (h d)")))
                nrm.zs_free = (*nrm.zs_free, zst)
                c.pe.need(*w["done"], *held["LG"])
                for t in range(TPB):
                    mm = split3(c, LG[:, t, :], lambda h, k: w["zT"][:, h, k, t * P:(t + 1) * P],
                                lambda h, k: wgt[:, h, k, :], range(KT))
                w["logits"] = c.pe.mark(mm)

            def choose(b):
                w = blocks[b]
                v = nc.vector
                c.vec.need(w["logits"], *held["route"])
                a = c.vec.mark(v.tensor_reduce(mx[:, :], LG[:, :, 0:E], AX.X, ALU.max))
                c.vec.need(a)
                a = c.vec.mark(v.tensor_tensor(ex[:, :, :], LG[:, :, 0:E], mx[:, :, None].broadcast_to([P, TPB, E]),
                                               ALU.subtract))
                c.act.need(a, w["logits"])
                e1 = c.act.mark(nc.scalar.activation(ex[:, :, :], ex[:, :, :], ACT.Exp, scale=1.0 / WS))
                e2 = c.act.mark(nc.scalar.activation(sg[:, :], LG[:, :, E], ACT.Exp, scale=-1.0 / WS))
                held["LG"] = (a, e2)
                c.vec.need(e1)
                for t in range(TPB):
                    a = c.vec.mark(v.max(top[:, t, :], ex[:, t, :]))
                c.vec.need(a)
                for t in range(TPB):
                    c.vec.mark(v.max_index(idx[:, t, :], top[:, t, :], ex[:, t, :]))
                    a = c.vec.mark(v.match_replace(rep[:, t, :], top[:, t, :], ex[:, t, :], -1.0))
                b_ = c.vec.mark(v.tensor_reduce(sm[:, :], top[:, :, :], AX.X, ALU.add))
                c.vec.need(a)
                w["chosen"] = c.vec.mark(v.tensor_scalar(M[:, :, :], rep[:, :, :], 0.0, None, ALU.is_lt))
                c.vec.mark(v.tensor_scalar(idxf[:, :, :], idx[:, :, :], float(CAP), None, ALU.mult))
                c.vec.need(b_)
                a = c.vec.mark(v.reciprocal(rs[:, :], sm[:, :]))
                c.vec.need(a, e2)
                c.vec.mark(v.tensor_tensor(w8[:, :, :], top[:, :, :], rs[:, :, None].broadcast_to([P, TPB, TOPK]),
                                           ALU.mult))
                a = c.vec.mark(v.tensor_scalar(sg[:, :], sg[:, :], 1.0, None, ALU.add))
                c.vec.need(a)
                a = c.vec.mark(v.reciprocal(sg[:, :], sg[:, :]))
                c.vec.need(a)
                w["sg"] = c.vec.mark(v.tensor_scalar(sg[:, :], sg[:, :], K.tgw[:, 2:3], None, ALU.mult))

            def positions(b):
                w = blocks[b]
                bank, bi, free = gen.take()
                c.pe.need(*free)
                c.pe.need(w["chosen"], *held["pos"])
                pos = bank[:, 0:TPB * E].rearrange("p (t e) -> p t e", t=TPB)
                for t in range(TPB):
                    nc.tensor.matmul(pos[:, t, :], ones[:, :], countb[:, :], start=True, stop=False)
                    for t2 in range(t):
                        nc.tensor.matmul(pos[:, t, :], ones[:, :], M[:, t2, :], start=False, stop=False)
                    mm = nc.tensor.matmul(pos[:, t, :], tri[:, :], M[:, t, :], start=False, stop=True)
                tok = c.pe.mark(mm)
                v = nc.vector
                c.vec.need(tok)
                a = c.vec.mark(v.tensor_tensor(slot[:, :, :], pos, iexp[:, None, :].broadcast_to([P, TPB, E]), ALU.add))
                b_ = c.vec.mark(v.tensor_scalar(far[:, :, :], pos, float(CAP), BIG, ALU.is_ge, ALU.mult))
                gen.give(bi, b_)
                c.vec.need(b_)
                a = c.vec.mark(v.tensor_tensor(slot[:, :, :], slot[:, :, :], far[:, :, :], ALU.max))
                d = c.vec.mark(v.tensor_reduce(sum4[:, :], M[:, :, :].rearrange("p t e -> p e t"), AX.X, ALU.add))
                c.vec.need(d)
                d = c.vec.mark(v.tensor_tensor(count[:, :], count[:, :], sum4[:, :], ALU.add))
                c.vec.need(d)
                d = c.vec.mark(v.tensor_copy(countb[:, :], count[:, :]))
                held["pos"] = (d,)
                shape = [P, TPB, TOPK, E]
                a = c.vec.mark(v.tensor_tensor(eq[:, :, :, :], iexp[:, None, None, :].broadcast_to(shape),
                                               idxf[:, :, :, None].broadcast_to(shape), ALU.is_equal))
                c.vec.need(a)
                a = c.vec.mark(v.tensor_tensor(eq[:, :, :, :], eq[:, :, :, :],
                                               slot[:, :, None, :].broadcast_to(shape), ALU.mult))
                c.vec.need(a)
                a = c.vec.mark(v.tensor_reduce(slotk[:, :, :], eq[:, :, :, :], AX.X, ALU.add))
                c.vec.need(a)
                su, si, free = slotu.take()
                c.vec.need(*free)
                tk, ti, free = tokb.take()
                c.vec.need(*free)
                tl = bass.ds(g * (SEQ // P) + b * TPB, TPB)
                c.vec.mark(v.tensor_copy(R.slots[:, tl, :], slotk[:, :, :]))
                c.vec.mark(v.tensor_copy(tk[:, :], tokf[:, :]))
                a = c.vec.mark(v.tensor_copy(su[:, :, :], slotk[:, :, :]))
                c.vec.need(a)
                c.vec.mark(v.tensor_scalar(tokf[:, :], tokf[:, :], float(BLK), None, ALU.add))
                k = c.vec.mark(v.tensor_scalar(kept[:, :, :], slotk[:, :, :], BIG, K.tg[:, 2:3], ALU.is_lt, ALU.mult))
                c.vec.need(k)
                k = c.vec.mark(v.tensor_tensor(R.weights[:, tl, :], w8[:, :, :], kept[:, :, :], ALU.mult))
                held["route"] = (k, tok)
                c.pool.need(a)
                for t in range(TPB):
                    for j in range(TOPK):
                        s_ = psc[si].mark(nc.gpsimd.indirect_dma_start(
                            ids, bass.IndirectOffsetOnAxis(su[:, t, j:j + 1], 0), tk[:, t:t + 1], None,
                            bounds_check=SLOTS - 1, oob_is_err=False))
                slotu.give(si, s_)
                tokb.give(ti, s_)

            def up(b, f):
                w = blocks[b]
                bank, bi, free = gu.take()
                c.pe.need(*free)
                for j in range(2):
                    o = j * IS + f * P
                    mm = split3(c, bank[:, j, :], lambda h, k: wgu[:, h, k, o:o + P],
                                lambda h, k: w["zT"][:, h, k, :], range(KT))
                tok = c.pe.mark(mm)
                si_, sii, free = silu.take()
                c.act.need(*free)
                c.act.need(tok)
                s_ = c.act.mark(nc.scalar.activation(si_[:, :], bank[:, 0, :], ACT.Silu, scale=1.0 / WS))
                a_, ai, free = act32.take()
                c.vec.need(*free)
                c.vec.need(s_, tok)
                a = c.vec.mark(nc.vector.scalar_tensor_tensor(a_[:, :], bank[:, 1, :], 1.0 / WS, si_[:, :],
                                                              ALU.mult, ALU.mult))
                gu.give(bi, s_, a)
                silu.give(sii, a)
                c.act.need(a, *(held["actT"] if f == 0 else ()))
                hi = c.act.mark(nc.scalar.copy(actT[:, 0, f, :], a_[:, :]))
                c.pool.need(hi)
                lo = c.pool.mark(nc.gpsimd.tensor_tensor(actT[:, 1, f, :], a_[:, :], actT[:, 0, f, :], ALU.subtract))
                act32.give(ai, lo)
                w["lo"] = lo
                if f == FB - 1:
                    nrm.zT.give(w["zi"], tok)

            def down(b):
                w = blocks[b]
                x = w["x"]
                c.pe.need(w["lo"])
                for t in range(TPB):
                    bank, bi, free = gen.take()
                    c.pe.need(*free)
                    mm = split3(c, bank[:, :], lambda h, k: actT[:, h, k, t * P:(t + 1) * P],
                                lambda h, k: wdn[:, h, k, :], range(FB))
                    tok = c.pe.mark(mm)
                    c.vec.need(tok, w["sg"])
                    out = c.vec.mark(nc.vector.scalar_tensor_tensor(x[:, t, :], bank[:, :], w["sgt"][:, t:t + 1],
                                                                    x[:, t, :], ALU.mult, ALU.add))
                    gen.give(bi, out)
                held["actT"] = (tok,)
                c.sp.need(out)
                st = pst[w["xi"]].mark(nc.sync.dma_start(
                    dst[bass.ds(w["row"], BLK), :].rearrange("(t p) d -> p t d", p=P), x[:, :, :]))
                nrm.x.give(w["xi"], st)

            load(0)
            project(0)
            choose(0)
            for b in range(NBB):
                blocks[b]["sgt"] = sg
                if b + 1 < NBB:
                    load(b + 1)
                for f in range(FB):
                    up(b, f)
                    if f == 0:
                        positions(b)
                    if f == 4 and b + 1 < NBB:
                        project(b + 1)
                down(b)
                if b + 1 < NBB:
                    choose(b + 1)
            c.meet()


def experts(c, K, I, zrows, ids, oute):
    nc = c.nc
    with ExitStack() as ctx:
        sb = lambda n, s, d: ctx.enter_context(nc.sbuf_tensor(f"ex_{n}", s, d))
        port = lambda n: c.port(f"ex_{n}")
        ps = lambda n, s: ctx.enter_context(nc.psum_tensor(f"ex_{n}", s, F32))
        NS = CAP // P
        EK = EI // P
        tr = Ring([ps(f"t{i}", [P, 512]) for i in range(2)])
        gu = Ring([ps(f"gu{i}", [P, 2, 512]) for i in range(2)])
        ob = Ring([ps(f"o{i}", [P, 512]) for i in range(2)])
        rows, idxu = sb("rows", [P, P], F32), sb("idxu", [P, E * NS], U32)
        cols = sb("cols", [P, EPL * NS], U32)
        st1 = Ring([sb(f"w1_{i}", [P, KT, 2 * EI], F32) for i in range(3)])
        st2 = Ring([sb(f"w2_{i}", [P, EK, D], F32) for i in range(3)])
        w1 = Ring([sb(f"h1_{i}", [P, 2, KT, 2 * EI], F16) for i in range(2)])
        w2 = Ring([sb(f"h2_{i}", [P, 2, EK, D], F16) for i in range(2)])
        xg = Ring([sb(f"xg{i}", [P, 2, KT, P], F16) for i in range(4)])
        xT = Ring([sb(f"xT{i}", [P, 2, KT, CAP], F16) for i in range(2)])
        silu, a32 = (Ring([sb(f"{n}{i}", [P, EK, CAP], F32) for i in range(2)]) for n in ("si", "a"))
        aT = Ring([sb(f"aT{i}", [P, 2, EK, CAP], F16) for i in range(2)])
        o32 = Ring([sb(f"oo{i}", [P, NS, D], F32) for i in range(2)])
        p1, p2 = [port(f"w1{i}") for i in range(3)], [port(f"w2{i}") for i in range(3)]
        px, po, pi = [c.soft_port(f"ex_x{i}", 16 * EPL * NS // 4) for i in range(4)], [port(f"o{i}") for i in range(2)], port("ids")
        got = pi.mark(nc.sync.dma_start(rows[:, :], ids.rearrange("(r n) a -> r (n a)", r=P)))
        c.pe.need(got)
        bank, _, free = tr.take()
        c.pe.need(*free)
        tok = c.pe.mark(nc.tensor.transpose(bank[:, 0:P], rows[:, :], K.id32[:, :]))
        c.vec.need(tok)
        c.vec.mark(nc.vector.tensor_copy(idxu[:, :], bank[:, 0:P]))
        c.meet()
        with nc.Fori(0, E // EPL) as g:
            for r in (tr, gu, ob, st1, st2, w1, w2, xg, xT, silu, a32, aT, o32):
                r.reset()
            for q in px:
                q.turn(g)
            ci = c.vec.mark(nc.vector.tensor_copy(cols[:, :], idxu[:, bass.ds(g * (EPL * NS), EPL * NS)]))
            ex = {}

            def fetch(e):
                q = ex[e] = {}
                q["s1"], q["i1"], free = st1.take()
                c.sp.need(*free)
                q["g1"] = p1[q["i1"]].mark(nc.sync.dma_start(
                    q["s1"][:, :, :], I["L0_ffn_expert_gate_up_w"][bass.ds(g * EPL + e, 1), :, :]
                    .rearrange("a (k p) n -> p (a k) n", p=P)))
                q["s2"], q["i2"], free = st2.take()
                c.sp.need(*free)
                q["g2"] = p2[q["i2"]].mark(nc.sync.dma_start(
                    q["s2"][:, :, :], I["L0_ffn_expert_down_w"][bass.ds(g * EPL + e, 1), :, :]
                    .rearrange("a (k p) n -> p (a k) n", p=P)))
                q["x"] = []
                for s in range(NS):
                    x, xi, free = xg.take()
                    c.pool.need(*free)
                    c.pool.need(ci)
                    n = e * NS + s
                    gx = px[xi].mark(nc.gpsimd.indirect_dma_start(
                        x[:, :, :, :].rearrange("p h k n -> p (h k n)"), None, zrows,
                        bass.IndirectOffsetOnAxis(cols[:, n:n + 1], 0)))
                    q["x"].append((x, xi, gx))

            def prepare(e):
                q = ex[e]
                q["w1"], q["j1"], free = w1.take()
                c.act.need(*free)
                c.vec.need(*w1.was[q["j1"]])
                c.act.need(q["g1"])
                q["w1r"] = []
                for k in range(0, KT, 2):
                    h1 = c.act.mark(nc.scalar.activation(q["w1"][:, 0, k:k + 2, :], q["s1"][:, k:k + 2, :],
                                                         ACT.Copy, scale=WS))
                    c.vec.need(h1, q["g1"])
                    q["w1r"].append(c.vec.mark(nc.vector.scalar_tensor_tensor(
                        q["w1"][:, 1, k:k + 2, :], q["s1"][:, k:k + 2, :], WS, q["w1"][:, 0, k:k + 2, :],
                        ALU.mult, ALU.subtract)))
                st1.give(q["i1"], q["w1r"][-1])
                xt, q["xti"], free = xT.take()
                c.act.need(*free)
                c.vec.need(*xT.was[q["xti"]])
                q["xT"], q["xTr"] = xt, []
                for s, (x, xi, gx) in enumerate(q["x"]):
                    bank, bi, free = tr.take()
                    c.pe.need(*free)
                    c.pe.need(gx)
                    turned = bank[:, :].bitcast(F16).rearrange("p (h k n) -> p h k n", h=2, k=KT)
                    for h in range(2):
                        for k in range(KT):
                            mm = nc.tensor.transpose(turned[:, h, k, :], x[:, h, k, :], K.id16[:, :])
                    tok = c.pe.mark(mm)
                    xg.give(xi, tok)
                    en = c.act if s == 0 else c.vec
                    en.need(tok)
                    d_ = xt[:, :, :, s * P:(s + 1) * P]
                    out = en.mark(nc.scalar.copy(d_, turned) if s == 0 else nc.vector.tensor_copy(d_, turned))
                    tr.give(bi, out)
                    q["xTr"].append(out)
                q["w2"], q["j2"], free = w2.take()
                c.act.need(*free)
                c.pool.need(*w2.was[q["j2"]])
                c.act.need(q["g2"])
                h2 = c.act.mark(nc.scalar.activation(q["w2"][:, 0, :, :], q["s2"][:, :, :], ACT.Copy, scale=WS))
                c.pool.need(h2, q["g2"])
                sc_ = c.pool.mark(nc.gpsimd.tensor_scalar(q["s2"][:, :, :], q["s2"][:, :, :], WS, None, ALU.mult))
                c.pool.need(sc_)
                q["w2r"] = c.pool.mark(nc.gpsimd.tensor_tensor(q["w2"][:, 1, :, :], q["s2"][:, :, :],
                                                               q["w2"][:, 0, :, :], ALU.subtract))
                st2.give(q["i2"], q["w2r"])

            def up(e):
                q = ex[e]
                bank, bi, free = gu.take()
                c.pe.need(*free)
                c.pe.need(*q["xTr"], *q["w1r"])
                for f in range(2 * EK):
                    mm = split3(c, bank[:, f // EK, (f % EK) * CAP:(f % EK + 1) * CAP],
                                lambda h, k: q["w1"][:, h, k, f * P:(f + 1) * P],
                                lambda h, k: q["xT"][:, h, k, :], range(KT))
                tok = c.pe.mark(mm)
                w1.give(q["j1"], tok)
                xT.give(q["xti"], tok)
                si_, sii, free = silu.take()
                c.act.need(*free)
                c.act.need(tok)
                G, U = (bank[:, j, :].rearrange("p (k n) -> p k n", k=EK) for j in range(2))
                s_ = c.act.mark(nc.scalar.activation(si_[:, :, :], G, ACT.Silu, scale=1.0 / WS))
                a_, ai, free = a32.take()
                c.vec.need(*free)
                c.vec.need(s_, tok)
                a = c.vec.mark(nc.vector.scalar_tensor_tensor(a_[:, :, :], U, 1.0 / WS, si_[:, :, :],
                                                              ALU.mult, ALU.mult))
                gu.give(bi, s_, a)
                silu.give(sii, a)
                at, ati, free = aT.take()
                c.act.need(*free)
                c.vec.need(*aT.was[ati])
                c.act.need(a)
                hi = c.act.mark(nc.scalar.copy(at[:, 0, :, :], a_[:, :, :]))
                c.vec.need(hi)
                q["aTr"] = c.vec.mark(nc.vector.tensor_tensor(at[:, 1, :, :], a_[:, :, :], at[:, 0, :, :],
                                                              ALU.subtract))
                a32.give(ai, q["aTr"])
                q["aT"], q["ati"] = at, ati

            def down(e):
                q = ex[e]
                c.pe.need(q["aTr"], q["w2r"])
                o, oi, free = o32.take()
                c.act.need(*free)
                for s in range(NS):
                    bank, bi, free = ob.take()
                    c.pe.need(*free)
                    mm = split3(c, bank[:, :], lambda h, k: q["aT"][:, h, k, s * P:(s + 1) * P],
                                lambda h, k: q["w2"][:, h, k, :], range(EK))
                    tok = c.pe.mark(mm)
                    c.act.need(tok)
                    out = c.act.mark(nc.scalar.activation(o[:, s, :], bank[:, :], ACT.Copy, scale=1.0 / WS))
                    ob.give(bi, out)
                w2.give(q["j2"], tok)
                aT.give(q["ati"], tok)
                c.sp.need(out)
                st = po[oi].mark(nc.sync.dma_start(
                    oute[bass.ds((g * EPL + e) * CAP, CAP), :].rearrange("(s p) d -> p s d", p=P), o[:, :, :]))
                o32.give(oi, st)

            fetch(0)
            fetch(1)
            prepare(0)
            for e in range(EPL):
                up(e)
                if e + 1 < EPL:
                    prepare(e + 1)
                if e + 2 < EPL:
                    fetch(e + 2)
                down(e)
            c.meet()


class ReturnBuffers:

    def __init__(self, c, ctx):
        nc = c.nc
        sb = lambda n, s, d: ctx.enter_context(nc.sbuf_tensor(f"rt_{n}", s, d))
        self.rows = Ring([sb(f"g{i}", [P, TOPK, D], F32) for i in range(2)])
        self.slots, self.weights = sb("at", [P, TPB, TOPK], U32), sb("w", [P, TPB, TOPK], F32)
        self.ports = [c.soft_port(f"rt_p{i}", 16 * TOPK * TPB * NBB // 2) for i in range(2)]
        for b in self.rows.bufs:
            c.vec.mark(nc.vector.memset(b[:, :, :], 0.0))

    def turn(self, g):
        self.rows.reset()
        self.gathered, self.added = (), ()
        for q in self.ports:
            q.turn(g)


def add_returns(c, R, rb, oute, x, got, tile):
    nc = c.nc
    c.vec.need(*rb.gathered, *rb.added)
    a = c.vec.mark(nc.vector.tensor_copy(rb.slots[:, :, :], R.slots[:, bass.ds(tile, TPB), :]))
    ww = c.vec.mark(nc.vector.tensor_copy(rb.weights[:, :, :], R.weights[:, bass.ds(tile, TPB), :]))
    c.pool.need(a)
    c.vec.need(got, ww)
    for t in range(TPB):
        buf, bi, free = rb.rows.take()
        c.pool.need(*free)
        for k in range(TOPK):
            tok = rb.ports[bi].mark(nc.gpsimd.indirect_dma_start(
                buf[:, k, :], None, oute, bass.IndirectOffsetOnAxis(rb.slots[:, t, k:k + 1], 0),
                bounds_check=SLOTS - 1, oob_is_err=False))
        c.vec.need(tok)
        for k in range(TOPK):
            a = c.vec.mark(nc.vector.scalar_tensor_tensor(x[:, t, :], buf[:, k, :], rb.weights[:, t, k:k + 1],
                                                          x[:, t, :], ALU.mult, ALU.add))
            c.vec.need(a)
        rb.rows.give(bi, a)
    rb.gathered, rb.added = (tok,), (a,)
    return a


def fused_experts(c, K, I, src, dst):
    nc = c.nc
    PS = 1.0 / 64.0
    with ExitStack() as ctx:
        sb = lambda n, s, d: ctx.enter_context(nc.sbuf_tensor(f"fe_{n}", s, d))
        port = lambda n: c.port(f"fe_{n}")
        ps = lambda n, s: ctx.enter_context(nc.psum_tensor(f"fe_{n}", s, F32))
        gen = Ring([ps(f"g{i}", [P, 512]) for i in range(2)])
        trio = Ring([ps(f"p{i}", [P, 3, 512]) for i in range(2)])
        nrm = NormBuffers(c, ctx, "fe", gen)
        NJ = 2 * KR // P
        left, right = ([sb(f"{n}{i}", [P, 2, KT, KR], F16) for i in range(2)] for n in ("lf", "rt"))
        router = [sb(f"ro{i}", [P, 2, KT, RH], F16) for i in range(2)]
        up = sb("up", [P, 2, NJ, D], F16)
        cz = Ring([sb(f"cz{i}", [P, KT, BLK], F32) for i in range(2)])
        czs = sb("czs", [P, 2, KT, BLK], F16)
        h32 = Ring([sb(f"h{i}", [P, KT, BLK], F32) for i in range(1)])
        prodT = sb("prodT", [P, 2, NJ, BLK], F16)
        t32, p32, c32 = (Ring([sb(f"{n}{i}", [P, BLK], F32) for i in range(2)]) for n in ("t", "pp", "c"))
        r2 = sb("r2", [P, KT, KE], F32)
        b1 = sb("b1", [P, KT], F32)
        b2, b2x, alpha = sb("b2", [P, KE], F32), sb("b2x", [P, KE], F32), sb("alpha", [P, 1], F32)
        bT, bo = sb("bT", [P, KT, P], F32), sb("bo", [2 * KE, 2, D], F16)
        sel32, sel = sb("sel32", [2 * KE, NJ, P], F32), sb("sel", [2 * KE, NJ, P], F16)
        lg, ex = sb("lg", [P, TPB, 2, KE], F32), sb("exr", [P, TPB, 2, KE], F32)
        mx, sm, rs = (sb(n, [P, TPB, 2], F32) for n in ("mx", "sm", "rs"))
        wr = sb("wr", [P, TPB, 2, KE], F32)
        wT = Ring([sb(f"wT{i}", [2 * KE, 2, BLK], F16) for i in range(2)])
        ni, nf = sb("ni", [P, SEQ // P], mybir.dt.int32), sb("nf", [P, SEQ // P], F32)
        pst = [port(f"st{i}") for i in range(3)]
        pl = [port(f"l{i}") for i in range(5)]
        psm = port("small")

        view = lambda n: I["L1_ffn_" + n].rearrange("(k p) m -> p k m", p=P)
        bufs = [*nrm.x.bufs, nrm.z, cz.bufs[0], cz.bufs[1], h32.bufs[0]]
        wq, wk, winv = bufs[0:3]
        q1 = pl[0].mark(nc.sync.dma_start(wq[:, :, :], view("W_Q")))
        q3 = pl[2].mark(nc.sync.dma_start(winv[:, :, :], view("W_inv")))
        q2 = pl[1].mark(nc.sync.dma_start(wk[:, :, :], view("W_K")))
        small = lambda d_, s_: psm.mark(nc.sync.dma_start(d_, s_))
        small(bT[:, :, :], I["L1_ffn_bT"].rearrange("(k p) m -> p k m", p=P))
        small(r2[:, :, :], I["L1_ffn_router_w2T"].rearrange("(k p) m -> p k m", p=P))
        with nc.allow_non_contiguous_dma(reason="a bias by feature, once"):
            small(b1[:, :], I["L1_ffn_router_b1"].rearrange("(k p) -> p k", p=P))
        row = lambda n, w: I["L1_ffn_" + n].rearrange("(a n) -> a n", a=1).broadcast_to([P, w])
        small(b2[:, :], row("router_b2", KE))
        small(b2x[:, :], row("expert_bias", KE))
        sm_in = small(alpha[:, :], row("alpha_bi", 1))
        xs, bs = Ring([bufs[3], bufs[4]]), Ring([bufs[5], bufs[6]])

        def fetch(name):
            b, i, free = xs.take()
            c.sp.need(*free)
            return b, i, pl[3 + i].mark(nc.sync.dma_start(b[:, :, :], view(name)))

        def chain(lhs, lhs_in, rhs, rhs_in, out32=None, out16=None, after=()):
            c.pe.need(*lhs_in, *rhs_in)
            for m in range(KT):
                bank, bi, free = gen.take()
                c.pe.need(*free)
                for k in range(KT):
                    mm = nc.tensor.matmul(bank[:, :], lhs[:, k, m * P:(m + 1) * P], rhs[:, k, :],
                                          start=(k == 0), stop=(k == KT - 1))
                tok = c.pe.mark(mm)
                c.act.need(tok, *after)
                if out32 is not None:
                    out = c.act.mark(nc.scalar.copy(out32[:, m, :], bank[:, :]))
                else:
                    hi = c.act.mark(nc.scalar.activation(out16(0, m), bank[:, :], ACT.Copy, scale=WS))
                    c.vec.need(hi)
                    out = c.vec.mark(nc.vector.scalar_tensor_tensor(out16(1, m), bank[:, :], WS, out16(0, m),
                                                                    ALU.mult, ALU.subtract))
                gen.give(bi, out)
            return tok, out

        for name, proj, qp, into in (("W_inv_exp", wq, q1, left[1]), ("V_inv", wk, q2, right[1]),
                                     ("router_w1T", wq, q1, router[1])):
            f, fi, fin_ = fetch(name)
            m_, mi, free = bs.take()
            c.act.need(*free)
            tok, out = chain(winv, (q3,), f, (fin_,), out32=m_)
            if name != "router_w1T":
                xs.give(fi, tok)
            tok, _ = chain(proj, (qp,), m_, (out,), out16=lambda h, m: into[:, h, m, :])
            bs.give(mi, tok)
        tok, _ = chain(wq, (q1,), f, (), out16=lambda h, m: router[0][:, h, m, :])
        xs.give(fi, tok)
        for name, proj, qp, into in (("V_fwd", wq, q1, left[0]), ("W_fwd", wk, q2, right[0])):
            f, fi, fin_ = fetch(name)
            tok, _ = chain(proj, (qp,), f, (fin_,), out16=lambda h, m: into[:, h, m, :])
            xs.give(fi, tok)
        c.sp.need(tok)
        wo = winv
        q3 = pl[2].mark(nc.sync.dma_start(wo[:, :, :], view("W_OT")))
        for i, name in enumerate(("U_fwd", "U_inv")):
            f, fi, fin_ = fetch(name)
            tok, _ = chain(f, (fin_,), wo, (q3,), out16=lambda h, m: up[:, h, i * KT + m, :])
            xs.give(fi, tok)
        c.pe.need(sm_in)
        bank, bi, free = gen.take()
        c.pe.need(*free)
        for k in range(KT):
            mm = nc.tensor.matmul(bank[:, :], bT[:, k, :], wo[:, k, :], start=(k == 0), stop=(k == KT - 1))
        tok = c.pe.mark(mm)
        c.act.need(tok)
        hi = c.act.mark(nc.scalar.activation(bo[:, 0, :], bank[0:2 * KE, :], ACT.Copy, scale=WS * PS))
        c.vec.need(hi)
        gen.give(bi, c.vec.mark(nc.vector.scalar_tensor_tensor(bo[:, 1, :], bank[0:2 * KE, :], WS * PS, bo[:, 0, :],
                                                               ALU.mult, ALU.subtract)))
        a = c.pool.mark(nc.gpsimd.memset(sel32[:, :, :], 1.0))
        c.pool.need(a)
        a = c.pool.mark(nc.gpsimd.affine_select(out=sel32[:, :, :], in_=sel32[:, :, :], compare_op=ALU.is_ge, fill=0.0,
                                                base=0, pattern=[[P, NJ], [1, P]], channel_multiplier=-RR))
        c.pool.need(a)
        a = c.pool.mark(nc.gpsimd.affine_select(out=sel32[:, :, :], in_=sel32[:, :, :], compare_op=ALU.is_ge, fill=0.0,
                                                base=RR - 1, pattern=[[-P, NJ], [-1, P]], channel_multiplier=RR))
        b_ = c.pool.mark(nc.gpsimd.iota(ni[:, :], pattern=[[P, SEQ // P]], base=1, channel_multiplier=1))
        c.vec.need(a, b_, sm_in)
        c.vec.mark(nc.vector.tensor_copy(sel[:, :, :], sel32[:, :, :]))
        c.vec.mark(nc.vector.tensor_tensor(b2[:, :], b2[:, :], b2x[:, :], ALU.add))
        a = c.vec.mark(nc.vector.tensor_copy(nf[:, :], ni[:, :]))
        c.vec.need(a)
        a = c.vec.mark(nc.vector.reciprocal(nf[:, :], nf[:, :]))
        c.vec.need(a)
        c.vec.mark(nc.vector.tensor_scalar(nf[:, :], nf[:, :], K.tgw[:, 3:4], 1.0 / PS, ALU.mult, ALU.mult))
        c.meet()

        with nc.Fori(0, BATCH) as g:
            for r in (gen, trio, cz, h32, t32, p32, c32, wT):
                r.reset()
            nrm.reset()
            blocks, held = {}, dict(czs=(), prod=(), lg=())

            def load(b):
                row_ = g * SEQ + b * BLK
                x, xi, got = load_tokens(c, nrm, src, row_)
                blocks[b] = dict(x=x, xi=xi, got=got, row=row_)

            def project(b):
                w = blocks[b]
                w["zT"], w["zi"], w["done"], _ = normalise(c, K, nrm, w["x"], w["got"])
                s_, w["ci"], free = cz.take()
                c.vec.need(*free)
                c.vec.need(*w["done"])
                before = blocks[b - 1] if b else None
                if b:
                    c.vec.need(before["scan"])
                for k in range(KT):
                    w["scan"] = c.vec.mark(nc.vector.tensor_tensor_scan(
                        s_[:, k, :], w["zT"][:, 0, k, :], w["zT"][:, 1, k, :],
                        before["cz"][:, k, BLK - 1:BLK] if b else 0.0, ALU.add, ALU.add))
                w["cz"] = s_
                if b:
                    cz.give(before["ci"], *before["cz_used"], w["scan"])
                w["cz_used"] = ()

            def halve(b):
                w = blocks[b]
                c.act.need(w["scan"], *held["czs"])
                for k in range(KT):
                    hi = c.act.mark(nc.scalar.copy(czs[:, 0, k, :], w["cz"][:, k, :]))
                    c.pool.need(hi)
                    w["czs"] = c.pool.mark(nc.gpsimd.tensor_tensor(czs[:, 1, k, :], w["cz"][:, k, :],
                                                                   czs[:, 0, k, :], ALU.subtract))
                w["cz_used"] = (w["czs"],)

            def route(b):
                w = blocks[b]
                c.pe.need(*w["done"])
                v = nc.vector
                c.vec.need(*held["lg"])
                for r in range(2):
                    h_, hi_, free = h32.take()
                    c.act.need(*free)
                    for m in range(KT):
                        bank, bi, free = gen.take()
                        c.pe.need(*free)
                        tok = c.pe.mark(split3(c, bank[:, :], lambda h, k: router[r][:, h, k, m * P:(m + 1) * P],
                                               lambda h, k: w["zT"][:, h, k, :], range(KT)))
                        c.act.need(tok)
                        a = c.act.mark(nc.scalar.activation(h_[:, m, :], bank[:, :], ACT.Gelu, bias=b1[:, m:m + 1],
                                                            scale=1.0 / WS))
                        gen.give(bi, a)
                    bank, bi, free = gen.take()
                    c.pe.need(*free)
                    c.pe.need(a)
                    for t in range(TPB):
                        for k in range(KT):
                            mm = nc.tensor.matmul(bank[:, t * KE:(t + 1) * KE], h_[:, k, t * P:(t + 1) * P],
                                                  r2[:, k, :], start=(k == 0), stop=(k == KT - 1))
                    tok = c.pe.mark(mm)
                    h32.give(hi_, tok)
                    c.vec.need(tok)
                    a = c.vec.mark(v.tensor_tensor(
                        lg[:, :, r, :], bank[:, 0:TPB * KE].rearrange("p (t e) -> p t e", t=TPB),
                        b2[:, None, :].broadcast_to([P, TPB, KE]), ALU.add))
                    gen.give(bi, a)
                shape = [P, TPB, 2, KE]
                c.vec.need(a)
                a = c.vec.mark(v.tensor_reduce(mx[:, :, :], lg[:, :, :, :], AX.X, ALU.max))
                c.vec.need(a)
                a = c.vec.mark(v.tensor_tensor(lg[:, :, :, :], lg[:, :, :, :], mx[:, :, :, None].broadcast_to(shape),
                                               ALU.subtract))
                c.act.need(a)
                e = c.act.mark(nc.scalar.activation(ex[:, :, :, :], lg[:, :, :, :], ACT.Exp))
                c.vec.need(e)
                a = c.vec.mark(v.tensor_reduce(sm[:, :, :], ex[:, :, :, :], AX.X, ALU.add))
                c.vec.need(a)
                a = c.vec.mark(v.reciprocal(rs[:, :, :], sm[:, :, :]))
                c.vec.need(a)
                a = c.vec.mark(v.tensor_scalar(rs[:, :, 1], rs[:, :, 1], alpha[:, 0:1], None, ALU.mult))
                c.vec.need(a)
                w["wr"] = c.vec.mark(v.tensor_tensor(wr[:, :, :, :], ex[:, :, :, :],
                                                     rs[:, :, :, None].broadcast_to(shape), ALU.mult))

            def turn_weights(b):
                w = blocks[b]
                bank, bi, free = gen.take()
                c.pe.need(*free)
                c.pe.need(w["wr"])
                for t in range(TPB):
                    mm = nc.tensor.transpose(bank[0:2 * KE, t * P:(t + 1) * P],
                                             wr[:, t, :, :].rearrange("p r e -> p (r e)"), K.id32[:, :])
                tok = c.pe.mark(mm)
                held["lg"] = (tok,)
                o, w["wi"], free = wT.take()
                c.act.need(*free)
                c.vec.need(*wT.was[w["wi"]])
                c.act.need(tok)
                hi = c.act.mark(nc.scalar.copy(o[:, 0, :], bank[0:2 * KE, :]))
                c.vec.need(hi)
                w["wTr"] = c.vec.mark(nc.vector.tensor_tensor(o[:, 1, :], bank[0:2 * KE, :], o[:, 0, :], ALU.subtract))
                gen.give(bi, w["wTr"])
                w["wT"] = o

            def factors(b, j):
                w = blocks[b]
                br, m = divmod(j, KT)
                bank, bi, free = trio.take()
                c.pe.need(*free)
                ms = slice(m * P, (m + 1) * P)
                split3(c, bank[:, 0, :], lambda h, k: left[br][:, h, k, ms], lambda h, k: w["zT"][:, h, k, :], range(KT))
                c.pe.need(w["czs"])
                mm = split3(c, bank[:, 1, :], lambda h, k: right[br][:, h, k, ms], lambda h, k: czs[:, h, k, :],
                            range(KT))
                tok = c.pe.mark(mm)
                if j == NJ - 1:
                    nrm.zT.give(w["zi"], tok)
                    held["czs"] = (tok,)
                c_, ci, free = c32.take()
                c.act.need(*free)
                c.act.need(tok)
                cp = c.act.mark(nc.scalar.copy(c_[:, :], bank[:, 1, :]))
                t_, ti, free = t32.take()
                c.vec.need(*free)
                c.vec.need(tok, cp)
                pr = c.vec.mark(nc.vector.tensor_tensor(t_[:, :], bank[:, 0, :], c_[:, :], ALU.mult))
                c32.give(ci, pr)
                w[j] = (bank, bi, t_, ti, pr)

            def weigh(b, j):
                w = blocks[b]
                bank, bi, t_, ti, pr = w.pop(j)
                c.pe.need(w["wTr"])
                for h in range(2):
                    mm = nc.tensor.matmul(bank[:, 2, :], sel[:, j, :], w["wT"][:, h, :], start=(h == 0), stop=(h == 1))
                tok = c.pe.mark(mm)
                p_, pi, free = p32.take()
                c.vec.need(*free)
                c.vec.need(tok, pr)
                a = c.vec.mark(nc.vector.scalar_tensor_tensor(p_[:, :], t_[:, :], PS / WS / WS, bank[:, 2, :],
                                                              ALU.mult, ALU.mult))
                trio.give(bi, a)
                t32.give(ti, a)
                c.act.need(a, *held["prod"])
                hi = c.act.mark(nc.scalar.copy(prodT[:, 0, j, :], p_[:, :]))
                c.pool.need(hi)
                lo = c.pool.mark(nc.gpsimd.tensor_tensor(prodT[:, 1, j, :], p_[:, :], prodT[:, 0, j, :], ALU.subtract))
                p32.give(pi, lo)
                w["lo"] = lo

            def finish(b):
                w = blocks[b]
                x = w["x"]
                c.pe.need(w["lo"])
                for t in range(TPB):
                    ts_ = slice(t * P, (t + 1) * P)
                    bank, bi, free = gen.take()
                    c.pe.need(*free)
                    split3(c, bank[:, :], lambda h, j: prodT[:, h, j, ts_], lambda h, j: up[:, h, j, :], range(NJ),
                           stop=False)
                    mm = split3(c, bank[:, :], lambda h, k: w["wT"][:, h, ts_], lambda h, k: bo[:, h, :], [0],
                                start=False)
                    tok = c.pe.mark(mm)
                    c.vec.need(tok)
                    n_ = b * TPB + t
                    out = c.vec.mark(nc.vector.scalar_tensor_tensor(x[:, t, :], bank[:, :], nf[:, n_:n_ + 1],
                                                                    x[:, t, :], ALU.mult, ALU.add))
                    gen.give(bi, out)
                held["prod"] = (tok,)
                wT.give(w["wi"], tok)
                c.sp.need(out)
                st = pst[w["xi"]].mark(nc.sync.dma_start(
                    dst[bass.ds(w["row"], BLK), :].rearrange("(t p) d -> p t d", p=P), x[:, :, :]))
                nrm.x.give(w["xi"], st)

            load(0)
            project(0)
            halve(0)
            route(0)
            for b in range(NBB):
                if b + 1 < NBB:
                    load(b + 1)
                factors(b, 0)
                turn_weights(b)
                weigh(b, 0)
                for j in range(1, NJ):
                    factors(b, j)
                    weigh(b, j)
                    if j == 4 and b + 1 < NBB:
                        project(b + 1)
                if b + 1 < NBB:
                    halve(b + 1)
                    route(b + 1)
                finish(b)
            c.meet()


def program(nc, I, out):
    scratch = lambda n, s, d: nc.dram_tensor(n, s, d, kind="Internal").ap()
    x1, xp, x3 = (scratch(n, (T, D), F32) for n in ("x1", "xp", "x3"))
    zrows, ids = scratch("zrows", (T, 2 * D), F16), scratch("ids", (SLOTS, 1), F32)
    oute = scratch("oute", (SLOTS, D), F32)
    with ExitStack() as ctx:
        c = Core(nc, ctx)
        K = constants(c, ctx, I)
        R = Routing(nc, ctx)
        attention(c, K, I, 0, I["x"], x1)
        shared_and_route(c, K, I, R, x1, xp, zrows, ids)
        experts(c, K, I, zrows, ids, oute)
        attention(c, K, I, 1, xp, x3, R=R, oute=oute)
        fused_experts(c, K, I, x3, out)


def layout(inputs):
    import numpy as np

    a = {n: np.asarray(v) for n, v in inputs.items()}
    out = {"x": a["x"].reshape(T, D), "mask": a["mask_Bx1xSxS2_ik1"].reshape(T, CTX)}
    ctxT = a["ctx_1024"].transpose(0, 2, 1)
    out["ctxT"] = ctxT
    rem = np.zeros((BATCH, D, HG, HD), ctxT.dtype)
    rem[:, :, :, 0:REM] = ctxT[:, :, None, P:CTX]
    out["ctxR"] = rem.reshape(BATCH, D, P)
    for n in ("g_xattn", "g_ffn", "L0_xattn_bq", "L0_xattn_bk", "L0_xattn_bv", "L0_xattn_bo"):
        out[n] = a[n]
    for n in ("L0_xattn_wq", "L0_xattn_wk", "L0_xattn_wv", "L0_xattn_wo",
              "L1_xattn_wq", "L1_xattn_wk", "L1_xattn_wv", "L1_ffn_W_O", "L1_ffn_router_w1", "L1_ffn_router_w2"):
        out[n + "T"] = a[n].T
    out["gates65"] = np.concatenate([a["L0_ffn_gate_w"], a["L0_ffn_shared_gate_w"]], axis=1)
    for n in ("L0_ffn_shared_gate_up_w", "L0_ffn_shared_down_w", "L0_ffn_expert_gate_up_w", "L0_ffn_expert_down_w",
              "L1_ffn_W_Q", "L1_ffn_W_K", "L1_ffn_W_inv", "L1_ffn_router_b1", "L1_ffn_router_b2",
              "L1_ffn_expert_bias"):
        out[n] = a[n]
    out["L1_ffn_alpha_bi"] = a["L1_ffn_alpha_bi"].reshape(1)
    for n in ("V_fwd", "W_fwd", "U_fwd", "V_inv", "W_inv_exp", "U_inv"):
        out["L1_ffn_" + n] = a["L1_ffn_" + n].transpose(1, 0, 2).reshape(D, KR)
    bT = np.zeros((D, P), a["L1_ffn_b_fwd"].dtype)
    bT[:, 0:KE], bT[:, KE:2 * KE] = a["L1_ffn_b_fwd"].T, a["L1_ffn_b_inv"].T
    out["L1_ffn_bT"] = bT
    return {n: np.ascontiguousarray(v) for n, v in out.items()}


def kernel(**inputs):
    import concourse.bacc as _bacc
    from concourse.bass_utils import run_bass_kernel_spmd as _run

    nc = _bacc.Bacc("TRN2", target_bir_lowering=False, num_devices=1)
    arrays = layout(inputs)
    I = {n: nc.dram_tensor(n, v.shape, mybir.dt.from_np(v.dtype), kind="ExternalInput").ap()
         for n, v in arrays.items()}
    out = nc.dram_tensor("out", (T, D), F32, kind="ExternalOutput").ap()
    program(nc, I, out)
    r = _run(nc, [arrays], core_ids=[0])
    return r.results[0]["out"].reshape(BATCH, SEQ, D)
```

```python
from contextlib import ExitStack

import concourse.bass as bass
from concourse import mybir

F32, F16, BF16 = mybir.dt.float32, mybir.dt.float16, mybir.dt.bfloat16
U32 = mybir.dt.uint32
ALU, ACT = mybir.AluOpType, mybir.ActivationFunctionType
AX = mybir.AxisListType

P = 128
D = 512
KT = D // P
BATCH, SEQ, CTX = 2, 2048, 154
T = BATCH * SEQ
BLK = 512
TPB = BLK // P
NBB = SEQ // BLK
HEADS, HD = 16, 32
HH = HEADS // 2
REM = CTX - P
HG = P // HD
E, TOPK, CAP = 64, 8, 256
SLOTS = E * CAP
EI = 256
IS = 1024
FB = IS // P
RH, KE, RR = 512, 8, 64
KR = KE * RR
WS = 256.0
EPS = 1e-5
BIG = 65536.0
EPL = 16


class Engine:

    def __init__(self, eng, sem):
        self.eng, self.sem, self.n = eng, sem, 0

    def mark(self, ins):
        ins.then_inc(self.sem, 1)
        self.n += 1
        return (self.sem, self.n)

    def need(self, *tokens):
        for sem, value in tokens:
            self.eng.wait_ge(sem, value)


class Port:

    def __init__(self, sem):
        self.sem, self.n = sem, 0

    def mark(self, ins):
        ins.then_inc(self.sem, 16)
        self.n += 16
        return (self.sem, self.n)


class SoftPort:

    def __init__(self, sem, per_turn):
        self.sem, self.per_turn, self.n, self.base = sem, per_turn, 0, 0

    def turn(self, g):
        self.base = g * self.per_turn

    def mark(self, ins):
        ins.then_inc(self.sem, 16)
        self.n += 16
        return (self.sem, self.base + self.n)


class Ring:

    def __init__(self, bufs):
        self.bufs = bufs
        self.reset()

    def reset(self):
        self.free, self.was, self.at = [()] * len(self.bufs), [()] * len(self.bufs), 0

    def take(self):
        i = self.at % len(self.bufs)
        self.at += 1
        free = self.free[i]
        assert free is not None, "taken before its last user gave it back"
        self.was[i], self.free[i] = free, None
        return self.bufs[i], i, free

    def give(self, i, *tokens):
        self.free[i] = tokens


class Core:
    def __init__(self, nc, ctx):
        self.nc, self.ctx = nc, ctx
        self.sems, self.ports, self.soft = [], [], []
        self.engines = []
        for name, engine in (("tensor", nc.tensor), ("scalar", nc.scalar), ("vector", nc.vector),
                             ("gpsimd", nc.gpsimd), ("sync", nc.sync)):
            sem = ctx.enter_context(nc.semaphore(f"s_{name}"))
            self.engines.append(Engine(engine, sem))
            self.sems.append(sem)
        self.pe, self.act, self.vec, self.pool, self.sp = self.engines
        self.idle = ctx.enter_context(nc.sbuf_tensor("idle", [P, 2], F32))
        nc.gpsimd.memset(self.idle[:, :], 0.0)

    def port(self, name):
        sem = self.ctx.enter_context(self.nc.semaphore(name))
        self.sems.append(sem)
        self.ports.append(Port(sem))
        return self.ports[-1]

    def soft_port(self, name, per_turn):
        self.soft.append(SoftPort(self.ctx.enter_context(self.nc.semaphore(name)), per_turn))
        return self.soft[-1]

    def meet(self):
        for p in self.ports:
            if p.n:
                self.sp.need((p.sem, p.n))
        for p in self.soft:
            if p.n:
                assert p.n == p.per_turn
                self.pool.need((p.sem, p.base + p.n))
        if any(p.n for p in self.soft):
            self.nc.gpsimd.tensor_tensor(self.idle[:, 0:1], self.idle[:, 1:2], self.idle[:, 1:2], ALU.add)
        self.nc.all_engine_barrier()
        for sem in self.sems:
            self.nc.sync.sem_clear(sem)
        self.nc.all_engine_barrier()
        for e in self.engines:
            e.n = 0
        for p in self.ports + self.soft:
            p.n = 0


def split3(c, out, lhs, rhs, ks, start=True, stop=True):
    n = len(ks)
    for i, k in enumerate(ks):
        for j, (a, b) in enumerate(((0, 0), (0, 1), (1, 0))):
            mm = c.nc.tensor.matmul(out, lhs(a, k), rhs(b, k), start=start and i == 0 and j == 0,
                                    stop=stop and i == n - 1 and j == 2)
    return mm


def load_split(c, stage, port, dst, src, after=()):
    c.sp.need(*after)
    got = port.mark(c.nc.sync.dma_start(stage, src))
    c.act.need(got)
    hi = c.act.mark(c.nc.scalar.activation(dst(0), stage, ACT.Copy, scale=WS))
    c.vec.need(hi, got)
    return (c.vec.mark(c.nc.vector.scalar_tensor_tensor(dst(1), stage, WS, dst(0), ALU.mult, ALU.subtract)),)


class NormBuffers:

    def __init__(self, c, ctx, tag, banks, turned=2):
        nc = c.nc
        sb = lambda n, s, d: ctx.enter_context(nc.sbuf_tensor(f"{tag}_{n}", s, d))
        self.x = Ring([sb(f"x{i}", [P, TPB, D], F32) for i in range(3)])
        self.z = Ring([sb(f"z{i}", [P, D], F32) for i in range(2)])
        self.zs = Ring([sb(f"zs{i}", [P, 2, D], F16) for i in range(2)])
        self.zT = Ring([sb(f"zT{i}", [P, 2, KT, BLK], F16) for i in range(turned)])
        self.stats = sb("stats", [P, TPB, 6], F32)
        self.mv = sb("mv", [P, TPB, 2], F32)
        self.sd = sb("sd", [P, TPB], F32)
        self.rstd = sb("rstd", [P, TPB], F32)
        self.px = [c.port(f"{tag}_x{i}") for i in range(3)]
        self.banks = banks

    def reset(self):
        for r in (self.x, self.z, self.zs, self.zT):
            r.reset()


def load_tokens(c, nb, src, row):
    x, i, free = nb.x.take()
    c.sp.need(*free)
    got = nb.px[i].mark(c.nc.sync.dma_start(
        x[:, :, :], src[bass.ds(row, BLK), :].rearrange("(t p) d -> p t d", p=P)))
    return x, i, got


def statistics(c, K, nb, w):
    nc, x = c.nc, w["x"]
    c.vec.need(w["got"])
    for t in range(TPB):
        tok = c.vec.mark(nc.vector.bn_stats(nb.stats[:, t, :], x[:, t, :]))
    c.vec.need(tok)
    for t in range(TPB):
        tok = c.vec.mark(nc.vector.bn_aggr(nb.mv[:, t, :], nb.stats[:, t, :]))
    c.act.need(tok)
    sd = c.act.mark(nc.scalar.activation(nb.sd[:, :], nb.mv[:, :, 1], ACT.Sqrt, bias=K.eps[:, 0:1]))
    c.vec.need(sd)
    w["rstd"] = c.vec.mark(nc.vector.reciprocal(nb.rstd[:, :], nb.sd[:, :]))
    w["zT"], w["zi"], w["zT_free"] = nb.zT.take()
    w["turned"] = []


def halves(c, nb, w, t, low):
    nc = c.nc
    z, i, free = nb.z.take()
    c.vec.need(w["rstd"], *free)
    w["x_done"] = c.vec.mark(nc.vector.tensor_scalar(z[:, :], w["x"][:, t, :], nb.mv[:, t, 0:1],
                                                     nb.rstd[:, t:t + 1], ALU.subtract, ALU.mult))
    zs, j, free = nb.zs.take()
    c.act.need(w["x_done"], *free)
    hi = c.act.mark(nc.scalar.copy(zs[:, 0, :], z[:, :]))
    low.need(hi)
    lo = low.mark(low.eng.tensor_tensor(zs[:, 1, :], z[:, :], zs[:, 0, :], ALU.subtract))
    nb.z.give(i, lo)
    w["zs", t] = (zs, j, lo)


def turn_tile(c, K, nb, w, t, stored=()):
    nc = c.nc
    zs, j, lo = w["zs", t]
    bank, bi, free = nb.banks.take()
    c.pe.need(lo, *free)
    turned = bank[:, :].bitcast(F16).rearrange("p (h k n) -> p h k n", h=2, k=KT)
    for h in range(2):
        for k in range(KT):
            mm = nc.tensor.transpose(turned[:, h, k, :], zs[:, h, k * P:(k + 1) * P], K.id16[:, :])
    tp = c.pe.mark(mm)
    nb.zs.give(j, tp, *stored)
    dst = w["zT"][:, :, :, t * P:(t + 1) * P]
    e = c.act if t % 2 == 0 else c.vec
    e.need(tp, *w["zT_free"])
    out = e.mark(nc.scalar.copy(dst, turned) if t % 2 == 0 else nc.vector.tensor_copy(dst, turned))
    nb.banks.give(bi, out)
    w["turned"].append(out)


def place(h):
    return (h % HG) * (HH // HG) + h // HG


class Consts:
    pass


def constants(c, ctx, I):
    nc, K = c.nc, Consts()
    sb = lambda n, s, d: ctx.enter_context(nc.sbuf_tensor(n, s, d))
    K.id32, K.id16, K.eps = sb("id32", [P, P], F32), sb("id16", [P, P], F16), sb("eps", [P, 1], F32)
    K.gates, K.tg, K.tgw = sb("gates", [P, 4], F32), sb("tg", [P, 4], F32), sb("tgw", [P, 4], F32)
    pg = c.port("gates_in")
    tok = c.pool.mark(nc.gpsimd.memset(K.id32[:, :], 0.0))
    c.pool.need(tok)
    tok = c.pool.mark(nc.gpsimd.affine_select(out=K.id32[:, :], in_=K.id32[:, :], compare_op=ALU.not_equal,
                                              fill=1.0, base=0, pattern=[[-1, P]], channel_multiplier=1))
    c.vec.need(tok)
    c.vec.mark(nc.vector.tensor_copy(K.id16[:, :], K.id32[:, :]))
    c.vec.mark(nc.vector.memset(K.eps[:, :], EPS))
    for i, g in enumerate((I["g_xattn"], I["g_ffn"])):
        got = pg.mark(nc.sync.dma_start(K.gates[:, 2 * i:2 * i + 2],
                                        g.rearrange("(a n) -> a n", a=1).broadcast_to([P, 2])))
        c.sp.need(got)
    c.act.need(got)
    tok = c.act.mark(nc.scalar.activation(K.tg[:, :], K.gates[:, :], ACT.Tanh))
    c.vec.need(tok)
    c.vec.mark(nc.vector.tensor_scalar(K.tgw[:, :], K.tg[:, :], 1.0 / WS, None, ALU.mult))
    c.meet()
    return K


def attention(c, K, I, layer, src, dst, R=None, oute=None):
    nc = c.nc
    L0 = layer == 0
    with ExitStack() as ctx:
        sb = lambda n, s, d: ctx.enter_context(nc.sbuf_tensor(f"at{layer}_{n}", s, d))
        port = lambda n: c.port(f"at{layer}_{n}")
        gen = Ring([ctx.enter_context(nc.psum_tensor(f"at{layer}_g{i}", [P, 512], F32)) for i in range(2)])
        trp = Ring([ctx.enter_context(nc.psum_tensor(f"at{layer}_t{i}", [P, 512], F32)) for i in range(2)])
        S = ctx.enter_context(nc.psum_tensor(f"at{layer}_S", [P, HH, 256], F32))
        nrm = NormBuffers(c, ctx, f"at{layer}", gen, turned=1)
        wq = sb("wq", [P, 2, KT, D], F16)
        wk, wv = sb("wk", [P, KT, D], F32), sb("wv", [P, KT, D], F32)
        kctx = sb("kctx", [P, KT, CTX], F32)
        rctx = sb("rctx", [P, KT, P], F32)
        KTn = sb("KT", [P, KT, CTX], F32)
        V = sb("V", [P, HEADS, P], F32)
        VR = sb("VR", [P, KT, P], F32)
        qT = Ring([sb(f"qT{i}", [P, KT, BLK], F32) for i in range(2)])
        s = Ring([sb(f"s{i}", [P, HH, CTX], F32) for i in range(3)])
        prob = Ring([sb(f"p{i}", [P, HH * (P + HD)], F32) for i in range(2)])
        pT = Ring([sb(f"pT{i}", [P, HH + 2, BLK], F32) for i in range(2)])
        mx, sm, rs = (Ring([sb(f"{n}{i}", [P, HH], F32) for i in range(3)]) for n in ("mx", "sm", "rs"))
        pw, pk, pv, pc, pr = (port(n) for n in ("wq", "wk", "wv", "kctx", "rctx"))
        pst = [port(f"st{i}") for i in range(3)]
        wk_d, wv_d, wq_d = (I[f"L{layer}_xattn_{n}"].rearrange("(k p) m -> p k m", p=P) for n in ("wkT", "wvT", "wqT"))
        stage = qT.bufs[0]
        load_split(c, stage[:, :, :], pw, lambda h: wq[:, h, :, :], wq_d)
        pk.mark(nc.sync.dma_start(wk[:, :, :], wk_d))
        pv.mark(nc.sync.dma_start(wv[:, :, :], wv_d))
        if L0:
            wo = sb("wo", [P, 2, KT, D], F16)
            oT = Ring([sb(f"oT{i}", [P, 2, KT, BLK], F16) for i in range(1)])
            bq, bqs, bk = sb("bq", [P, KT], F32), sb("bqs", [P, KT], F32), sb("bk", [P, KT], F32)
            bv, bo, tbo = sb("bv", [P, D], F32), sb("bo", [P, D], F32), sb("tbo", [P, D], F32)
            limi = [sb(f"mi{i}", [P, TPB, CTX], mybir.dt.int32) for i in range(1)]
            lim = Ring([sb(f"lim{i}", [P, TPB, CTX], F32) for i in range(2)])
            pb, pm = port("bias"), port("mask")
            stage1 = qT.bufs[1]
            load_split(c, stage1[:, :, :], port("wo"), lambda h: wo[:, h, :, :],
                       I["L0_xattn_woT"].rearrange("(k p) m -> p k m", p=P))
            with nc.allow_non_contiguous_dma(reason="biases by head dim, once"):
                for dstb, n in ((bq, "bq"), (bk, "bk")):
                    got = pb.mark(nc.sync.dma_start(dstb[:, :], I[f"L0_xattn_{n}"].rearrange("(k p) -> p k", p=P)))
            for dstb, n in ((bv, "bv"), (bo, "bo")):
                got = pb.mark(nc.sync.dma_start(dstb[:, :], I[f"L0_xattn_{n}"].rearrange("(a n) -> a n", a=1)
                                                .broadcast_to([P, D])))
            c.vec.need(got)
            c.vec.mark(nc.vector.tensor_scalar(bqs[:, :], bq[:, :], HD ** -0.5, None, ALU.mult))
            c.vec.mark(nc.vector.tensor_scalar(tbo[:, :], bo[:, :], K.tg[:, 0:1], None, ALU.mult))
        else:
            oF = Ring([sb(f"oF{i}", [P, KT, BLK], F32) for i in range(1)])
        c.vec.mark(nc.vector.memset(V[:, :, :], 0.0))
        c.vec.mark(nc.vector.memset(VR[:, :, :], 0.0))
        for b in prob.bufs:
            c.pool.mark(nc.gpsimd.memset(b[:, :], 0.0))
        if not L0:
            rb = ReturnBuffers(c, ctx)
        c.meet()

        with nc.Fori(0, BATCH) as g:
            for r in (gen, trp, qT, s, prob, pT, mx, sm, rs, *((oT, lim) if L0 else (oF,))):
                r.reset()
            nrm.reset()
            if not L0:
                rb.turn(g)
            gotc = pc.mark(nc.sync.dma_start(kctx[:, :, :], I["ctxT"][bass.ds(g, 1), :, :]
                                             .rearrange("a (k p) n -> p (a k) n", p=P)))
            gotr = pr.mark(nc.sync.dma_start(rctx[:, :, :], I["ctxR"][bass.ds(g, 1), :, :]
                                             .rearrange("a (k p) n -> p (a k) n", p=P)))
            blocks = {}

            def load(b):
                row = g * SEQ + b * BLK
                x, xi, got = load_tokens(c, nrm, src, row)
                w = blocks[b] = dict(x=x, xi=xi, got=got, row=row, tile=g * (SEQ // P) + b * TPB)
                if L0:
                    c.sp.need(*mask_free[0])
                    w["mask"] = pm.mark(nc.sync.dma_start(limi[0][:, :, :], I["mask"][bass.ds(row, BLK), :]
                                                          .rearrange("(t p) n -> p t n", p=P)))

            mask_free = [()]

            def limits(b):
                l, li, free = lim.take()
                c.vec.need(blocks[b]["mask"], *free)
                a = c.vec.mark(nc.vector.tensor_scalar(l[:, :, :], limi[0][:, :, :], 0.0, None, ALU.not_equal))
                mask_free[0] = (a,)
                c.vec.need(a)
                a = c.vec.mark(nc.vector.tensor_scalar(l[:, :, :], l[:, :, :], 1e30, -1e30, ALU.mult, ALU.add))
                c.vec.need(a)
                a = c.vec.mark(nc.vector.tensor_scalar(l[:, :, :], l[:, :, :], 100.0, None, ALU.add))
                blocks[b]["m"] = (l, li, a)

            def gather_returns_begin(b):
                begin_returns(c, R, rb, blocks[b])

            def gather_returns(b, t):
                gather_tile(c, rb, oute, blocks[b], t)

            def add_returns(b, t):
                add_tile(c, rb, blocks[b], t)

            def stats(b):
                statistics(c, K, nrm, blocks[b])

            def turn_z(b, t):
                turn_tile(c, K, nrm, blocks[b], t)

            def prepare(b, t):
                w = blocks[b]
                halves(c, nrm, w, t, c.vec)
                w["x_ready"] = w["x_done"]
                if L0:
                    c.pool.need(w["x_done"])
                    w["x_ready"] = c.pool.mark(nc.gpsimd.tensor_tensor(w["x"][:, t, :], w["x"][:, t, :],
                                                                       tbo[:, :], ALU.add))

            def project(b):
                w = blocks[b]
                q, qi, free = qT.take()
                c.act.need(*free)
                c.pe.need(*w["turned"])
                for m in range(KT):
                    bank, bi, free = gen.take()
                    c.pe.need(*free)
                    mm = split3(c, bank[:, :], lambda h, k: wq[:, h, k, m * P:(m + 1) * P],
                                lambda h, k: w["zT"][:, h, k, :], range(KT))
                    tok = c.pe.mark(mm)
                    c.act.need(tok)
                    sc = HD ** -0.5 / WS
                    if L0:
                        out = c.act.mark(nc.scalar.activation(q[:, m, :], bank[:, :], ACT.Identity,
                                                              bias=bqs[:, m:m + 1], scale=sc))
                    else:
                        out = c.act.mark(nc.scalar.activation(q[:, m, :], bank[:, :], ACT.Copy, scale=sc))
                    gen.give(bi, out)
                nrm.zT.give(w["zi"], tok)
                w["q"], w["qi"], w["q_ready"] = q, qi, out

            score_free = [()]

            def scores(b, u, t):
                w = blocks[b]
                c.pe.need(w["q_ready"], *score_free[0])
                for h in range(HH):
                    o, m = HD * (h % HG), 2 * u + h // HG
                    mm = nc.tensor.matmul(S[:, place(h), 0:CTX], w["q"][o:o + HD, m, t * P:(t + 1) * P],
                                          KTn[o:o + HD, m, :], start=True, stop=True)
                tok = c.pe.mark(mm)
                if (u, t) == (1, TPB - 1):
                    qT.give(w["qi"], tok)
                sb_, si, free = s.take()
                c.vec.need(*free)
                mxb, mi, free = mx.take()
                c.vec.need(*free)
                smb, smi, free = sm.take()
                c.vec.need(*free)
                rsb, ri, free = rs.take()
                c.vec.need(*free)
                c.vec.need(tok)
                if L0:
                    l, li, lt = w["m"]
                    c.vec.need(lt)
                    a = c.vec.mark(nc.vector.scalar_tensor_tensor(
                        sb_[:, :, :], S[:, :, 0:CTX], -100.0,
                        l[:, t:t + 1, :].broadcast_to([P, HH, CTX]), ALU.max, ALU.min))
                    score_free[0] = (a,)
                    if (u, t) == (1, TPB - 1):
                        lim.give(li, a)
                    c.vec.need(a)
                    top = c.vec.mark(nc.vector.tensor_reduce(mxb[:, :], sb_[:, :, :], AX.X, ALU.max))
                    c.pool.need(top)
                    sub = c.pool.mark(nc.gpsimd.tensor_tensor(
                        sb_[:, :, :], sb_[:, :, :], mxb[:, :, None].broadcast_to([P, HH, CTX]), ALU.subtract))
                else:
                    top = c.vec.mark(nc.vector.tensor_reduce(mxb[:, :], S[:, :, 0:CTX], AX.X, ALU.max))
                    c.vec.need(top)
                    sub = c.vec.mark(nc.vector.tensor_tensor(
                        sb_[:, :, :], S[:, :, 0:CTX], mxb[:, :, None].broadcast_to([P, HH, CTX]), ALU.subtract))
                    score_free[0] = (sub,)
                mx.give(mi, sub)
                return dict(b=b, u=u, t=t, s=sb_, si=si, sm=smb, smi=smi, rs=rsb, ri=ri, sub=sub)

            def exponentials(v):
                c.act.need(v["sub"])
                v["ex"] = c.act.mark(nc.scalar.activation(v["s"][:, :, :], v["s"][:, :, :], ACT.Exp))

            def probabilities(v):
                sb_, smb, rsb = v["s"], v["sm"], v["rs"]
                pb_, v["pi"], free = prob.take()
                c.pool.need(*free)
                v["p"] = pb_
                c.vec.need(v["ex"])
                a = c.vec.mark(nc.vector.tensor_reduce(smb[:, :], sb_[:, :, :], AX.X, ALU.add))
                c.vec.need(a)
                r = c.vec.mark(nc.vector.reciprocal(rsb[:, :], smb[:, :]))
                sm.give(v["smi"], r)
                c.pool.need(r)
                main = pb_[:, 0:HH * P].rearrange("p (h n) -> p h n", h=HH)
                rem = pb_[:, HH * P:].rearrange("p (j r n) -> p r j n", r=HG, n=HD)
                srem = sb_[:, :, P:CTX].rearrange("p (r j) n -> p r j n", r=HG)
                rrem = rsb[:, :].rearrange("p (r j) -> p r j", r=HG)[:, :, :, None]
                nc.gpsimd.tensor_tensor(main, sb_[:, :, 0:P], rsb[:, :, None].broadcast_to([P, HH, P]), ALU.mult)
                tok = c.pool.mark(nc.gpsimd.tensor_tensor(rem[:, :, :, 0:REM], srem,
                                                          rrem.broadcast_to([P, HG, HH // HG, REM]), ALU.mult))
                s.give(v["si"], tok)
                rs.give(v["ri"], tok)
                v["p_ready"] = tok

            def turn(v):
                w, u, t = blocks[v["b"]], v["u"], v["t"]
                if t == 0:
                    w["pT", u] = (*pT.take(), [])
                ptb, _, pT_free, outs = w["pT", u]
                c.pe.need(v["p_ready"])
                for j0 in range(0, HH + 2, 4):
                    n = min(4, HH + 2 - j0)
                    bank, bi, free = trp.take()
                    c.pe.need(*free)
                    for j in range(n):
                        mm = nc.tensor.transpose(bank[:, j * P:(j + 1) * P],
                                                 v["p"][:, (j0 + j) * P:(j0 + j + 1) * P], K.id32[:, :])
                    tok = c.pe.mark(mm)
                    e = c.vec if j0 == 8 else c.act
                    e.need(tok, *pT_free)
                    dst_ = ptb[:, j0:j0 + n, t * P:(t + 1) * P]
                    srcb = bank[:, 0:n * P].rearrange("p (j n) -> p j n", j=n)
                    out = e.mark(nc.vector.tensor_copy(dst_, srcb) if j0 == 8 else nc.scalar.copy(dst_, srcb))
                    trp.give(bi, out)
                    outs.append(out)
                prob.give(v["pi"], tok)

            def values(b, u):
                w = blocks[b]
                ptb, pti, _, ready = w["pT", u]
                c.pe.need(*ready)
                if u == 0:
                    w["o"], w["oi"], free = (oT if L0 else oF).take()
                    c.act.need(*free)
                    c.vec.need(*(oT if L0 else oF).was[w["oi"]])
                    w["o_ready"] = []
                for gi in range(2):
                    grp = 2 * u + gi
                    bank, bi, free = gen.take()
                    c.pe.need(*free)
                    for j in range(HG):
                        nc.tensor.matmul(bank[:, :], V[:, grp * HG + j, :],
                                         ptb[:, place(gi * HG + j), :],
                                         start=(j == 0), stop=False)
                    tok = c.pe.mark(nc.tensor.matmul(bank[:, :], VR[:, grp, :], ptb[:, HH + gi, :],
                                                     start=False, stop=True))
                    c.act.need(tok)
                    if L0:
                        hi = c.act.mark(nc.scalar.copy(w["o"][:, 0, grp, :], bank[:, :]))
                        c.vec.need(hi)
                        out = c.vec.mark(nc.vector.tensor_tensor(w["o"][:, 1, grp, :], bank[:, :],
                                                                 w["o"][:, 0, grp, :], ALU.subtract))
                    else:
                        out = c.act.mark(nc.scalar.copy(w["o"][:, grp, :], bank[:, :]))
                    gen.give(bi, out)
                    w["o_ready"].append(out)
                pT.give(pti, tok)

            def finish(b, tiles):
                w = blocks[b]
                x, xi = w["x"], w["xi"]
                c.pe.need(*w["o_ready"])
                for t in tiles:
                    bank, bi, free = gen.take()
                    c.pe.need(*free)
                    if L0:
                        mm = split3(c, bank[:, :], lambda h, k: w["o"][:, h, k, t * P:(t + 1) * P],
                                    lambda h, k: wo[:, h, k, :], range(KT))
                    else:
                        for k in range(KT):
                            mm = nc.tensor.transpose(bank[:, k * P:(k + 1) * P],
                                                     w["o"][:, k, t * P:(t + 1) * P], K.id32[:, :])
                    tok = c.pe.mark(mm)
                    c.vec.need(tok, w["x_ready"])
                    out = c.vec.mark(nc.vector.scalar_tensor_tensor(
                        x[:, t, :], bank[:, :], K.tgw[:, 0:1] if L0 else K.tg[:, 1:2], x[:, t, :],
                        ALU.mult, ALU.add))
                    gen.give(bi, out)
                if TPB - 1 not in tiles:
                    return
                (oT if L0 else oF).give(w["oi"], tok)
                c.sp.need(out)
                st = pst[xi].mark(nc.sync.dma_start(
                    dst[bass.ds(w["row"], BLK), :].rearrange("(t p) d -> p t d", p=P), x[:, :, :]))
                nrm.x.give(xi, st)

            load(0)
            c.pe.need(gotc, gotr)
            kv = []
            for m in range(KT):
                bank, bi, free = gen.take()
                c.pe.need(*free)
                for k in range(KT):
                    mm = nc.tensor.matmul(bank[:, 0:CTX], wk[:, k, m * P:(m + 1) * P], kctx[:, k, :],
                                          start=(k == 0), stop=(k == KT - 1))
                tok = c.pe.mark(mm)
                c.vec.need(tok)
                if L0:
                    out = c.vec.mark(nc.vector.tensor_scalar(KTn[:, m, :], bank[:, 0:CTX], bk[:, m:m + 1],
                                                             None, ALU.add))
                else:
                    out = c.vec.mark(nc.vector.tensor_copy(KTn[:, m, :], bank[:, 0:CTX]))
                gen.give(bi, out)
            for rem in range(2):
                bank, bi, free = gen.take()
                c.pe.need(*free)
                for k in range(KT):
                    mm = nc.tensor.matmul(bank[:, :], rctx[:, k, :] if rem else kctx[:, k, 0:P], wv[:, k, :],
                                          start=(k == 0), stop=(k == KT - 1))
                tok = c.pe.mark(mm)
                c.vec.need(tok)
                for h in range(HG):
                    rows = slice(HD * h, HD * h + HD) if rem else slice(0, P)
                    o = (VR[rows, :, HD * h:HD * h + HD] if rem else
                         V[:, :, :].rearrange("p (g h) n -> p g h n", h=HG)[:, :, h, HD * h:HD * h + HD])
                    i_ = bank[:, :].rearrange("p (g h n) -> p g h n", g=KT, h=HG)[rows, :, h, :]
                    if L0:
                        b_ = bv[:, :].rearrange("p (g h n) -> p g h n", g=KT, h=HG)[rows, :, h, :]
                        out = c.vec.mark(nc.vector.tensor_tensor(o, i_, b_, ALU.add))
                    else:
                        out = c.vec.mark(nc.vector.tensor_copy(o, i_))
                gen.give(bi, out)
            c.pe.need(out)
            UPB = 2 * TPB
            units = [(b, u, t) for b in range(NBB) for u in range(2) for t in range(TPB)]
            tasks = {n: [] for n in range(-1, len(units) + 8)}

            def plan(n, f, *args):
                tasks[max(n, -1)].append((f, args))

            for b in range(NBB):
                n = b * UPB
                if b:
                    plan(n - (8 if L0 else 10), load, b)
                if L0:
                    plan(n - 6, limits, b)
                else:
                    plan(n - 10, gather_returns_begin, b)
                    for t in range(TPB):
                        plan(n - 10 + t + t // 2, gather_returns, b, t)
                        plan(n - 8 + t + t // 2, add_returns, b, t)
                plan(n - 3, stats, b)
                for t in range(TPB):
                    plan(n - 3 + t // 2, prepare, b, t)
                    plan(n - 2 + t // 2, turn_z, b, t)
                plan(n - 1, project, b)
                for u in range(2):
                    plan(n + TPB * (u + 1) + 3, values, b, u)
                for t in range(2):
                    plan(n + UPB + 4 + t, finish, b, range(2 * t, 2 * t + 2))
            for f, args in tasks[-1]:
                f(*args)
            v = {}
            for n in range(len(units) + 8):
                if n - 3 in v:
                    turn(v[n - 3])
                if n - 2 in v:
                    probabilities(v[n - 2])
                if n < len(units):
                    v[n] = scores(*units[n])
                if n - 1 in v:
                    exponentials(v[n - 1])
                for f, args in tasks[n]:
                    f(*args)
            c.meet()


class Routing:

    def __init__(self, nc, ctx):
        sb = lambda n, s, d: ctx.enter_context(nc.sbuf_tensor(n, s, d))
        self.slots = sb("slots", [P, T // P, TOPK], U32)
        self.weights = sb("weights", [P, T // P, TOPK], F32)


def shared_and_route(c, K, I, R, src, dst, zrows, ids):
    nc = c.nc
    with ExitStack() as ctx:
        sb = lambda n, s, d: ctx.enter_context(nc.sbuf_tensor(f"sh_{n}", s, d))
        port = lambda n: c.port(f"sh_{n}")
        ps = lambda n, s: ctx.enter_context(nc.psum_tensor(f"sh_{n}", s, F32))
        gen = Ring([ps(f"g{i}", [P, 512]) for i in range(3)])
        gu = Ring([ps(f"gu{i}", [P, 2, 512]) for i in range(2)])
        LG = ps("LG", [P, TPB, E + 1])
        nrm = NormBuffers(c, ctx, "sh", gen)
        wgu, wdn = sb("wgu", [P, 2, KT, 2 * IS], F16), sb("wdn", [P, 2, FB, D], F16)
        wgt = sb("wgt", [P, 2, KT, E + 1], F16)
        actT = sb("actT", [P, 2, FB, BLK], F16)
        act32 = Ring([sb(f"a{i}", [P, BLK], F32) for i in range(2)])
        silu = Ring([sb(f"si{i}", [P, BLK], F32) for i in range(2)])
        stage = nrm.x.bufs
        pw, pst, pz, psc = port("w"), [port(f"st{i}") for i in range(3)], port("z"), [c.soft_port(f"sh_sc{i}", 16 * TPB * TOPK * NBB // 2) for i in range(2)]
        pzs = [port(f"zs{i}") for i in range(2)]
        tri, ones = sb("tri", [P, P], BF16), sb("ones", [P, P], BF16)
        one32 = sb("one32", [P, P], F32)
        iexp, iexpi = sb("iexp", [P, E], F32), sb("iexpi", [P, E], mybir.dt.int32)
        tokf, toki = sb("tokf", [P, TPB], F32), sb("toki", [P, TPB], mybir.dt.int32)
        tokb = Ring([sb(f"tk{i}", [P, TPB], F32) for i in range(2)])
        count, countb, sum4 = sb("count", [P, E], F32), sb("countb", [P, E], BF16), sb("sum4", [P, E], F32)
        ex, rep = sb("ex", [P, TPB, E], F32), sb("rep", [P, TPB, E], F32)
        M = sb("M", [P, TPB, E], BF16)
        top, idx, idxf = sb("top", [P, TPB, TOPK], F32), sb("idx", [P, TPB, TOPK], U32), sb("idxf", [P, TPB, TOPK], F32)
        mx, sm, rs = sb("mx", [P, TPB], F32), sb("sm", [P, TPB], F32), sb("rs", [P, TPB], F32)
        w8, slot, far = sb("w8", [P, TPB, TOPK], F32), sb("slot", [P, TPB, E], F32), sb("far", [P, TPB, E], F32)
        eq, slotk = sb("eq", [P, TPB, TOPK, E], F32), sb("slotk", [P, TPB, TOPK], F32)
        kept = sb("kept", [P, TPB, TOPK], F32)
        slotu = Ring([sb(f"su{i}", [P, TPB, TOPK], U32) for i in range(2)])
        sg = sb("sg", [P, TPB], F32)

        wgu_d = I["L0_ffn_shared_gate_up_w"].rearrange("(k p) n -> p k n", p=P)
        wdn_d = I["L0_ffn_shared_down_w"].rearrange("(k p) n -> p k n", p=P)
        last = ()
        for n in range(4):
            st = stage[n % 2]
            last = load_split(c, st[:, :, :], pw, lambda h: wgu[:, h, :, n * 512:(n + 1) * 512],
                              wgu_d[:, :, n * 512:(n + 1) * 512], after=last)
        for n in range(2):
            last = load_split(c, stage[n][:, :, :], pw, lambda h: wdn[:, h, 4 * n:4 * n + 4, :],
                              wdn_d[:, 4 * n:4 * n + 4, :], after=last)
        load_split(c, stage[0][:, :, 0:E + 1], pw, lambda h: wgt[:, h, :, :],
                   I["gates65"].rearrange("(k p) n -> p k n", p=P), after=last)
        a = c.pool.mark(nc.gpsimd.memset(one32[:, :], 1.0))
        c.pool.need(a)
        a = c.pool.mark(nc.gpsimd.affine_select(out=one32[:, :], in_=one32[:, :], compare_op=ALU.is_gt, fill=0.0,
                                                base=0, pattern=[[1, P]], channel_multiplier=-1))
        b = c.pool.mark(nc.gpsimd.iota(iexpi[:, :], pattern=[[CAP, E]], base=0, channel_multiplier=0))
        b = c.pool.mark(nc.gpsimd.iota(toki[:, :], pattern=[[P, TPB]], base=0, channel_multiplier=1))
        c.vec.need(a, b)
        c.vec.mark(nc.vector.tensor_copy(tri[:, :], one32[:, :]))
        c.vec.mark(nc.vector.memset(ones[:, :], 1.0))
        c.vec.mark(nc.vector.tensor_copy(iexp[:, :], iexpi[:, :]))
        c.vec.mark(nc.vector.tensor_copy(tokf[:, :], toki[:, :]))
        c.vec.mark(nc.vector.memset(count[:, :], 0.0))
        c.vec.mark(nc.vector.memset(countb[:, :], 0.0))
        z = c.vec.mark(nc.vector.memset(eq[:, :, :, :], 0.0))
        c.sp.need(z)
        pz.mark(nc.sync.dma_start(ids.rearrange("(p n) a -> p (n a)", p=P), eq[:, 0, 0:2, :].rearrange("p a b -> p (a b)")))
        c.meet()

        with nc.Fori(0, BATCH) as g:
            for r in (gen, gu, act32, silu, tokb, slotu):
                r.reset()
            nrm.reset()
            for q in psc:
                q.turn(g)
            blocks, held = {}, dict(route=(), scat=(), actT=(), LG=(), pos=())

            def load(b):
                row = g * SEQ + b * BLK
                x, xi, got = load_tokens(c, nrm, src, row)
                blocks[b] = dict(x=x, xi=xi, got=got, row=row)

            def keep_rows(b, t):
                w = blocks[b]
                halves(c, nrm, w, t, c.vec)
                zs, j, lo = w["zs", t]
                c.sp.need(lo)
                w["stored", t] = pzs[j].mark(nc.sync.dma_start(
                    zrows[bass.ds(w["row"] + t * P, P), :], zs[:, :, :].rearrange("p h d -> p (h d)")))

            def turn_rows(b, t):
                turn_tile(c, K, nrm, blocks[b], t, stored=(blocks[b]["stored", t],))

            def logits(b):
                w = blocks[b]
                c.pe.need(*w["turned"], *held["LG"])
                for t in range(TPB):
                    mm = split3(c, LG[:, t, :], lambda h, k: w["zT"][:, h, k, t * P:(t + 1) * P],
                                lambda h, k: wgt[:, h, k, :], range(KT))
                w["logits"] = c.pe.mark(mm)

            def choose(b):
                w = blocks[b]
                v = nc.vector
                c.vec.need(w["logits"], *held["route"])
                a = c.vec.mark(v.tensor_reduce(mx[:, :], LG[:, :, 0:E], AX.X, ALU.max))
                c.vec.need(a)
                a = c.vec.mark(v.tensor_tensor(ex[:, :, :], LG[:, :, 0:E], mx[:, :, None].broadcast_to([P, TPB, E]),
                                               ALU.subtract))
                c.act.need(a, w["logits"])
                e1 = c.act.mark(nc.scalar.activation(ex[:, :, :], ex[:, :, :], ACT.Exp, scale=1.0 / WS))
                e2 = c.act.mark(nc.scalar.activation(sg[:, :], LG[:, :, E], ACT.Exp, scale=-1.0 / WS))
                held["LG"] = (a, e2)
                c.vec.need(e1)
                for t in range(TPB):
                    a = c.vec.mark(v.max(top[:, t, :], ex[:, t, :]))
                c.vec.need(a)
                for t in range(TPB):
                    c.vec.mark(v.max_index(idx[:, t, :], top[:, t, :], ex[:, t, :]))
                    a = c.vec.mark(v.match_replace(rep[:, t, :], top[:, t, :], ex[:, t, :], -1.0))
                b_ = c.vec.mark(v.tensor_reduce(sm[:, :], top[:, :, :], AX.X, ALU.add))
                c.vec.need(a)
                w["chosen"] = c.vec.mark(v.tensor_scalar(M[:, :, :], rep[:, :, :], 0.0, None, ALU.is_lt))
                c.vec.mark(v.tensor_scalar(idxf[:, :, :], idx[:, :, :], float(CAP), None, ALU.mult))
                c.vec.need(b_)
                a = c.vec.mark(v.reciprocal(rs[:, :], sm[:, :]))
                c.vec.need(a, e2)
                c.vec.mark(v.tensor_tensor(w8[:, :, :], top[:, :, :], rs[:, :, None].broadcast_to([P, TPB, TOPK]),
                                           ALU.mult))
                a = c.vec.mark(v.tensor_scalar(sg[:, :], sg[:, :], 1.0, None, ALU.add))
                c.vec.need(a)
                a = c.vec.mark(v.reciprocal(sg[:, :], sg[:, :]))
                c.vec.need(a)
                w["sg"] = c.vec.mark(v.tensor_scalar(sg[:, :], sg[:, :], K.tgw[:, 2:3], None, ALU.mult))

            def positions(b):
                w = blocks[b]
                bank, bi, free = gen.take()
                c.pe.need(*free)
                c.pe.need(w["chosen"], *held["pos"])
                pos = bank[:, 0:TPB * E].rearrange("p (t e) -> p t e", t=TPB)
                for t in range(TPB):
                    nc.tensor.matmul(pos[:, t, :], ones[:, :], countb[:, :], start=True, stop=False)
                    for t2 in range(t):
                        nc.tensor.matmul(pos[:, t, :], ones[:, :], M[:, t2, :], start=False, stop=False)
                    mm = nc.tensor.matmul(pos[:, t, :], tri[:, :], M[:, t, :], start=False, stop=True)
                tok = c.pe.mark(mm)
                v = nc.vector
                c.vec.need(tok)
                a = c.vec.mark(v.tensor_tensor(slot[:, :, :], pos, iexp[:, None, :].broadcast_to([P, TPB, E]), ALU.add))
                b_ = c.vec.mark(v.tensor_scalar(far[:, :, :], pos, float(CAP), BIG, ALU.is_ge, ALU.mult))
                gen.give(bi, b_)
                c.vec.need(b_)
                a = c.vec.mark(v.tensor_tensor(slot[:, :, :], slot[:, :, :], far[:, :, :], ALU.max))
                d = c.vec.mark(v.tensor_reduce(sum4[:, :], M[:, :, :].rearrange("p t e -> p e t"), AX.X, ALU.add))
                c.vec.need(d)
                d = c.vec.mark(v.tensor_tensor(count[:, :], count[:, :], sum4[:, :], ALU.add))
                c.vec.need(d)
                d = c.vec.mark(v.tensor_copy(countb[:, :], count[:, :]))
                held["pos"] = (d,)
                shape = [P, TPB, TOPK, E]
                a = c.vec.mark(v.tensor_tensor(eq[:, :, :, :], iexp[:, None, None, :].broadcast_to(shape),
                                               idxf[:, :, :, None].broadcast_to(shape), ALU.is_equal))
                c.vec.need(a)
                a = c.vec.mark(v.tensor_tensor(eq[:, :, :, :], eq[:, :, :, :],
                                               slot[:, :, None, :].broadcast_to(shape), ALU.mult))
                c.vec.need(a)
                a = c.vec.mark(v.tensor_reduce(slotk[:, :, :], eq[:, :, :, :], AX.X, ALU.add))
                c.vec.need(a)
                su, si, free = slotu.take()
                c.vec.need(*free)
                tk, ti, free = tokb.take()
                c.vec.need(*free)
                tl = bass.ds(g * (SEQ // P) + b * TPB, TPB)
                c.vec.mark(v.tensor_copy(R.slots[:, tl, :], slotk[:, :, :]))
                c.vec.mark(v.tensor_copy(tk[:, :], tokf[:, :]))
                a = c.vec.mark(v.tensor_copy(su[:, :, :], slotk[:, :, :]))
                c.vec.need(a)
                c.vec.mark(v.tensor_scalar(tokf[:, :], tokf[:, :], float(BLK), None, ALU.add))
                k = c.vec.mark(v.tensor_scalar(kept[:, :, :], slotk[:, :, :], BIG, K.tg[:, 2:3], ALU.is_lt, ALU.mult))
                c.vec.need(k)
                k = c.vec.mark(v.tensor_tensor(R.weights[:, tl, :], w8[:, :, :], kept[:, :, :], ALU.mult))
                held["route"] = (k, tok)
                c.pool.need(a)
                for t in range(TPB):
                    for j in range(TOPK):
                        s_ = psc[si].mark(nc.gpsimd.indirect_dma_start(
                            ids, bass.IndirectOffsetOnAxis(su[:, t, j:j + 1], 0), tk[:, t:t + 1], None,
                            bounds_check=SLOTS - 1, oob_is_err=False))
                slotu.give(si, s_)
                tokb.give(ti, s_)

            def up(b, f):
                w = blocks[b]
                bank, bi, free = gu.take()
                c.pe.need(*free)
                for j in range(2):
                    o = j * IS + f * P
                    mm = split3(c, bank[:, j, :], lambda h, k: wgu[:, h, k, o:o + P],
                                lambda h, k: w["zT"][:, h, k, :], range(KT))
                tok = c.pe.mark(mm)
                si_, sii, free = silu.take()
                c.act.need(*free)
                c.act.need(tok)
                s_ = c.act.mark(nc.scalar.activation(si_[:, :], bank[:, 0, :], ACT.Silu, scale=1.0 / WS))
                a_, ai, free = act32.take()
                c.vec.need(*free)
                c.vec.need(s_, tok)
                a = c.vec.mark(nc.vector.scalar_tensor_tensor(a_[:, :], bank[:, 1, :], 1.0 / WS, si_[:, :],
                                                              ALU.mult, ALU.mult))
                gu.give(bi, s_, a)
                silu.give(sii, a)
                c.act.need(a, *(held["actT"] if f == 0 else ()))
                hi = c.act.mark(nc.scalar.copy(actT[:, 0, f, :], a_[:, :]))
                w["a"] = (a_, ai, hi, f)
                if f == FB - 1:
                    nrm.zT.give(w["zi"], tok)

            def low(b):
                a_, ai, hi, f = blocks[b]["a"]
                c.vec.need(hi)
                lo = c.vec.mark(nc.vector.tensor_tensor(actT[:, 1, f, :], a_[:, :], actT[:, 0, f, :], ALU.subtract))
                act32.give(ai, lo)
                blocks[b]["lo"] = lo

            def down(b):
                w = blocks[b]
                x = w["x"]
                c.pe.need(w["lo"])
                for t in range(TPB):
                    bank, bi, free = gen.take()
                    c.pe.need(*free)
                    mm = split3(c, bank[:, :], lambda h, k: actT[:, h, k, t * P:(t + 1) * P],
                                lambda h, k: wdn[:, h, k, :], range(FB))
                    tok = c.pe.mark(mm)
                    c.vec.need(tok, w["sg"])
                    out = c.vec.mark(nc.vector.scalar_tensor_tensor(x[:, t, :], bank[:, :], sg[:, t:t + 1],
                                                                    x[:, t, :], ALU.mult, ALU.add))
                    gen.give(bi, out)
                held["actT"] = (tok,)
                c.sp.need(out)
                st = pst[w["xi"]].mark(nc.sync.dma_start(
                    dst[bass.ds(w["row"], BLK), :].rearrange("(t p) d -> p t d", p=P), x[:, :, :]))
                nrm.x.give(w["xi"], st)

            load(0)
            statistics(c, K, nrm, blocks[0])
            for t in range(TPB):
                keep_rows(0, t)
                turn_rows(0, t)
            logits(0)
            choose(0)
            for b in range(NBB):
                nxt = b + 1 < NBB
                if nxt:
                    load(b + 1)
                for f in range(FB):
                    up(b, f)
                    if f == 1:
                        positions(b)
                    if nxt and f == 3:
                        statistics(c, K, nrm, blocks[b + 1])
                    if nxt and f >= 4:
                        keep_rows(b + 1, f - 4)
                    if nxt and f >= 5:
                        turn_rows(b + 1, f - 5)
                    low(b)
                if nxt:
                    turn_rows(b + 1, 3)
                    logits(b + 1)
                down(b)
                if nxt:
                    choose(b + 1)
            c.meet()


def experts(c, K, I, zrows, ids, oute):
    nc = c.nc
    with ExitStack() as ctx:
        sb = lambda n, s, d: ctx.enter_context(nc.sbuf_tensor(f"ex_{n}", s, d))
        port = lambda n: c.port(f"ex_{n}")
        ps = lambda n, s: ctx.enter_context(nc.psum_tensor(f"ex_{n}", s, F32))
        NS = CAP // P
        EK = EI // P
        tr = Ring([ps(f"t{i}", [P, 512]) for i in range(2)])
        gu = Ring([ps(f"gu{i}", [P, 2, 512]) for i in range(2)])
        ob = Ring([ps(f"o{i}", [P, 512]) for i in range(2)])
        rows, idxu = sb("rows", [P, P], F32), sb("idxu", [P, E * NS], U32)
        cols = sb("cols", [P, EPL * NS], U32)
        st1 = Ring([sb(f"w1_{i}", [P, KT, 2 * EI], F32) for i in range(3)])
        st2 = Ring([sb(f"w2_{i}", [P, EK, D], F32) for i in range(3)])
        w1 = Ring([sb(f"h1_{i}", [P, 2, KT, 2 * EI], F16) for i in range(2)])
        w2 = Ring([sb(f"h2_{i}", [P, 2, EK, D], F16) for i in range(3)])
        xg = Ring([sb(f"xg{i}", [P, 2, KT, P], F16) for i in range(4)])
        xT = Ring([sb(f"xT{i}", [P, 2, KT, CAP], F16) for i in range(2)])
        silu, a32 = (Ring([sb(f"{n}{i}", [P, EK, CAP], F32) for i in range(2)]) for n in ("si", "a"))
        aT = Ring([sb(f"aT{i}", [P, 2, EK, CAP], F16) for i in range(2)])
        o32 = Ring([sb(f"oo{i}", [P, NS, D], F32) for i in range(2)])
        p1, p2 = [port(f"w1{i}") for i in range(3)], [port(f"w2{i}") for i in range(3)]
        px, po, pi = [c.soft_port(f"ex_x{i}", 16 * EPL * NS // 4) for i in range(4)], [port(f"o{i}") for i in range(2)], port("ids")
        got = pi.mark(nc.sync.dma_start(rows[:, :], ids.rearrange("(r n) a -> r (n a)", r=P)))
        c.pe.need(got)
        bank, _, free = tr.take()
        c.pe.need(*free)
        tok = c.pe.mark(nc.tensor.transpose(bank[:, 0:P], rows[:, :], K.id32[:, :]))
        c.vec.need(tok)
        c.vec.mark(nc.vector.tensor_copy(idxu[:, :], bank[:, 0:P]))
        c.meet()
        with nc.Fori(0, E // EPL) as g:
            for r in (tr, gu, ob, st1, st2, w1, w2, xg, xT, silu, a32, aT, o32):
                r.reset()
            for q in px:
                q.turn(g)
            ci = c.vec.mark(nc.vector.tensor_copy(cols[:, :], idxu[:, bass.ds(g * (EPL * NS), EPL * NS)]))
            ex = {}

            def fetch(e):
                q = ex[e] = {}
                q["s1"], q["i1"], free = st1.take()
                c.sp.need(*free)
                q["g1"] = p1[q["i1"]].mark(nc.sync.dma_start(
                    q["s1"][:, :, :], I["L0_ffn_expert_gate_up_w"][bass.ds(g * EPL + e, 1), :, :]
                    .rearrange("a (k p) n -> p (a k) n", p=P)))
                q["s2"], q["i2"], free = st2.take()
                c.sp.need(*free)
                q["g2"] = p2[q["i2"]].mark(nc.sync.dma_start(
                    q["s2"][:, :, :], I["L0_ffn_expert_down_w"][bass.ds(g * EPL + e, 1), :, :]
                    .rearrange("a (k p) n -> p (a k) n", p=P)))
                q["x"] = []
                for s in range(NS):
                    x, xi, free = xg.take()
                    c.pool.need(*free)
                    c.pool.need(ci)
                    n = e * NS + s
                    gx = px[xi].mark(nc.gpsimd.indirect_dma_start(
                        x[:, :, :, :].rearrange("p h k n -> p (h k n)"), None, zrows,
                        bass.IndirectOffsetOnAxis(cols[:, n:n + 1], 0)))
                    q["x"].append((x, xi, gx))

            def split_weights(e):
                q = ex[e]
                q["w1"], q["j1"], free = w1.take()
                c.act.need(q["g1"], *free)
                q["w1r"] = []
                for k in range(0, KT, 2):
                    h1 = c.act.mark(nc.scalar.activation(q["w1"][:, 0, k:k + 2, :], q["s1"][:, k:k + 2, :],
                                                         ACT.Copy, scale=WS))
                    c.vec.need(h1)
                    q["w1r"].append(c.vec.mark(nc.vector.scalar_tensor_tensor(
                        q["w1"][:, 1, k:k + 2, :], q["s1"][:, k:k + 2, :], WS, q["w1"][:, 0, k:k + 2, :],
                        ALU.mult, ALU.subtract)))
                st1.give(q["i1"], q["w1r"][-1])
                q["w2"], q["j2"], free = w2.take()
                c.act.need(q["g2"], *free)
                h2 = c.act.mark(nc.scalar.activation(q["w2"][:, 0, :, :], q["s2"][:, :, :], ACT.Copy, scale=WS))
                c.vec.need(h2)
                q["w2r"] = c.vec.mark(nc.vector.scalar_tensor_tensor(
                    q["w2"][:, 1, :, :], q["s2"][:, :, :], WS, q["w2"][:, 0, :, :], ALU.mult, ALU.subtract))
                st2.give(q["i2"], q["w2r"])

            def turn_rows(e):
                q = ex[e]
                xt, q["xti"], xT_free = xT.take()
                q["xT"], q["xTr"] = xt, []
                for s, (x, xi, gx) in enumerate(q["x"]):
                    bank, bi, free = tr.take()
                    c.pe.need(gx, *free)
                    turned = bank[:, :].bitcast(F16).rearrange("p (h k n) -> p h k n", h=2, k=KT)
                    for h in range(2):
                        for k in range(KT):
                            mm = nc.tensor.transpose(turned[:, h, k, :], x[:, h, k, :], K.id16[:, :])
                    tok = c.pe.mark(mm)
                    xg.give(xi, tok)
                    en = c.act if s == 0 else c.vec
                    en.need(tok, *xT_free)
                    d_ = xt[:, :, :, s * P:(s + 1) * P]
                    out = en.mark(nc.scalar.copy(d_, turned) if s == 0 else nc.vector.tensor_copy(d_, turned))
                    tr.give(bi, out)
                    q["xTr"].append(out)

            def up(e):
                q = ex[e]
                bank, bi, free = gu.take()
                c.pe.need(*q["xTr"], *q["w1r"], *free)
                for f in range(2 * EK):
                    mm = split3(c, bank[:, f // EK, (f % EK) * CAP:(f % EK + 1) * CAP],
                                lambda h, k: q["w1"][:, h, k, f * P:(f + 1) * P],
                                lambda h, k: q["xT"][:, h, k, :], range(KT))
                q["up"] = tok = c.pe.mark(mm)
                w1.give(q["j1"], tok)
                xT.give(q["xti"], tok)
                q["bank"], q["bi"] = bank, bi

            def activate(e):
                q = ex[e]
                si_, sii, free = silu.take()
                c.act.need(q["up"], *free)
                G, U = (q["bank"][:, j, :].rearrange("p (k n) -> p k n", k=EK) for j in range(2))
                s_ = c.act.mark(nc.scalar.activation(si_[:, :, :], G, ACT.Silu, scale=1.0 / WS))
                a_, ai, free = a32.take()
                c.vec.need(s_, *free)
                a = c.vec.mark(nc.vector.scalar_tensor_tensor(a_[:, :, :], U, 1.0 / WS, si_[:, :, :],
                                                              ALU.mult, ALU.mult))
                gu.give(q["bi"], s_, a)
                silu.give(sii, a)
                at, ati, free = aT.take()
                c.act.need(a, *free)
                hi = c.act.mark(nc.scalar.copy(at[:, 0, :, :], a_[:, :, :]))
                c.vec.need(hi)
                q["aTr"] = c.vec.mark(nc.vector.tensor_tensor(at[:, 1, :, :], a_[:, :, :], at[:, 0, :, :],
                                                              ALU.subtract))
                a32.give(ai, q["aTr"])
                q["aT"], q["ati"] = at, ati

            def down(e):
                q = ex[e]
                c.pe.need(q["aTr"], q["w2r"])
                o, oi, free = o32.take()
                c.act.need(*free)
                for s in range(NS):
                    bank, bi, free = ob.take()
                    c.pe.need(*free)
                    mm = split3(c, bank[:, :], lambda h, k: q["aT"][:, h, k, s * P:(s + 1) * P],
                                lambda h, k: q["w2"][:, h, k, :], range(EK))
                    tok = c.pe.mark(mm)
                    c.act.need(tok)
                    out = c.act.mark(nc.scalar.activation(o[:, s, :], bank[:, :], ACT.Copy, scale=1.0 / WS))
                    ob.give(bi, out)
                w2.give(q["j2"], tok)
                aT.give(q["ati"], tok)
                c.sp.need(out)
                st = po[oi].mark(nc.sync.dma_start(
                    oute[bass.ds((g * EPL + e) * CAP, CAP), :].rearrange("(s p) d -> p s d", p=P), o[:, :, :]))
                o32.give(oi, st)

            fetch(0)
            fetch(1)
            split_weights(0)
            turn_rows(0)
            fetch(2)
            up(0)
            split_weights(1)
            turn_rows(1)
            activate(0)
            for e in range(EPL):
                if e + 1 < EPL:
                    up(e + 1)
                if e + 3 < EPL:
                    fetch(e + 3)
                if e + 2 < EPL:
                    split_weights(e + 2)
                    turn_rows(e + 2)
                if e + 1 < EPL:
                    activate(e + 1)
                down(e)
            c.meet()


class ReturnBuffers:

    def __init__(self, c, ctx):
        nc = c.nc
        sb = lambda n, s, d: ctx.enter_context(nc.sbuf_tensor(f"rt_{n}", s, d))
        self.rows = Ring([sb(f"g{i}", [P, TOPK, D], F32) for i in range(2)])
        self.slots, self.weights = sb("at", [P, TPB, TOPK], U32), sb("w", [P, TPB, TOPK], F32)
        self.ports = [c.soft_port(f"rt_p{i}", 16 * TOPK * TPB * NBB // 2) for i in range(2)]
        for b in self.rows.bufs:
            c.vec.mark(nc.vector.memset(b[:, :, :], 0.0))

    def turn(self, g):
        self.rows.reset()
        self.gathered, self.added = (), ()
        for q in self.ports:
            q.turn(g)


def begin_returns(c, R, rb, w):
    nc = c.nc
    c.vec.need(*rb.gathered, *rb.added)
    w["slots"] = c.vec.mark(nc.vector.tensor_copy(rb.slots[:, :, :], R.slots[:, bass.ds(w["tile"], TPB), :]))
    w["weights"] = c.vec.mark(nc.vector.tensor_copy(rb.weights[:, :, :], R.weights[:, bass.ds(w["tile"], TPB), :]))


def gather_tile(c, rb, oute, w, t):
    buf, bi, free = rb.rows.take()
    c.pool.need(w["slots"], *free)
    for k in range(TOPK):
        tok = rb.ports[bi].mark(c.nc.gpsimd.indirect_dma_start(
            buf[:, k, :], None, oute, bass.IndirectOffsetOnAxis(rb.slots[:, t, k:k + 1], 0),
            bounds_check=SLOTS - 1, oob_is_err=False))
    rb.gathered = (tok,)
    w["rows", t] = (buf, bi, tok)


def add_tile(c, rb, w, t):
    x = w["x"]
    buf, bi, tok = w["rows", t]
    c.vec.need(w["got"], w["weights"], tok)
    for k in range(TOPK):
        a = c.vec.mark(c.nc.vector.scalar_tensor_tensor(x[:, t, :], buf[:, k, :], rb.weights[:, t, k:k + 1],
                                                        x[:, t, :], ALU.mult, ALU.add))
        c.vec.need(a)
    rb.rows.give(bi, a)
    rb.added = (a,)


def fused_experts(c, K, I, src, dst):
    nc = c.nc
    PS = 1.0 / 64.0
    with ExitStack() as ctx:
        sb = lambda n, s, d: ctx.enter_context(nc.sbuf_tensor(f"fe_{n}", s, d))
        port = lambda n: c.port(f"fe_{n}")
        ps = lambda n, s: ctx.enter_context(nc.psum_tensor(f"fe_{n}", s, F32))
        gen = Ring([ps(f"g{i}", [P, 512]) for i in range(2)])
        trio = Ring([ps(f"p{i}", [P, 3, 512]) for i in range(2)])
        nrm = NormBuffers(c, ctx, "fe", gen)
        NJ = 2 * KR // P
        left, right = ([sb(f"{n}{i}", [P, 2, KT, KR], F16) for i in range(2)] for n in ("lf", "rt"))
        router = [sb(f"ro{i}", [P, 2, KT, RH], F16) for i in range(2)]
        up = sb("up", [P, 2, NJ, D], F16)
        cz = Ring([sb(f"cz{i}", [P, KT, BLK], F32) for i in range(2)])
        czs = sb("czs", [P, 2, KT, BLK], F16)
        h32 = Ring([sb(f"h{i}", [P, KT, BLK], F32) for i in range(2)])
        prodT = sb("prodT", [P, 2, NJ, BLK], F16)
        t32, p32, c32 = (Ring([sb(f"{n}{i}", [P, BLK], F32) for i in range(2)]) for n in ("t", "pp", "c"))
        r2 = sb("r2", [P, KT, KE], F32)
        b1 = sb("b1", [P, KT], F32)
        b2, b2x, alpha = sb("b2", [P, KE], F32), sb("b2x", [P, KE], F32), sb("alpha", [P, 1], F32)
        bT, bo = sb("bT", [P, KT, P], F32), sb("bo", [2 * KE, 2, D], F16)
        sel32, sel = sb("sel32", [2 * KE, NJ, P], F32), sb("sel", [2 * KE, NJ, P], F16)
        lg, ex = sb("lg", [P, TPB, 2, KE], F32), sb("exr", [P, TPB, 2, KE], F32)
        mx, sm, rs = (sb(n, [P, TPB, 2], F32) for n in ("mx", "sm", "rs"))
        wr = sb("wr", [P, TPB, 2, KE], F32)
        wT = Ring([sb(f"wT{i}", [2 * KE, 2, BLK], F16) for i in range(2)])
        ni, nf = sb("ni", [P, SEQ // P], mybir.dt.int32), sb("nf", [P, SEQ // P], F32)
        pst = [port(f"st{i}") for i in range(3)]
        pl = [port(f"l{i}") for i in range(5)]
        psm = port("small")

        view = lambda n: I["L1_ffn_" + n].rearrange("(k p) m -> p k m", p=P)
        bufs = [*nrm.x.bufs, h32.bufs[1], cz.bufs[0], cz.bufs[1], h32.bufs[0]]
        wq, wk, winv = bufs[0:3]
        q1 = pl[0].mark(nc.sync.dma_start(wq[:, :, :], view("W_Q")))
        q3 = pl[2].mark(nc.sync.dma_start(winv[:, :, :], view("W_inv")))
        q2 = pl[1].mark(nc.sync.dma_start(wk[:, :, :], view("W_K")))
        small = lambda d_, s_: psm.mark(nc.sync.dma_start(d_, s_))
        small(bT[:, :, :], I["L1_ffn_bT"].rearrange("(k p) m -> p k m", p=P))
        small(r2[:, :, :], I["L1_ffn_router_w2T"].rearrange("(k p) m -> p k m", p=P))
        with nc.allow_non_contiguous_dma(reason="a bias by feature, once"):
            small(b1[:, :], I["L1_ffn_router_b1"].rearrange("(k p) -> p k", p=P))
        row = lambda n, w: I["L1_ffn_" + n].rearrange("(a n) -> a n", a=1).broadcast_to([P, w])
        small(b2[:, :], row("router_b2", KE))
        small(b2x[:, :], row("expert_bias", KE))
        sm_in = small(alpha[:, :], row("alpha_bi", 1))
        xs, bs = Ring([bufs[3], bufs[4]]), Ring([bufs[5], bufs[6]])

        def fetch(name):
            b, i, free = xs.take()
            c.sp.need(*free)
            return b, i, pl[3 + i].mark(nc.sync.dma_start(b[:, :, :], view(name)))

        def chain(lhs, lhs_in, rhs, rhs_in, out32=None, out16=None, after=()):
            c.pe.need(*lhs_in, *rhs_in)
            for m in range(KT):
                bank, bi, free = gen.take()
                c.pe.need(*free)
                for k in range(KT):
                    mm = nc.tensor.matmul(bank[:, :], lhs[:, k, m * P:(m + 1) * P], rhs[:, k, :],
                                          start=(k == 0), stop=(k == KT - 1))
                tok = c.pe.mark(mm)
                c.act.need(tok, *after)
                if out32 is not None:
                    out = c.act.mark(nc.scalar.copy(out32[:, m, :], bank[:, :]))
                else:
                    hi = c.act.mark(nc.scalar.activation(out16(0, m), bank[:, :], ACT.Copy, scale=WS))
                    c.vec.need(hi)
                    out = c.vec.mark(nc.vector.scalar_tensor_tensor(out16(1, m), bank[:, :], WS, out16(0, m),
                                                                    ALU.mult, ALU.subtract))
                gen.give(bi, out)
            return tok, out

        for name, proj, qp, into in (("W_inv_exp", wq, q1, left[1]), ("V_inv", wk, q2, right[1]),
                                     ("router_w1T", wq, q1, router[1])):
            f, fi, fin_ = fetch(name)
            m_, mi, free = bs.take()
            c.act.need(*free)
            tok, out = chain(winv, (q3,), f, (fin_,), out32=m_)
            if name != "router_w1T":
                xs.give(fi, tok)
            tok, _ = chain(proj, (qp,), m_, (out,), out16=lambda h, m: into[:, h, m, :])
            bs.give(mi, tok)
        tok, _ = chain(wq, (q1,), f, (), out16=lambda h, m: router[0][:, h, m, :])
        xs.give(fi, tok)
        for name, proj, qp, into in (("V_fwd", wq, q1, left[0]), ("W_fwd", wk, q2, right[0])):
            f, fi, fin_ = fetch(name)
            tok, _ = chain(proj, (qp,), f, (fin_,), out16=lambda h, m: into[:, h, m, :])
            xs.give(fi, tok)
        c.sp.need(tok)
        wo = winv
        q3 = pl[2].mark(nc.sync.dma_start(wo[:, :, :], view("W_OT")))
        for i, name in enumerate(("U_fwd", "U_inv")):
            f, fi, fin_ = fetch(name)
            tok, _ = chain(f, (fin_,), wo, (q3,), out16=lambda h, m: up[:, h, i * KT + m, :])
            xs.give(fi, tok)
        c.pe.need(sm_in)
        bank, bi, free = gen.take()
        c.pe.need(*free)
        for k in range(KT):
            mm = nc.tensor.matmul(bank[:, :], bT[:, k, :], wo[:, k, :], start=(k == 0), stop=(k == KT - 1))
        tok = c.pe.mark(mm)
        c.act.need(tok)
        hi = c.act.mark(nc.scalar.activation(bo[:, 0, :], bank[0:2 * KE, :], ACT.Copy, scale=WS * PS))
        c.vec.need(hi)
        gen.give(bi, c.vec.mark(nc.vector.scalar_tensor_tensor(bo[:, 1, :], bank[0:2 * KE, :], WS * PS, bo[:, 0, :],
                                                               ALU.mult, ALU.subtract)))
        a = c.pool.mark(nc.gpsimd.memset(sel32[:, :, :], 1.0))
        c.pool.need(a)
        a = c.pool.mark(nc.gpsimd.affine_select(out=sel32[:, :, :], in_=sel32[:, :, :], compare_op=ALU.is_ge, fill=0.0,
                                                base=0, pattern=[[P, NJ], [1, P]], channel_multiplier=-RR))
        c.pool.need(a)
        a = c.pool.mark(nc.gpsimd.affine_select(out=sel32[:, :, :], in_=sel32[:, :, :], compare_op=ALU.is_ge, fill=0.0,
                                                base=RR - 1, pattern=[[-P, NJ], [-1, P]], channel_multiplier=RR))
        b_ = c.pool.mark(nc.gpsimd.iota(ni[:, :], pattern=[[P, SEQ // P]], base=1, channel_multiplier=1))
        c.vec.need(a, b_, sm_in)
        c.vec.mark(nc.vector.tensor_copy(sel[:, :, :], sel32[:, :, :]))
        c.vec.mark(nc.vector.tensor_tensor(b2[:, :], b2[:, :], b2x[:, :], ALU.add))
        a = c.vec.mark(nc.vector.tensor_copy(nf[:, :], ni[:, :]))
        c.vec.need(a)
        a = c.vec.mark(nc.vector.reciprocal(nf[:, :], nf[:, :]))
        c.vec.need(a)
        c.vec.mark(nc.vector.tensor_scalar(nf[:, :], nf[:, :], K.tgw[:, 3:4], 1.0 / PS, ALU.mult, ALU.mult))
        c.meet()

        with nc.Fori(0, BATCH) as g:
            for r in (gen, trio, cz, h32, t32, p32, c32, wT):
                r.reset()
            nrm.reset()
            blocks, held = {}, dict(czs=(), prod=(), lg=())

            def load(b):
                row_ = g * SEQ + b * BLK
                x, xi, got = load_tokens(c, nrm, src, row_)
                blocks[b] = dict(x=x, xi=xi, got=got, row=row_)

            def running(b):
                w = blocks[b]
                s_, w["ci"], free = cz.take()
                c.vec.need(*free, *w["turned"])
                before = blocks[b - 1] if b else None
                if b:
                    c.vec.need(before["scan"])
                for k in range(KT):
                    w["scan"] = c.vec.mark(nc.vector.tensor_tensor_scan(
                        s_[:, k, :], w["zT"][:, 0, k, :], w["zT"][:, 1, k, :],
                        before["cz"][:, k, BLK - 1:BLK] if b else 0.0, ALU.add, ALU.add))
                w["cz"] = s_
                if b:
                    cz.give(before["ci"], *before["cz_used"], w["scan"])
                w["cz_used"] = ()

            def halve(b):
                w = blocks[b]
                c.act.need(w["scan"], *held["czs"])
                for k in range(KT):
                    hi = c.act.mark(nc.scalar.copy(czs[:, 0, k, :], w["cz"][:, k, :]))
                    c.pool.need(hi)
                    w["czs"] = c.pool.mark(nc.gpsimd.tensor_tensor(czs[:, 1, k, :], w["cz"][:, k, :],
                                                                   czs[:, 0, k, :], ALU.subtract))
                w["cz_used"] = (w["czs"],)

            def route(b):
                w = blocks[b]
                c.pe.need(*w["turned"])
                v = nc.vector
                c.vec.need(*held["lg"])
                hidden = []
                for r in range(2):
                    h_, hi_, free = h32.take()
                    c.act.need(*free)
                    for m in range(KT):
                        bank, bi, free = gen.take()
                        c.pe.need(*free)
                        tok = c.pe.mark(split3(c, bank[:, :], lambda h, k: router[r][:, h, k, m * P:(m + 1) * P],
                                               lambda h, k: w["zT"][:, h, k, :], range(KT)))
                        c.act.need(tok)
                        a = c.act.mark(nc.scalar.activation(h_[:, m, :], bank[:, :], ACT.Gelu, bias=b1[:, m:m + 1],
                                                            scale=1.0 / WS))
                        gen.give(bi, a)
                    hidden.append((h_, hi_, a))
                for r, (h_, hi_, a) in enumerate(hidden):
                    bank, bi, free = gen.take()
                    c.pe.need(*free)
                    c.pe.need(a)
                    for t in range(TPB):
                        for k in range(KT):
                            mm = nc.tensor.matmul(bank[:, t * KE:(t + 1) * KE], h_[:, k, t * P:(t + 1) * P],
                                                  r2[:, k, :], start=(k == 0), stop=(k == KT - 1))
                    tok = c.pe.mark(mm)
                    h32.give(hi_, tok)
                    c.vec.need(tok)
                    a = c.vec.mark(v.tensor_tensor(
                        lg[:, :, r, :], bank[:, 0:TPB * KE].rearrange("p (t e) -> p t e", t=TPB),
                        b2[:, None, :].broadcast_to([P, TPB, KE]), ALU.add))
                    gen.give(bi, a)
                shape = [P, TPB, 2, KE]
                c.vec.need(a)
                a = c.vec.mark(v.tensor_reduce(mx[:, :, :], lg[:, :, :, :], AX.X, ALU.max))
                c.vec.need(a)
                a = c.vec.mark(v.tensor_tensor(lg[:, :, :, :], lg[:, :, :, :], mx[:, :, :, None].broadcast_to(shape),
                                               ALU.subtract))
                c.act.need(a)
                e = c.act.mark(nc.scalar.activation(ex[:, :, :, :], lg[:, :, :, :], ACT.Exp))
                c.vec.need(e)
                a = c.vec.mark(v.tensor_reduce(sm[:, :, :], ex[:, :, :, :], AX.X, ALU.add))
                c.vec.need(a)
                a = c.vec.mark(v.reciprocal(rs[:, :, :], sm[:, :, :]))
                c.vec.need(a)
                a = c.vec.mark(v.tensor_scalar(rs[:, :, 1], rs[:, :, 1], alpha[:, 0:1], None, ALU.mult))
                c.vec.need(a)
                w["wr"] = c.vec.mark(v.tensor_tensor(wr[:, :, :, :], ex[:, :, :, :],
                                                     rs[:, :, :, None].broadcast_to(shape), ALU.mult))

            def turn_weights(b):
                w = blocks[b]
                bank, bi, free = gen.take()
                c.pe.need(*free)
                c.pe.need(w["wr"])
                for t in range(TPB):
                    mm = nc.tensor.transpose(bank[0:2 * KE, t * P:(t + 1) * P],
                                             wr[:, t, :, :].rearrange("p r e -> p (r e)"), K.id32[:, :])
                tok = c.pe.mark(mm)
                held["lg"] = (tok,)
                o, w["wi"], free = wT.take()
                c.act.need(*free)
                c.vec.need(*wT.was[w["wi"]])
                c.act.need(tok)
                hi = c.act.mark(nc.scalar.copy(o[:, 0, :], bank[0:2 * KE, :]))
                c.vec.need(hi)
                w["wTr"] = c.vec.mark(nc.vector.tensor_tensor(o[:, 1, :], bank[0:2 * KE, :], o[:, 0, :], ALU.subtract))
                gen.give(bi, w["wTr"])
                w["wT"] = o

            def factors(b, j):
                w = blocks[b]
                br, m = divmod(j, KT)
                bank, bi, free = trio.take()
                c.pe.need(*free)
                ms = slice(m * P, (m + 1) * P)
                split3(c, bank[:, 0, :], lambda h, k: left[br][:, h, k, ms], lambda h, k: w["zT"][:, h, k, :], range(KT))
                c.pe.need(w["czs"])
                mm = split3(c, bank[:, 1, :], lambda h, k: right[br][:, h, k, ms], lambda h, k: czs[:, h, k, :],
                            range(KT))
                tok = c.pe.mark(mm)
                if j == NJ - 1:
                    nrm.zT.give(w["zi"], tok)
                    held["czs"] = (tok,)
                c_, ci, free = c32.take()
                c.act.need(*free)
                c.act.need(tok)
                cp = c.act.mark(nc.scalar.copy(c_[:, :], bank[:, 1, :]))
                t_, ti, free = t32.take()
                c.vec.need(*free)
                c.vec.need(tok, cp)
                pr = c.vec.mark(nc.vector.tensor_tensor(t_[:, :], bank[:, 0, :], c_[:, :], ALU.mult))
                c32.give(ci, pr)
                w[j] = (bank, bi, t_, ti, pr)

            def weigh(b, j):
                w = blocks[b]
                bank, bi, t_, ti, pr = w.pop(j)
                c.pe.need(w["wTr"])
                for h in range(2):
                    mm = nc.tensor.matmul(bank[:, 2, :], sel[:, j, :], w["wT"][:, h, :], start=(h == 0), stop=(h == 1))
                tok = c.pe.mark(mm)
                p_, pi, free = p32.take()
                c.vec.need(*free)
                c.vec.need(tok, pr)
                a = c.vec.mark(nc.vector.scalar_tensor_tensor(p_[:, :], t_[:, :], PS / WS / WS, bank[:, 2, :],
                                                              ALU.mult, ALU.mult))
                trio.give(bi, a)
                t32.give(ti, a)
                c.act.need(a, *held["prod"])
                hi = c.act.mark(nc.scalar.copy(prodT[:, 0, j, :], p_[:, :]))
                c.pool.need(hi)
                lo = c.pool.mark(nc.gpsimd.tensor_tensor(prodT[:, 1, j, :], p_[:, :], prodT[:, 0, j, :], ALU.subtract))
                p32.give(pi, lo)
                w["lo"] = lo

            def finish(b):
                w = blocks[b]
                x = w["x"]
                c.pe.need(w["lo"])
                for t in range(TPB):
                    ts_ = slice(t * P, (t + 1) * P)
                    bank, bi, free = gen.take()
                    c.pe.need(*free)
                    split3(c, bank[:, :], lambda h, j: prodT[:, h, j, ts_], lambda h, j: up[:, h, j, :], range(NJ),
                           stop=False)
                    mm = split3(c, bank[:, :], lambda h, k: w["wT"][:, h, ts_], lambda h, k: bo[:, h, :], [0],
                                start=False)
                    tok = c.pe.mark(mm)
                    c.vec.need(tok)
                    n_ = b * TPB + t
                    out = c.vec.mark(nc.vector.scalar_tensor_tensor(x[:, t, :], bank[:, :], nf[:, n_:n_ + 1],
                                                                    x[:, t, :], ALU.mult, ALU.add))
                    gen.give(bi, out)
                held["prod"] = (tok,)
                wT.give(w["wi"], tok)
                c.sp.need(out)
                st = pst[w["xi"]].mark(nc.sync.dma_start(
                    dst[bass.ds(w["row"], BLK), :].rearrange("(t p) d -> p t d", p=P), x[:, :, :]))
                nrm.x.give(w["xi"], st)

            load(0)
            statistics(c, K, nrm, blocks[0])
            for t in range(TPB):
                halves(c, nrm, blocks[0], t, c.vec)
                turn_tile(c, K, nrm, blocks[0], t)
            running(0)
            halve(0)
            route(0)
            for b in range(NBB):
                nxt = b + 1 < NBB
                if nxt:
                    load(b + 1)
                factors(b, 0)
                turn_weights(b)
                weigh(b, 0)
                for j in range(1, NJ):
                    factors(b, j)
                    if nxt and j == 2:
                        statistics(c, K, nrm, blocks[b + 1])
                    if nxt and 3 <= j < 3 + TPB:
                        halves(c, nrm, blocks[b + 1], j - 3, c.vec)
                    weigh(b, j)
                    if nxt and j >= 4:
                        turn_tile(c, K, nrm, blocks[b + 1], j - 4)
                if nxt:
                    running(b + 1)
                    halve(b + 1)
                    route(b + 1)
                finish(b)
            c.meet()


def program(nc, I, out):
    scratch = lambda n, s, d: nc.dram_tensor(n, s, d, kind="Internal").ap()
    x1, xp, x3 = (scratch(n, (T, D), F32) for n in ("x1", "xp", "x3"))
    zrows, ids = scratch("zrows", (T, 2 * D), F16), scratch("ids", (SLOTS, 1), F32)
    oute = scratch("oute", (SLOTS, D), F32)
    with ExitStack() as ctx:
        c = Core(nc, ctx)
        K = constants(c, ctx, I)
        R = Routing(nc, ctx)
        attention(c, K, I, 0, I["x"], x1)
        shared_and_route(c, K, I, R, x1, xp, zrows, ids)
        experts(c, K, I, zrows, ids, oute)
        attention(c, K, I, 1, xp, x3, R=R, oute=oute)
        fused_experts(c, K, I, x3, out)


def layout(inputs):
    import numpy as np

    a = {n: np.asarray(v) for n, v in inputs.items()}
    out = {"x": a["x"].reshape(T, D), "mask": a["mask_Bx1xSxS2_ik1"].reshape(T, CTX)}
    ctxT = a["ctx_1024"].transpose(0, 2, 1)
    out["ctxT"] = ctxT
    rem = np.zeros((BATCH, D, HG, HD), ctxT.dtype)
    rem[:, :, :, 0:REM] = ctxT[:, :, None, P:CTX]
    out["ctxR"] = rem.reshape(BATCH, D, P)
    for n in ("g_xattn", "g_ffn", "L0_xattn_bq", "L0_xattn_bk", "L0_xattn_bv", "L0_xattn_bo"):
        out[n] = a[n]
    for n in ("L0_xattn_wq", "L0_xattn_wk", "L0_xattn_wv", "L0_xattn_wo",
              "L1_xattn_wq", "L1_xattn_wk", "L1_xattn_wv", "L1_ffn_W_O", "L1_ffn_router_w1", "L1_ffn_router_w2"):
        out[n + "T"] = a[n].T
    out["gates65"] = np.concatenate([a["L0_ffn_gate_w"], a["L0_ffn_shared_gate_w"]], axis=1)
    for n in ("L0_ffn_shared_gate_up_w", "L0_ffn_shared_down_w", "L0_ffn_expert_gate_up_w", "L0_ffn_expert_down_w",
              "L1_ffn_W_Q", "L1_ffn_W_K", "L1_ffn_W_inv", "L1_ffn_router_b1", "L1_ffn_router_b2",
              "L1_ffn_expert_bias"):
        out[n] = a[n]
    out["L1_ffn_alpha_bi"] = a["L1_ffn_alpha_bi"].reshape(1)
    for n in ("V_fwd", "W_fwd", "U_fwd", "V_inv", "W_inv_exp", "U_inv"):
        out["L1_ffn_" + n] = a["L1_ffn_" + n].transpose(1, 0, 2).reshape(D, KR)
    bT = np.zeros((D, P), a["L1_ffn_b_fwd"].dtype)
    bT[:, 0:KE], bT[:, KE:2 * KE] = a["L1_ffn_b_fwd"].T, a["L1_ffn_b_inv"].T
    out["L1_ffn_bT"] = bT
    return {n: np.ascontiguousarray(v) for n, v in out.items()}


def kernel(**inputs):
    import concourse.bacc as _bacc
    from concourse.bass_utils import run_bass_kernel_spmd as _run

    nc = _bacc.Bacc("TRN2", target_bir_lowering=False, num_devices=1)
    arrays = layout(inputs)
    I = {n: nc.dram_tensor(n, v.shape, mybir.dt.from_np(v.dtype), kind="ExternalInput").ap()
         for n, v in arrays.items()}
    out = nc.dram_tensor("out", (T, D), F32, kind="ExternalOutput").ap()
    program(nc, I, out)
    r = _run(nc, [arrays], core_ids=[0])
    return r.results[0]["out"].reshape(BATCH, SEQ, D)
```

```python
from contextlib import ExitStack

import concourse.bass as bass
from concourse import mybir

F32, F16, BF16 = mybir.dt.float32, mybir.dt.float16, mybir.dt.bfloat16
U32 = mybir.dt.uint32
ALU, ACT = mybir.AluOpType, mybir.ActivationFunctionType
AX = mybir.AxisListType

P = 128
D = 512
KT = D // P
BATCH, SEQ, CTX = 2, 2048, 154
T = BATCH * SEQ
BLK = 512
TPB = BLK // P
NBB = SEQ // BLK
HEADS, HD = 16, 32
HH = HEADS // 2
REM = CTX - P
HG = P // HD
E, TOPK, CAP = 64, 8, 256
SLOTS = E * CAP
EI = 256
IS = 1024
FB = IS // P
RH, KE, RR = 512, 8, 64
KR = KE * RR
WS = 256.0
EPS = 1e-5
BIG = 65536.0
EPL = 16


class Engine:

    def __init__(self, eng, sem):
        self.eng, self.sem, self.n = eng, sem, 0

    def mark(self, ins):
        ins.then_inc(self.sem, 1)
        self.n += 1
        return (self.sem, self.n)

    def need(self, *tokens):
        for sem, value in tokens:
            self.eng.wait_ge(sem, value)


class Port:

    def __init__(self, sem):
        self.sem, self.n = sem, 0

    def mark(self, ins):
        ins.then_inc(self.sem, 16)
        self.n += 16
        return (self.sem, self.n)


class SoftPort:

    def __init__(self, sem, per_turn):
        self.sem, self.per_turn, self.n, self.base = sem, per_turn, 0, 0

    def turn(self, g):
        self.base = g * self.per_turn

    def mark(self, ins):
        ins.then_inc(self.sem, 16)
        self.n += 16
        return (self.sem, self.base + self.n)


class Ring:

    def __init__(self, bufs):
        self.bufs = bufs
        self.reset()

    def reset(self):
        self.free, self.was, self.at = [()] * len(self.bufs), [()] * len(self.bufs), 0

    def take(self):
        i = self.at % len(self.bufs)
        self.at += 1
        free = self.free[i]
        assert free is not None, "taken before its last user gave it back"
        self.was[i], self.free[i] = free, None
        return self.bufs[i], i, free

    def give(self, i, *tokens):
        self.free[i] = tokens


class Core:
    def __init__(self, nc, ctx):
        self.nc, self.ctx = nc, ctx
        self.sems, self.ports, self.soft = [], [], []
        self.engines = []
        for name, engine in (("tensor", nc.tensor), ("scalar", nc.scalar), ("vector", nc.vector),
                             ("gpsimd", nc.gpsimd), ("sync", nc.sync)):
            sem = ctx.enter_context(nc.semaphore(f"s_{name}"))
            self.engines.append(Engine(engine, sem))
            self.sems.append(sem)
        self.pe, self.act, self.vec, self.pool, self.sp = self.engines
        self.idle = ctx.enter_context(nc.sbuf_tensor("idle", [P, 2], F32))
        nc.gpsimd.memset(self.idle[:, :], 0.0)

    def port(self, name):
        sem = self.ctx.enter_context(self.nc.semaphore(name))
        self.sems.append(sem)
        self.ports.append(Port(sem))
        return self.ports[-1]

    def soft_port(self, name, per_turn):
        self.soft.append(SoftPort(self.ctx.enter_context(self.nc.semaphore(name)), per_turn))
        return self.soft[-1]

    def meet(self):
        for p in self.ports:
            if p.n:
                self.sp.need((p.sem, p.n))
        for p in self.soft:
            if p.n:
                assert p.n == p.per_turn
                self.pool.need((p.sem, p.base + p.n))
        if any(p.n for p in self.soft):
            self.nc.gpsimd.tensor_tensor(self.idle[:, 0:1], self.idle[:, 1:2], self.idle[:, 1:2], ALU.add)
        self.nc.all_engine_barrier()
        for sem in self.sems:
            self.nc.sync.sem_clear(sem)
        self.nc.all_engine_barrier()
        for e in self.engines:
            e.n = 0
        for p in self.ports + self.soft:
            p.n = 0


def split3(c, out, lhs, rhs, ks, start=True, stop=True):
    n = len(ks)
    for i, k in enumerate(ks):
        for j, (a, b) in enumerate(((0, 0), (0, 1), (1, 0))):
            mm = c.nc.tensor.matmul(out, lhs(a, k), rhs(b, k), start=start and i == 0 and j == 0,
                                    stop=stop and i == n - 1 and j == 2)
    return mm


def load_split(c, stage, port, dst, src, after=(), dst_free=()):
    c.sp.need(*after)
    got = port.mark(c.nc.sync.dma_start(stage, src))
    c.act.need(got, *dst_free)
    hi = c.act.mark(c.nc.scalar.activation(dst(0), stage, ACT.Copy, scale=WS))
    c.vec.need(hi, got)
    return (c.vec.mark(c.nc.vector.scalar_tensor_tensor(dst(1), stage, WS, dst(0), ALU.mult, ALU.subtract)),)


class NormBuffers:

    def __init__(self, c, ctx, tag, banks, turned=2, nx=3):
        nc = c.nc
        sb = lambda n, s, d: ctx.enter_context(nc.sbuf_tensor(f"{tag}_{n}", s, d))
        self.x = Ring([sb(f"x{i}", [P, TPB, D], F32) for i in range(nx)])
        self.z = Ring([sb(f"z{i}", [P, D], F32) for i in range(2)])
        self.zs = Ring([sb(f"zs{i}", [P, 2, D], F16) for i in range(2)])
        self.zT = Ring([sb(f"zT{i}", [P, 2, KT, BLK], F16) for i in range(turned)])
        self.stats = sb("stats", [P, TPB, 6], F32)
        self.mv = sb("mv", [P, TPB, 2], F32)
        self.sd = sb("sd", [P, TPB], F32)
        self.rstd = sb("rstd", [P, TPB], F32)
        self.px = [c.port(f"{tag}_x{i}") for i in range(nx)]
        self.banks = banks

    def reset(self):
        for r in (self.x, self.z, self.zs, self.zT):
            r.reset()


def load_tokens(c, nb, src, row):
    x, i, free = nb.x.take()
    c.sp.need(*free)
    got = nb.px[i].mark(c.nc.sync.dma_start(
        x[:, :, :], src[bass.ds(row, BLK), :].rearrange("(t p) d -> p t d", p=P)))
    return x, i, got


def statistics(c, K, nb, w):
    nc, x = c.nc, w["x"]
    c.vec.need(w["got"])
    for t in range(TPB):
        tok = c.vec.mark(nc.vector.bn_stats(nb.stats[:, t, :], x[:, t, :]))
    c.vec.need(tok)
    for t in range(TPB):
        tok = c.vec.mark(nc.vector.bn_aggr(nb.mv[:, t, :], nb.stats[:, t, :]))
    c.act.need(tok)
    sd = c.act.mark(nc.scalar.activation(nb.sd[:, :], nb.mv[:, :, 1], ACT.Sqrt, bias=K.eps[:, 0:1]))
    c.vec.need(sd)
    w["rstd"] = c.vec.mark(nc.vector.reciprocal(nb.rstd[:, :], nb.sd[:, :]))


def high_half(c, nb, w, t):
    nc = c.nc
    z, i, free = nb.z.take()
    c.vec.need(w["rstd"], *free)
    w["x_done"] = c.vec.mark(nc.vector.tensor_scalar(z[:, :], w["x"][:, t, :], nb.mv[:, t, 0:1],
                                                     nb.rstd[:, t:t + 1], ALU.subtract, ALU.mult))
    zs, j, free = nb.zs.take()
    c.act.need(w["x_done"], *free)
    w["high", t] = (z, i, zs, j, c.act.mark(nc.scalar.copy(zs[:, 0, :], z[:, :])))


def low_half(c, nb, w, t, low):
    z, i, zs, j, hi = w["high", t]
    low.need(hi)
    lo = low.mark(low.eng.tensor_tensor(zs[:, 1, :], z[:, :], zs[:, 0, :], ALU.subtract))
    nb.z.give(i, lo)
    w["zs", t] = (zs, j, lo)


def halves(c, nb, w, t, low):
    high_half(c, nb, w, t)
    low_half(c, nb, w, t, low)


def turn_tile(c, K, nb, w, t, stored=()):
    nc = c.nc
    if t == 0:
        w["zT"], w["zi"], w["zT_free"] = nb.zT.take()
        w["turned"] = []
    zs, j, lo = w["zs", t]
    bank, bi, free = nb.banks.take()
    c.pe.need(lo, *free)
    turned = bank[:, :].bitcast(F16).rearrange("p (h k n) -> p h k n", h=2, k=KT)
    for h in range(2):
        for k in range(KT):
            mm = nc.tensor.transpose(turned[:, h, k, :], zs[:, h, k * P:(k + 1) * P], K.id16[:, :])
    tp = c.pe.mark(mm)
    nb.zs.give(j, tp, *stored)
    dst = w["zT"][:, :, :, t * P:(t + 1) * P]
    e = c.act if t % 2 == 0 else c.vec
    e.need(tp, *w["zT_free"])
    out = e.mark(nc.scalar.copy(dst, turned) if t % 2 == 0 else nc.vector.tensor_copy(dst, turned))
    nb.banks.give(bi, out)
    w["turned"].append(out)


def place(h):
    return (h % HG) * (HH // HG) + h // HG


class Consts:
    pass


def constants(c, ctx, I):
    nc, K = c.nc, Consts()
    sb = lambda n, s, d: ctx.enter_context(nc.sbuf_tensor(n, s, d))
    K.id32, K.id16, K.eps = sb("id32", [P, P], F32), sb("id16", [P, P], F16), sb("eps", [P, 1], F32)
    K.gates, K.tg, K.tgw = sb("gates", [P, 4], F32), sb("tg", [P, 4], F32), sb("tgw", [P, 4], F32)
    pg = c.port("gates_in")
    tok = c.pool.mark(nc.gpsimd.memset(K.id32[:, :], 0.0))
    c.pool.need(tok)
    tok = c.pool.mark(nc.gpsimd.affine_select(out=K.id32[:, :], in_=K.id32[:, :], compare_op=ALU.not_equal,
                                              fill=1.0, base=0, pattern=[[-1, P]], channel_multiplier=1))
    c.vec.need(tok)
    c.vec.mark(nc.vector.tensor_copy(K.id16[:, :], K.id32[:, :]))
    c.vec.mark(nc.vector.memset(K.eps[:, :], EPS))
    for i, g in enumerate((I["g_xattn"], I["g_ffn"])):
        got = pg.mark(nc.sync.dma_start(K.gates[:, 2 * i:2 * i + 2],
                                        g.rearrange("(a n) -> a n", a=1).broadcast_to([P, 2])))
        c.sp.need(got)
    c.act.need(got)
    tok = c.act.mark(nc.scalar.activation(K.tg[:, :], K.gates[:, :], ACT.Tanh))
    c.vec.need(tok)
    c.vec.mark(nc.vector.tensor_scalar(K.tgw[:, :], K.tg[:, :], 1.0 / WS, None, ALU.mult))
    c.meet()
    return K


def attention(c, K, I, layer, src, dst, R=None, oute=None):
    nc = c.nc
    L0 = layer == 0
    with ExitStack() as ctx:
        sb = lambda n, s, d: ctx.enter_context(nc.sbuf_tensor(f"at{layer}_{n}", s, d))
        port = lambda n: c.port(f"at{layer}_{n}")
        gen = Ring([ctx.enter_context(nc.psum_tensor(f"at{layer}_g{i}", [P, 512], F32)) for i in range(2)])
        trp = Ring([ctx.enter_context(nc.psum_tensor(f"at{layer}_t{i}", [P, 512], F32)) for i in range(2)])
        S = ctx.enter_context(nc.psum_tensor(f"at{layer}_S", [P, HH, 256], F32))
        nrm = NormBuffers(c, ctx, f"at{layer}", gen, turned=1, nx=4)
        wq = sb("wq", [P, 2, KT, D], F16)
        wk, wv = sb("wk", [P, KT, D], F32), sb("wv", [P, KT, D], F32)
        KTn = sb("KT", [P, KT, CTX], F32)
        V = sb("V", [P, HEADS, P], F32)
        VR = sb("VR", [P, KT, P], F32)
        qT = Ring([sb(f"qT{i}", [P, KT, BLK], F32) for i in range(2)])
        s = Ring([sb(f"s{i}", [P, HH, CTX], F32) for i in range(3 if L0 else 2)])
        prob = Ring([sb(f"p{i}", [P, HH * (P + HD)], F32) for i in range(2)])
        pT = Ring([sb(f"pT{i}", [P, HH + 2, BLK], F32) for i in range(2)])
        mx, sm, rs = (Ring([sb(f"{n}{i}", [P, HH], F32) for i in range(3)]) for n in ("mx", "sm", "rs"))
        pw, pk, pv, pc, pr = (port(n) for n in ("wq", "wk", "wv", "kctx", "rctx"))
        pst = [port(f"st{i}") for i in range(len(nrm.x.bufs))]
        wk_d, wv_d, wq_d = (I[f"L{layer}_xattn_{n}"].rearrange("(k p) m -> p k m", p=P) for n in ("wkT", "wvT", "wqT"))
        stage = qT.bufs[0]
        load_split(c, stage[:, :, :], pw, lambda h: wq[:, h, :, :], wq_d)
        pk.mark(nc.sync.dma_start(wk[:, :, :], wk_d))
        pv.mark(nc.sync.dma_start(wv[:, :, :], wv_d))
        if L0:
            wo = sb("wo", [P, 2, KT, D], F16)
            oT = Ring([sb(f"oT{i}", [P, 2, KT, BLK], F16) for i in range(1)])
            bq, bqs, bk = sb("bq", [P, KT], F32), sb("bqs", [P, KT], F32), sb("bk", [P, KT], F32)
            bv, bo, tbo = sb("bv", [P, D], F32), sb("bo", [P, D], F32), sb("tbo", [P, D], F32)
            limi = [sb(f"mi{i}", [P, TPB, CTX], mybir.dt.int32) for i in range(1)]
            lim = Ring([sb(f"lim{i}", [P, TPB, CTX], F32) for i in range(2)])
            pb, pm = port("bias"), port("mask")
            stage1 = qT.bufs[1]
            load_split(c, stage1[:, :, :], port("wo"), lambda h: wo[:, h, :, :],
                       I["L0_xattn_woT"].rearrange("(k p) m -> p k m", p=P))
            with nc.allow_non_contiguous_dma(reason="biases by head dim, once"):
                for dstb, n in ((bq, "bq"), (bk, "bk")):
                    got = pb.mark(nc.sync.dma_start(dstb[:, :], I[f"L0_xattn_{n}"].rearrange("(k p) -> p k", p=P)))
            for dstb, n in ((bv, "bv"), (bo, "bo")):
                got = pb.mark(nc.sync.dma_start(dstb[:, :], I[f"L0_xattn_{n}"].rearrange("(a n) -> a n", a=1)
                                                .broadcast_to([P, D])))
            c.vec.need(got)
            c.vec.mark(nc.vector.tensor_scalar(bqs[:, :], bq[:, :], HD ** -0.5, None, ALU.mult))
            c.vec.mark(nc.vector.tensor_scalar(tbo[:, :], bo[:, :], K.tg[:, 0:1], None, ALU.mult))
        else:
            oF = Ring([sb(f"oF{i}", [P, KT, BLK], F32) for i in range(1)])
        turned_ctx = sb("ctx", [P, KT, CTX + P], F32) if L0 else oF.bufs[0]
        kctx, rctx = turned_ctx[:, :, 0:CTX], turned_ctx[:, :, CTX:CTX + P]
        c.vec.mark(nc.vector.memset(V[:, :, :], 0.0))
        c.vec.mark(nc.vector.memset(VR[:, :, :], 0.0))
        for b in prob.bufs:
            c.pool.mark(nc.gpsimd.memset(b[:, :], 0.0))
        if not L0:
            rb = ReturnBuffers(c, ctx)
        c.meet()

        with nc.Fori(0, BATCH) as g:
            for r in (gen, trp, qT, s, prob, pT, mx, sm, rs, *((oT, lim) if L0 else (oF,))):
                r.reset()
            nrm.reset()
            if not L0:
                rb.turn(g)
            gotc = pc.mark(nc.sync.dma_start(kctx[:, :, :], I["ctxT"][bass.ds(g, 1), :, :]
                                             .rearrange("a (k p) n -> p (a k) n", p=P)))
            gotr = pr.mark(nc.sync.dma_start(rctx[:, :, :], I["ctxR"][bass.ds(g, 1), :, :]
                                             .rearrange("a (k p) n -> p (a k) n", p=P)))
            blocks = {}

            def load(b):
                row = g * SEQ + b * BLK
                x, xi, got = load_tokens(c, nrm, src, row)
                w = blocks[b] = dict(x=x, xi=xi, got=got, row=row, tile=g * (SEQ // P) + b * TPB)
                if L0:
                    c.sp.need(*mask_free[0])
                    w["mask"] = pm.mark(nc.sync.dma_start(limi[0][:, :, :], I["mask"][bass.ds(row, BLK), :]
                                                          .rearrange("(t p) n -> p t n", p=P)))

            mask_free = [()]

            def limits(b):
                l, li, free = lim.take()
                c.vec.need(blocks[b]["mask"], *free)
                a = c.vec.mark(nc.vector.tensor_scalar(l[:, :, :], limi[0][:, :, :], 0.0, None, ALU.not_equal))
                mask_free[0] = (a,)
                c.vec.need(a)
                a = c.vec.mark(nc.vector.tensor_scalar(l[:, :, :], l[:, :, :], 1e30, -1e30, ALU.mult, ALU.add))
                c.vec.need(a)
                a = c.vec.mark(nc.vector.tensor_scalar(l[:, :, :], l[:, :, :], 100.0, None, ALU.add))
                blocks[b]["m"] = (l, li, a)

            def gather_returns_begin(b):
                begin_returns(c, R, rb, blocks[b])

            def gather_returns(b, t, ks):
                gather_tile(c, rb, oute, blocks[b], t, ks)

            def add_returns(b, t, ks):
                add_tile(c, rb, blocks[b], t, ks)

            def stats(b):
                statistics(c, K, nrm, blocks[b])

            def prepare_low(b, t):
                low_half(c, nrm, blocks[b], t, c.vec)

            def turn_z(b, t):
                turn_tile(c, K, nrm, blocks[b], t)

            def prepare(b, t):
                w = blocks[b]
                high_half(c, nrm, w, t)
                w["x_ready"] = w["x_done"]
                if L0:
                    c.pool.need(w["x_done"])
                    w["x_ready"] = c.pool.mark(nc.gpsimd.tensor_tensor(w["x"][:, t, :], w["x"][:, t, :],
                                                                       tbo[:, :], ALU.add))

            def project(b, m):
                w = blocks[b]
                if m == 0:
                    w["q"], w["qi"], free = qT.take()
                    c.act.need(*free)
                    c.pe.need(*w["turned"])
                bank, bi, free = gen.take()
                c.pe.need(*free)
                mm = split3(c, bank[:, :], lambda h, k: wq[:, h, k, m * P:(m + 1) * P],
                            lambda h, k: w["zT"][:, h, k, :], range(KT))
                tok = c.pe.mark(mm)
                c.act.need(tok)
                sc = HD ** -0.5 / WS
                if L0:
                    out = c.act.mark(nc.scalar.activation(w["q"][:, m, :], bank[:, :], ACT.Identity,
                                                          bias=bqs[:, m:m + 1], scale=sc))
                else:
                    out = c.act.mark(nc.scalar.activation(w["q"][:, m, :], bank[:, :], ACT.Copy, scale=sc))
                gen.give(bi, out)
                w["q_ready", m] = out
                if m == KT - 1:
                    nrm.zT.give(w["zi"], tok)

            score_free = [()]

            def scores(b, u, t):
                w = blocks[b]
                c.pe.need(w["q_ready", 2 * u + 1], *score_free[0])
                for h in range(HH):
                    o, m = HD * (h % HG), 2 * u + h // HG
                    mm = nc.tensor.matmul(S[:, place(h), 0:CTX], w["q"][o:o + HD, m, t * P:(t + 1) * P],
                                          KTn[o:o + HD, m, :], start=True, stop=True)
                tok = c.pe.mark(mm)
                if (u, t) == (1, TPB - 1):
                    qT.give(w["qi"], tok)
                sb_, si, free = s.take()
                (c.vec if L0 else c.act).need(*free)
                mxb, mi, free = mx.take()
                c.vec.need(*free)
                smb, smi, free = sm.take()
                c.act.need(*free)
                rsb, ri, free = rs.take()
                c.vec.need(*free)
                c.vec.need(tok)
                if L0:
                    l, li, lt = w["m"]
                    c.vec.need(lt)
                    a = c.vec.mark(nc.vector.scalar_tensor_tensor(
                        sb_[:, :, :], S[:, :, 0:CTX], -100.0,
                        l[:, t:t + 1, :].broadcast_to([P, HH, CTX]), ALU.max, ALU.min))
                    score_free[0] = (a,)
                    if (u, t) == (1, TPB - 1):
                        lim.give(li, a)
                    c.vec.need(a)
                    top = c.vec.mark(nc.vector.tensor_reduce(mxb[:, :], sb_[:, :, :], AX.X, ALU.max))
                else:
                    top = c.vec.mark(nc.vector.tensor_reduce(mxb[:, :], S[:, :, 0:CTX], AX.X, ALU.max))
                c.vec.need(top)
                neg = c.vec.mark(nc.vector.tensor_scalar(mxb[:, :], mxb[:, :], -1.0, None, ALU.mult))
                return dict(b=b, u=u, t=t, s=sb_, si=si, mx=mxb, mi=mi, sm=smb, smi=smi, rs=rsb, ri=ri, neg=neg)

            def exponentials(v):
                c.act.need(v["neg"])
                for h in range(HH):
                    v["ex"] = c.act.mark(nc.scalar.activation(
                        v["s"][:, h, :], v["s"][:, h, :] if L0 else S[:, h, 0:CTX], ACT.Exp,
                        bias=v["mx"][:, h:h + 1], accum_out=v["sm"][:, h:h + 1]))
                mx.give(v["mi"], v["ex"])
                if not L0:
                    score_free[0] = (v["ex"],)

            def probabilities(v):
                sb_, smb, rsb = v["s"], v["sm"], v["rs"]
                pb_, v["pi"], free = prob.take()
                c.pool.need(*free)
                v["p"] = pb_
                c.vec.need(v["ex"])
                r = c.vec.mark(nc.vector.reciprocal(rsb[:, :], smb[:, :]))
                sm.give(v["smi"], r)
                c.pool.need(r, v["ex"])
                main = pb_[:, 0:HH * P].rearrange("p (h n) -> p h n", h=HH)
                rem = pb_[:, HH * P:].rearrange("p (j r n) -> p r j n", r=HG, n=HD)
                srem = sb_[:, :, P:CTX].rearrange("p (r j) n -> p r j n", r=HG)
                rrem = rsb[:, :].rearrange("p (r j) -> p r j", r=HG)[:, :, :, None]
                nc.gpsimd.tensor_tensor(main, sb_[:, :, 0:P], rsb[:, :, None].broadcast_to([P, HH, P]), ALU.mult)
                tok = c.pool.mark(nc.gpsimd.tensor_tensor(rem[:, :, :, 0:REM], srem,
                                                          rrem.broadcast_to([P, HG, HH // HG, REM]), ALU.mult))
                s.give(v["si"], tok)
                rs.give(v["ri"], tok)
                v["p_ready"] = tok

            def turn(v):
                if v["t"] == 0:
                    blocks[v["b"]]["pT", v["u"]] = (*pT.take(), [])
                c.pe.need(v["p_ready"])
                turn_keys(v, 0, c.act)
                turn_keys(v, 4, c.act)

            def turn_rest(v):
                tok = turn_keys(v, HH, c.vec)
                prob.give(v["pi"], tok)

            def turn_keys(v, j0, e):
                ptb, _, pT_free, outs = blocks[v["b"]]["pT", v["u"]]
                n, t = min(4, HH + 2 - j0), v["t"]
                bank, bi, free = trp.take()
                c.pe.need(*free)
                for j in range(n):
                    mm = nc.tensor.transpose(bank[:, j * P:(j + 1) * P],
                                             v["p"][:, (j0 + j) * P:(j0 + j + 1) * P], K.id32[:, :])
                tok = c.pe.mark(mm)
                e.need(tok, *pT_free)
                dst_ = ptb[:, j0:j0 + n, t * P:(t + 1) * P]
                srcb = bank[:, 0:n * P].rearrange("p (j n) -> p j n", j=n)
                out = e.mark(nc.vector.tensor_copy(dst_, srcb) if e is c.vec else nc.scalar.copy(dst_, srcb))
                trp.give(bi, out)
                outs.append(out)
                return tok

            def values(b, u, gi):
                w = blocks[b]
                ptb, pti, _, ready = w["pT", u]
                c.pe.need(v_ready[0], *ready)
                if (u, gi) == (0, 0):
                    w["o"], w["oi"], free = (oT if L0 else oF).take()
                    c.act.need(*free)
                    c.vec.need(*(oT if L0 else oF).was[w["oi"]])
                    w["o_ready"] = []
                grp = 2 * u + gi
                bank, bi, free = gen.take()
                c.pe.need(*free)
                for j in range(HG):
                    nc.tensor.matmul(bank[:, :], V[:, grp * HG + j, :],
                                     ptb[:, place(gi * HG + j), :],
                                     start=(j == 0), stop=False)
                tok = c.pe.mark(nc.tensor.matmul(bank[:, :], VR[:, grp, :], ptb[:, HH + gi, :],
                                                 start=False, stop=True))
                c.act.need(tok)
                if L0:
                    hi = c.act.mark(nc.scalar.copy(w["o"][:, 0, grp, :], bank[:, :]))
                    c.vec.need(hi)
                    out = c.vec.mark(nc.vector.tensor_tensor(w["o"][:, 1, grp, :], bank[:, :],
                                                             w["o"][:, 0, grp, :], ALU.subtract))
                else:
                    out = c.act.mark(nc.scalar.copy(w["o"][:, grp, :], bank[:, :]))
                gen.give(bi, out)
                w["o_ready"].append(out)
                if gi == 1:
                    pT.give(pti, tok)

            def finish(b, tiles):
                w = blocks[b]
                x, xi = w["x"], w["xi"]
                c.pe.need(*w["o_ready"])
                for t in tiles:
                    bank, bi, free = gen.take()
                    c.pe.need(*free)
                    if L0:
                        mm = split3(c, bank[:, :], lambda h, k: w["o"][:, h, k, t * P:(t + 1) * P],
                                    lambda h, k: wo[:, h, k, :], range(KT))
                    else:
                        for k in range(KT):
                            mm = nc.tensor.transpose(bank[:, k * P:(k + 1) * P],
                                                     w["o"][:, k, t * P:(t + 1) * P], K.id32[:, :])
                    tok = c.pe.mark(mm)
                    c.vec.need(tok, w["x_ready"])
                    out = c.vec.mark(nc.vector.scalar_tensor_tensor(
                        x[:, t, :], bank[:, :], K.tgw[:, 0:1] if L0 else K.tg[:, 1:2], x[:, t, :],
                        ALU.mult, ALU.add))
                    gen.give(bi, out)
                if TPB - 1 not in tiles:
                    return
                (oT if L0 else oF).give(w["oi"], tok)
                c.sp.need(out)
                st = pst[xi].mark(nc.sync.dma_start(
                    dst[bass.ds(w["row"], BLK), :].rearrange("(t p) d -> p t d", p=P), x[:, :, :]))
                nrm.x.give(xi, st)

            load(0)
            c.pe.need(gotc, gotr)
            kv = []
            for m in range(KT):
                bank, bi, free = gen.take()
                c.pe.need(*free)
                for k in range(KT):
                    mm = nc.tensor.matmul(bank[:, 0:CTX], wk[:, k, m * P:(m + 1) * P], kctx[:, k, :],
                                          start=(k == 0), stop=(k == KT - 1))
                tok = c.pe.mark(mm)
                c.vec.need(tok)
                if L0:
                    out = c.vec.mark(nc.vector.tensor_scalar(KTn[:, m, :], bank[:, 0:CTX], bk[:, m:m + 1],
                                                             None, ALU.add))
                else:
                    out = c.vec.mark(nc.vector.tensor_copy(KTn[:, m, :], bank[:, 0:CTX]))
                gen.give(bi, out)
            c.pe.need(out)

            def value_rows(rem):
                bank, bi, free = gen.take()
                c.pe.need(*free)
                for k in range(KT):
                    mm = nc.tensor.matmul(bank[:, :], rctx[:, k, :] if rem else kctx[:, k, 0:P], wv[:, k, :],
                                          start=(k == 0), stop=(k == KT - 1))
                tok = c.pe.mark(mm)
                c.vec.need(tok)
                for h in range(HG):
                    rows = slice(HD * h, HD * h + HD) if rem else slice(0, P)
                    o = (VR[rows, :, HD * h:HD * h + HD] if rem else
                         V[:, :, :].rearrange("p (g h) n -> p g h n", h=HG)[:, :, h, HD * h:HD * h + HD])
                    i_ = bank[:, :].rearrange("p (g h n) -> p g h n", g=KT, h=HG)[rows, :, h, :]
                    if L0:
                        b_ = bv[:, :].rearrange("p (g h n) -> p g h n", g=KT, h=HG)[rows, :, h, :]
                        out = c.vec.mark(nc.vector.tensor_tensor(o, i_, b_, ALU.add))
                    else:
                        out = c.vec.mark(nc.vector.tensor_copy(o, i_))
                gen.give(bi, out)
                v_ready[0] = out

            v_ready = [()]
            UPB = 2 * TPB
            lag = 1 if L0 else 0
            order = {prepare_low: 0, turn_z: 2, prepare: 3}
            units = [(b, u, t) for b in range(NBB) for u in range(2) for t in range(TPB)]
            steps = len(units) + 9
            tasks = {n: [] for n in range(-1, steps)}

            def plan(n, f, *args):
                tasks[max(n, -1)].append((f, args))

            plan(1, value_rows, 0)
            plan(2, value_rows, 1)
            for b in range(NBB):
                n = b * UPB
                if b:
                    plan(n - 13, load, b)
                if L0:
                    plan(n - 7, limits, b)
                else:
                    plan(n - 13, gather_returns_begin, b)
                    for t in range(TPB):
                        if b < 2:
                            plan(n - 10 + max(t, 1), gather_returns, b, t, range(TOPK))
                            plan(n - 8 + t if b else -1, add_returns, b, t, range(TOPK))
                            continue
                        for half, ks in enumerate((range(TOPK // 2), range(TOPK // 2, TOPK))):
                            plan(n - 13 + 2 * t + half, gather_returns, b, t, ks)
                            plan(n - 12 + 2 * t + half, add_returns, b, t, ks)
                ready = n - (7 if L0 else 1)
                plan(ready - 4, stats, b)
                for t in range(0, TPB, 2):
                    for at, f in ((-3, prepare), (-2, prepare_low), (-2, turn_z)):
                        for t_ in (t, t + 1):
                            plan(ready + at + t // 2, f, b, t_)
                for m in range(KT):
                    plan(n + ((-7, -7, -6, -6) if L0 else (-1, -1, 1, 3))[m], project, b, m)
                for u in range(2):
                    for gi in range(2):
                        plan(n + TPB * (u + 1) + 2 + lag + gi * (1 if L0 else 2), values, b, u, gi)
                for t in range(TPB):
                    plan(n + UPB + (5 + t // 2 if L0 else 5), finish, b, [t])
            for f, args in tasks[-1]:
                f(*args)
            v = {}
            for n in range(steps):
                if n - lag - 1 in v:
                    probabilities(v[n - lag - 1])
                if n < len(units):
                    v[n] = scores(*units[n])
                if n - lag - 2 in v:
                    turn(v[n - lag - 2])
                if n - lag in v:
                    exponentials(v[n - lag])
                for f, args in sorted(tasks[n], key=lambda job: order.get(job[0], 1)):
                    f(*args)
                if n - lag - 2 in v:
                    turn_rest(v[n - lag - 2])
            c.meet()


class Routing:

    def __init__(self, nc, ctx):
        sb = lambda n, s, d: ctx.enter_context(nc.sbuf_tensor(n, s, d))
        self.slots = sb("slots", [P, T // P, TOPK], U32)
        self.weights = sb("weights", [P, T // P, TOPK], F32)


def shared_and_route(c, K, I, R, src, dst, zrows, ids):
    nc = c.nc
    with ExitStack() as ctx:
        sb = lambda n, s, d: ctx.enter_context(nc.sbuf_tensor(f"sh_{n}", s, d))
        port = lambda n: c.port(f"sh_{n}")
        ps = lambda n, s: ctx.enter_context(nc.psum_tensor(f"sh_{n}", s, F32))
        gen = Ring([ps(f"g{i}", [P, 512]) for i in range(3)])
        gu = Ring([ps(f"gu{i}", [P, 2, 512]) for i in range(2)])
        LG = ps("LG", [P, TPB, E + 1])
        nrm = NormBuffers(c, ctx, "sh", gen)
        wgu, wdn = sb("wgu", [P, 2, KT, 2 * IS], F16), sb("wdn", [P, 2, FB, D], F16)
        wgt = sb("wgt", [P, 2, KT, E + 1], F16)
        actT = sb("actT", [P, 2, FB, BLK], F16)
        act32 = Ring([sb(f"a{i}", [P, BLK], F32) for i in range(2)])
        silu = Ring([sb(f"si{i}", [P, BLK], F32) for i in range(2)])
        stage = nrm.x.bufs
        pst, pz, psc = [port(f"st{i}") for i in range(3)], port("z"), [c.soft_port(f"sh_sc{i}", 16 * TPB * TOPK * NBB // 2) for i in range(2)]
        pzs = [port(f"zs{i}") for i in range(2)]
        tri, ones = sb("tri", [P, P], BF16), sb("ones", [P, P], BF16)
        one32 = sb("one32", [P, P], F32)
        iexp, iexpi = sb("iexp", [P, E], F32), sb("iexpi", [P, E], mybir.dt.int32)
        tokf, toki = sb("tokf", [P, TPB], F32), sb("toki", [P, TPB], mybir.dt.int32)
        tokb = Ring([sb(f"tk{i}", [P, TPB], F32) for i in range(2)])
        count, countb, sum4 = sb("count", [P, E], F32), sb("countb", [P, E], BF16), sb("sum4", [P, E], F32)
        ex, rep = sb("ex", [P, TPB, E], F32), sb("rep", [P, TPB, E], F32)
        M = sb("M", [P, TPB, E], BF16)
        top, idx, idxf = sb("top", [P, TPB, TOPK], F32), sb("idx", [P, TPB, TOPK], U32), sb("idxf", [P, TPB, TOPK], F32)
        mx, sm, rs = sb("mx", [P, TPB], F32), sb("sm", [P, TPB], F32), sb("rs", [P, TPB], F32)
        w8, slot, far = sb("w8", [P, TPB, TOPK], F32), sb("slot", [P, TPB, E], F32), sb("far", [P, TPB, E], F32)
        eq, slotk = sb("eq", [P, TPB, TOPK, E], F32), sb("slotk", [P, TPB, TOPK], F32)
        kept = sb("kept", [P, TPB, TOPK], F32)
        slotu = Ring([sb(f"su{i}", [P, TPB, TOPK], U32) for i in range(2)])
        sg = sb("sg", [P, TPB], F32)

        wgu_d = I["L0_ffn_shared_gate_up_w"].rearrange("(k p) n -> p k n", p=P)
        wdn_d = I["L0_ffn_shared_down_w"].rearrange("(k p) n -> p k n", p=P)
        pieces = [(wgu_d[:, :, n * 512:(n + 1) * 512], lambda h, n=n: wgu[:, h, :, n * 512:(n + 1) * 512])
                  for n in range(4)]
        pieces += [(wdn_d[:, 4 * n:4 * n + 4, :], lambda h, n=n: wdn[:, h, 4 * n:4 * n + 4, :]) for n in range(2)]
        pieces += [(I["gates65"].rearrange("(k p) n -> p k n", p=P), lambda h: wgt[:, h, :, :])]
        used = [()] * len(stage)
        for n, (src_, piece) in enumerate(pieces):
            i = n % len(stage)
            used[i] = load_split(c, stage[i][:, :, 0:src_.shape[-1]], pst[i], piece, src_, after=used[i])
        a = c.pool.mark(nc.gpsimd.memset(one32[:, :], 1.0))
        c.pool.need(a)
        a = c.pool.mark(nc.gpsimd.affine_select(out=one32[:, :], in_=one32[:, :], compare_op=ALU.is_gt, fill=0.0,
                                                base=0, pattern=[[1, P]], channel_multiplier=-1))
        b = c.pool.mark(nc.gpsimd.iota(iexpi[:, :], pattern=[[CAP, E]], base=0, channel_multiplier=0))
        b = c.pool.mark(nc.gpsimd.iota(toki[:, :], pattern=[[P, TPB]], base=0, channel_multiplier=1))
        c.vec.need(a, b)
        c.vec.mark(nc.vector.tensor_copy(tri[:, :], one32[:, :]))
        c.vec.mark(nc.vector.memset(ones[:, :], 1.0))
        c.vec.mark(nc.vector.tensor_copy(iexp[:, :], iexpi[:, :]))
        c.vec.mark(nc.vector.tensor_copy(tokf[:, :], toki[:, :]))
        c.vec.mark(nc.vector.memset(count[:, :], 0.0))
        c.vec.mark(nc.vector.memset(countb[:, :], 0.0))
        z = c.vec.mark(nc.vector.memset(eq[:, :, :, :], 0.0))
        c.sp.need(z)
        pz.mark(nc.sync.dma_start(ids.rearrange("(p n) a -> p (n a)", p=P), eq[:, 0, 0:2, :].rearrange("p a b -> p (a b)")))
        c.meet()

        with nc.Fori(0, BATCH) as g:
            for r in (gen, gu, act32, silu, tokb, slotu):
                r.reset()
            nrm.reset()
            for q in psc:
                q.turn(g)
            blocks, held = {}, dict(route=(), scat=(), actT=(), LG=(), pos=())

            def load(b):
                row = g * SEQ + b * BLK
                x, xi, got = load_tokens(c, nrm, src, row)
                blocks[b] = dict(x=x, xi=xi, got=got, row=row)

            def keep_rows(b, t):
                w = blocks[b]
                halves(c, nrm, w, t, c.vec)
                zs, j, lo = w["zs", t]
                c.sp.need(lo)
                w["stored", t] = pzs[j].mark(nc.sync.dma_start(
                    zrows[bass.ds(w["row"] + t * P, P), :], zs[:, :, :].rearrange("p h d -> p (h d)")))

            def turn_rows(b, t):
                turn_tile(c, K, nrm, blocks[b], t, stored=(blocks[b]["stored", t],))

            def logits(b):
                w = blocks[b]
                c.pe.need(*w["turned"], *held["LG"])
                for t in range(TPB):
                    mm = split3(c, LG[:, t, :], lambda h, k: w["zT"][:, h, k, t * P:(t + 1) * P],
                                lambda h, k: wgt[:, h, k, :], range(KT))
                w["logits"] = c.pe.mark(mm)

            def choose(b):
                w = blocks[b]
                v = nc.vector
                c.vec.need(w["logits"], *held["route"])
                a = c.vec.mark(v.tensor_reduce(mx[:, :], LG[:, :, 0:E], AX.X, ALU.max))
                c.vec.need(a)
                a = c.vec.mark(v.tensor_tensor(ex[:, :, :], LG[:, :, 0:E], mx[:, :, None].broadcast_to([P, TPB, E]),
                                               ALU.subtract))
                c.act.need(a, w["logits"])
                e1 = c.act.mark(nc.scalar.activation(ex[:, :, :], ex[:, :, :], ACT.Exp, scale=1.0 / WS))
                e2 = c.act.mark(nc.scalar.activation(sg[:, :], LG[:, :, E], ACT.Exp, scale=-1.0 / WS))
                held["LG"] = (a, e2)
                c.vec.need(e1)
                for t in range(TPB):
                    a = c.vec.mark(v.max(top[:, t, :], ex[:, t, :]))
                c.vec.need(a)
                for t in range(TPB):
                    c.vec.mark(v.max_index(idx[:, t, :], top[:, t, :], ex[:, t, :]))
                    a = c.vec.mark(v.match_replace(rep[:, t, :], top[:, t, :], ex[:, t, :], -1.0))
                b_ = c.vec.mark(v.tensor_reduce(sm[:, :], top[:, :, :], AX.X, ALU.add))
                c.vec.need(a)
                w["chosen"] = c.vec.mark(v.tensor_scalar(M[:, :, :], rep[:, :, :], 0.0, None, ALU.is_lt))
                c.vec.mark(v.tensor_scalar(idxf[:, :, :], idx[:, :, :], float(CAP), None, ALU.mult))
                c.vec.need(b_)
                a = c.vec.mark(v.reciprocal(rs[:, :], sm[:, :]))
                c.vec.need(a, e2)
                c.vec.mark(v.tensor_tensor(w8[:, :, :], top[:, :, :], rs[:, :, None].broadcast_to([P, TPB, TOPK]),
                                           ALU.mult))
                a = c.vec.mark(v.tensor_scalar(sg[:, :], sg[:, :], 1.0, None, ALU.add))
                c.vec.need(a)
                a = c.vec.mark(v.reciprocal(sg[:, :], sg[:, :]))
                c.vec.need(a)
                w["sg"] = c.vec.mark(v.tensor_scalar(sg[:, :], sg[:, :], K.tgw[:, 2:3], None, ALU.mult))

            def positions(b):
                w = blocks[b]
                bank, bi, free = gen.take()
                c.pe.need(*free)
                c.pe.need(w["chosen"], *held["pos"])
                pos = bank[:, 0:TPB * E].rearrange("p (t e) -> p t e", t=TPB)
                for t in range(TPB):
                    nc.tensor.matmul(pos[:, t, :], ones[:, :], countb[:, :], start=True, stop=False)
                    for t2 in range(t):
                        nc.tensor.matmul(pos[:, t, :], ones[:, :], M[:, t2, :], start=False, stop=False)
                    mm = nc.tensor.matmul(pos[:, t, :], tri[:, :], M[:, t, :], start=False, stop=True)
                tok = c.pe.mark(mm)
                v = nc.vector
                c.vec.need(tok)
                a = c.vec.mark(v.tensor_tensor(slot[:, :, :], pos, iexp[:, None, :].broadcast_to([P, TPB, E]), ALU.add))
                b_ = c.vec.mark(v.tensor_scalar(far[:, :, :], pos, float(CAP), BIG, ALU.is_ge, ALU.mult))
                gen.give(bi, b_)
                c.vec.need(b_)
                a = c.vec.mark(v.tensor_tensor(slot[:, :, :], slot[:, :, :], far[:, :, :], ALU.max))
                d = c.vec.mark(v.tensor_reduce(sum4[:, :], M[:, :, :].rearrange("p t e -> p e t"), AX.X, ALU.add))
                c.vec.need(d)
                d = c.vec.mark(v.tensor_tensor(count[:, :], count[:, :], sum4[:, :], ALU.add))
                c.vec.need(d)
                d = c.vec.mark(v.tensor_copy(countb[:, :], count[:, :]))
                held["pos"] = (d,)
                shape = [P, TPB, TOPK, E]
                a = c.vec.mark(v.tensor_tensor(eq[:, :, :, :], iexp[:, None, None, :].broadcast_to(shape),
                                               idxf[:, :, :, None].broadcast_to(shape), ALU.is_equal))
                c.vec.need(a)
                a = c.vec.mark(v.tensor_tensor(eq[:, :, :, :], eq[:, :, :, :],
                                               slot[:, :, None, :].broadcast_to(shape), ALU.mult))
                c.vec.need(a)
                a = c.vec.mark(v.tensor_reduce(slotk[:, :, :], eq[:, :, :, :], AX.X, ALU.add))
                c.vec.need(a)
                su, si, free = slotu.take()
                c.vec.need(*free)
                tk, ti, free = tokb.take()
                c.vec.need(*free)
                tl = bass.ds(g * (SEQ // P) + b * TPB, TPB)
                c.vec.mark(v.tensor_copy(R.slots[:, tl, :], slotk[:, :, :]))
                c.vec.mark(v.tensor_copy(tk[:, :], tokf[:, :]))
                a = c.vec.mark(v.tensor_copy(su[:, :, :], slotk[:, :, :]))
                c.vec.need(a)
                c.vec.mark(v.tensor_scalar(tokf[:, :], tokf[:, :], float(BLK), None, ALU.add))
                k = c.vec.mark(v.tensor_scalar(kept[:, :, :], slotk[:, :, :], BIG, K.tg[:, 2:3], ALU.is_lt, ALU.mult))
                c.vec.need(k)
                k = c.vec.mark(v.tensor_tensor(R.weights[:, tl, :], w8[:, :, :], kept[:, :, :], ALU.mult))
                held["route"] = (k, tok)
                c.pool.need(a)
                for t in range(TPB):
                    for j in range(TOPK):
                        s_ = psc[si].mark(nc.gpsimd.indirect_dma_start(
                            ids, bass.IndirectOffsetOnAxis(su[:, t, j:j + 1], 0), tk[:, t:t + 1], None,
                            bounds_check=SLOTS - 1, oob_is_err=False))
                slotu.give(si, s_)
                tokb.give(ti, s_)

            def up(b, f):
                w = blocks[b]
                bank, bi, free = gu.take()
                c.pe.need(*free)
                for j in range(2):
                    o = j * IS + f * P
                    mm = split3(c, bank[:, j, :], lambda h, k: wgu[:, h, k, o:o + P],
                                lambda h, k: w["zT"][:, h, k, :], range(KT))
                tok = c.pe.mark(mm)
                si_, sii, free = silu.take()
                c.act.need(*free)
                c.act.need(tok)
                s_ = c.act.mark(nc.scalar.activation(si_[:, :], bank[:, 0, :], ACT.Silu, scale=1.0 / WS))
                a_, ai, free = act32.take()
                c.vec.need(*free)
                c.vec.need(s_, tok)
                a = c.vec.mark(nc.vector.scalar_tensor_tensor(a_[:, :], bank[:, 1, :], 1.0 / WS, si_[:, :],
                                                              ALU.mult, ALU.mult))
                gu.give(bi, s_, a)
                silu.give(sii, a)
                c.act.need(a, *(held["actT"] if f == 0 else ()))
                hi = c.act.mark(nc.scalar.copy(actT[:, 0, f, :], a_[:, :]))
                w["a"] = (a_, ai, hi, f)
                if f == FB - 1:
                    nrm.zT.give(w["zi"], tok)

            def low(b):
                a_, ai, hi, f = blocks[b]["a"]
                c.vec.need(hi)
                lo = c.vec.mark(nc.vector.tensor_tensor(actT[:, 1, f, :], a_[:, :], actT[:, 0, f, :], ALU.subtract))
                act32.give(ai, lo)
                blocks[b]["lo"] = lo

            def down(b):
                w = blocks[b]
                x = w["x"]
                c.pe.need(w["lo"])
                for t in range(TPB):
                    bank, bi, free = gen.take()
                    c.pe.need(*free)
                    mm = split3(c, bank[:, :], lambda h, k: actT[:, h, k, t * P:(t + 1) * P],
                                lambda h, k: wdn[:, h, k, :], range(FB))
                    tok = c.pe.mark(mm)
                    c.vec.need(tok, w["sg"])
                    out = c.vec.mark(nc.vector.scalar_tensor_tensor(x[:, t, :], bank[:, :], sg[:, t:t + 1],
                                                                    x[:, t, :], ALU.mult, ALU.add))
                    gen.give(bi, out)
                held["actT"] = (tok,)
                c.sp.need(out)
                st = pst[w["xi"]].mark(nc.sync.dma_start(
                    dst[bass.ds(w["row"], BLK), :].rearrange("(t p) d -> p t d", p=P), x[:, :, :]))
                nrm.x.give(w["xi"], st)

            load(0)
            statistics(c, K, nrm, blocks[0])
            for t in range(TPB):
                keep_rows(0, t)
                turn_rows(0, t)
            logits(0)
            choose(0)
            for b in range(NBB):
                nxt = b + 1 < NBB
                if nxt:
                    load(b + 1)
                for f in range(FB):
                    up(b, f)
                    if f == 1:
                        positions(b)
                    if nxt and f == 3:
                        statistics(c, K, nrm, blocks[b + 1])
                    if nxt and f >= 4:
                        keep_rows(b + 1, f - 4)
                    if nxt and f >= 5:
                        turn_rows(b + 1, f - 5)
                    low(b)
                if nxt:
                    turn_rows(b + 1, 3)
                    logits(b + 1)
                down(b)
                if nxt:
                    choose(b + 1)
            c.meet()


def experts(c, K, I, zrows, ids, oute):
    nc = c.nc
    with ExitStack() as ctx:
        sb = lambda n, s, d: ctx.enter_context(nc.sbuf_tensor(f"ex_{n}", s, d))
        port = lambda n: c.port(f"ex_{n}")
        ps = lambda n, s: ctx.enter_context(nc.psum_tensor(f"ex_{n}", s, F32))
        NS = CAP // P
        EK = EI // P
        tr = Ring([ps(f"t{i}", [P, 512]) for i in range(2)])
        gu = Ring([ps(f"gu{i}", [P, 2, 512]) for i in range(2)])
        ob = Ring([ps(f"o{i}", [P, 512]) for i in range(2)])
        rows, idxu = sb("rows", [P, P], F32), sb("idxu", [P, E * NS], U32)
        cols = sb("cols", [P, EPL * NS], U32)
        st1 = Ring([sb(f"w1_{i}", [P, KT, 2 * EI], F32) for i in range(3)])
        st2 = Ring([sb(f"w2_{i}", [P, EK, D], F32) for i in range(3)])
        w1 = Ring([sb(f"h1_{i}", [P, 2, KT, 2 * EI], F16) for i in range(2)])
        w2 = Ring([sb(f"h2_{i}", [P, 2, EK, D], F16) for i in range(3)])
        xg = Ring([sb(f"xg{i}", [P, 2, KT, P], F16) for i in range(4)])
        xT = Ring([sb(f"xT{i}", [P, 2, KT, CAP], F16) for i in range(2)])
        silu, a32 = (Ring([sb(f"{n}{i}", [P, EK, CAP], F32) for i in range(2)]) for n in ("si", "a"))
        aT = Ring([sb(f"aT{i}", [P, 2, EK, CAP], F16) for i in range(2)])
        o32 = Ring([sb(f"oo{i}", [P, NS, D], F32) for i in range(2)])
        p1, p2 = [port(f"w1{i}") for i in range(3)], [port(f"w2{i}") for i in range(3)]
        px, po, pi = [c.soft_port(f"ex_x{i}", 16 * EPL * NS // 4) for i in range(4)], [port(f"o{i}") for i in range(2)], port("ids")
        got = pi.mark(nc.sync.dma_start(rows[:, :], ids.rearrange("(r n) a -> r (n a)", r=P)))
        c.pe.need(got)
        bank, _, free = tr.take()
        c.pe.need(*free)
        tok = c.pe.mark(nc.tensor.transpose(bank[:, 0:P], rows[:, :], K.id32[:, :]))
        c.vec.need(tok)
        c.vec.mark(nc.vector.tensor_copy(idxu[:, :], bank[:, 0:P]))
        c.meet()
        with nc.Fori(0, E // EPL) as g:
            for r in (tr, gu, ob, st1, st2, w1, w2, xg, xT, silu, a32, aT, o32):
                r.reset()
            for q in px:
                q.turn(g)
            ci = c.vec.mark(nc.vector.tensor_copy(cols[:, :], idxu[:, bass.ds(g * (EPL * NS), EPL * NS)]))
            ex = {}

            def fetch(e):
                q = ex[e] = {}
                q["s1"], q["i1"], free = st1.take()
                c.sp.need(*free)
                q["g1"] = p1[q["i1"]].mark(nc.sync.dma_start(
                    q["s1"][:, :, :], I["L0_ffn_expert_gate_up_w"][bass.ds(g * EPL + e, 1), :, :]
                    .rearrange("a (k p) n -> p (a k) n", p=P)))
                q["s2"], q["i2"], free = st2.take()
                c.sp.need(*free)
                q["g2"] = p2[q["i2"]].mark(nc.sync.dma_start(
                    q["s2"][:, :, :], I["L0_ffn_expert_down_w"][bass.ds(g * EPL + e, 1), :, :]
                    .rearrange("a (k p) n -> p (a k) n", p=P)))
                q["x"] = []
                for s in range(NS):
                    x, xi, free = xg.take()
                    c.pool.need(*free)
                    c.pool.need(ci)
                    n = e * NS + s
                    gx = px[xi].mark(nc.gpsimd.indirect_dma_start(
                        x[:, :, :, :].rearrange("p h k n -> p (h k n)"), None, zrows,
                        bass.IndirectOffsetOnAxis(cols[:, n:n + 1], 0)))
                    q["x"].append((x, xi, gx))

            def split_weights(e):
                q = ex[e]
                q["w1"], q["j1"], free = w1.take()
                c.act.need(q["g1"], *free)
                q["w1r"] = []
                for k in range(0, KT, 2):
                    h1 = c.act.mark(nc.scalar.activation(q["w1"][:, 0, k:k + 2, :], q["s1"][:, k:k + 2, :],
                                                         ACT.Copy, scale=WS))
                    c.vec.need(h1)
                    q["w1r"].append(c.vec.mark(nc.vector.scalar_tensor_tensor(
                        q["w1"][:, 1, k:k + 2, :], q["s1"][:, k:k + 2, :], WS, q["w1"][:, 0, k:k + 2, :],
                        ALU.mult, ALU.subtract)))
                st1.give(q["i1"], q["w1r"][-1])
                q["w2"], q["j2"], free = w2.take()
                c.act.need(q["g2"], *free)
                h2 = c.act.mark(nc.scalar.activation(q["w2"][:, 0, :, :], q["s2"][:, :, :], ACT.Copy, scale=WS))
                c.vec.need(h2)
                q["w2r"] = c.vec.mark(nc.vector.scalar_tensor_tensor(
                    q["w2"][:, 1, :, :], q["s2"][:, :, :], WS, q["w2"][:, 0, :, :], ALU.mult, ALU.subtract))
                st2.give(q["i2"], q["w2r"])

            def turn_rows(e):
                q = ex[e]
                xt, q["xti"], xT_free = xT.take()
                q["xT"], q["xTr"] = xt, []
                for s, (x, xi, gx) in enumerate(q["x"]):
                    bank, bi, free = tr.take()
                    c.pe.need(gx, *free)
                    turned = bank[:, :].bitcast(F16).rearrange("p (h k n) -> p h k n", h=2, k=KT)
                    for h in range(2):
                        for k in range(KT):
                            mm = nc.tensor.transpose(turned[:, h, k, :], x[:, h, k, :], K.id16[:, :])
                    tok = c.pe.mark(mm)
                    xg.give(xi, tok)
                    en = c.act if s == 0 else c.vec
                    en.need(tok, *xT_free)
                    d_ = xt[:, :, :, s * P:(s + 1) * P]
                    out = en.mark(nc.scalar.copy(d_, turned) if s == 0 else nc.vector.tensor_copy(d_, turned))
                    tr.give(bi, out)
                    q["xTr"].append(out)

            def up(e):
                q = ex[e]
                bank, bi, free = gu.take()
                c.pe.need(*q["xTr"], *q["w1r"], *free)
                for f in range(2 * EK):
                    mm = split3(c, bank[:, f // EK, (f % EK) * CAP:(f % EK + 1) * CAP],
                                lambda h, k: q["w1"][:, h, k, f * P:(f + 1) * P],
                                lambda h, k: q["xT"][:, h, k, :], range(KT))
                q["up"] = tok = c.pe.mark(mm)
                w1.give(q["j1"], tok)
                xT.give(q["xti"], tok)
                q["bank"], q["bi"] = bank, bi

            def activate(e):
                q = ex[e]
                si_, sii, free = silu.take()
                c.act.need(q["up"], *free)
                G, U = (q["bank"][:, j, :].rearrange("p (k n) -> p k n", k=EK) for j in range(2))
                s_ = c.act.mark(nc.scalar.activation(si_[:, :, :], G, ACT.Silu, scale=1.0 / WS))
                a_, ai, free = a32.take()
                c.vec.need(s_, *free)
                a = c.vec.mark(nc.vector.scalar_tensor_tensor(a_[:, :, :], U, 1.0 / WS, si_[:, :, :],
                                                              ALU.mult, ALU.mult))
                gu.give(q["bi"], s_, a)
                silu.give(sii, a)
                at, ati, free = aT.take()
                c.act.need(a, *free)
                hi = c.act.mark(nc.scalar.copy(at[:, 0, :, :], a_[:, :, :]))
                c.vec.need(hi)
                q["aTr"] = c.vec.mark(nc.vector.tensor_tensor(at[:, 1, :, :], a_[:, :, :], at[:, 0, :, :],
                                                              ALU.subtract))
                a32.give(ai, q["aTr"])
                q["aT"], q["ati"] = at, ati

            def down(e):
                q = ex[e]
                c.pe.need(q["aTr"], q["w2r"])
                o, oi, free = o32.take()
                c.act.need(*free)
                for s in range(NS):
                    bank, bi, free = ob.take()
                    c.pe.need(*free)
                    mm = split3(c, bank[:, :], lambda h, k: q["aT"][:, h, k, s * P:(s + 1) * P],
                                lambda h, k: q["w2"][:, h, k, :], range(EK))
                    tok = c.pe.mark(mm)
                    c.act.need(tok)
                    out = c.act.mark(nc.scalar.activation(o[:, s, :], bank[:, :], ACT.Copy, scale=1.0 / WS))
                    ob.give(bi, out)
                w2.give(q["j2"], tok)
                aT.give(q["ati"], tok)
                c.sp.need(out)
                st = po[oi].mark(nc.sync.dma_start(
                    oute[bass.ds((g * EPL + e) * CAP, CAP), :].rearrange("(s p) d -> p s d", p=P), o[:, :, :]))
                o32.give(oi, st)

            fetch(0)
            fetch(1)
            split_weights(0)
            turn_rows(0)
            fetch(2)
            up(0)
            split_weights(1)
            turn_rows(1)
            activate(0)
            for e in range(EPL):
                if e + 1 < EPL:
                    up(e + 1)
                if e + 3 < EPL:
                    fetch(e + 3)
                if e + 2 < EPL:
                    split_weights(e + 2)
                    turn_rows(e + 2)
                if e + 1 < EPL:
                    activate(e + 1)
                down(e)
            c.meet()


class ReturnBuffers:

    def __init__(self, c, ctx):
        nc = c.nc
        sb = lambda n, s, d: ctx.enter_context(nc.sbuf_tensor(f"rt_{n}", s, d))
        self.rows = Ring([sb(f"g{i}", [P, TOPK, D], F32) for i in range(2)])
        self.slots, self.weights = sb("at", [P, TPB, TOPK], U32), sb("w", [P, TPB, TOPK], F32)
        self.ports = [[c.soft_port(f"rt_p{i}{h}", 16 * TOPK // 2 * TPB * NBB // 2) for h in range(2)]
                      for i in range(2)]
        for b in self.rows.bufs:
            c.vec.mark(nc.vector.memset(b[:, :, :], 0.0))

    def turn(self, g):
        self.rows.reset()
        self.gathered, self.added = (), ()
        for q in self.ports[0] + self.ports[1]:
            q.turn(g)


def begin_returns(c, R, rb, w):
    nc = c.nc
    c.vec.need(*rb.gathered, *rb.added)
    w["slots"] = c.vec.mark(nc.vector.tensor_copy(rb.slots[:, :, :], R.slots[:, bass.ds(w["tile"], TPB), :]))
    w["weights"] = c.vec.mark(nc.vector.tensor_copy(rb.weights[:, :, :], R.weights[:, bass.ds(w["tile"], TPB), :]))


def gather_tile(c, rb, oute, w, t, ks):
    if ks[0] == 0:
        buf, bi, free = rb.rows.take()
        c.pool.need(w["slots"], *free)
        w["rows", t] = (buf, bi, {})
    buf, bi, got = w["rows", t]
    for k in ks:
        half = k // (TOPK // 2)
        got[half] = rb.ports[bi][half].mark(c.nc.gpsimd.indirect_dma_start(
            buf[:, k, :], None, oute, bass.IndirectOffsetOnAxis(rb.slots[:, t, k:k + 1], 0),
            bounds_check=SLOTS - 1, oob_is_err=False))
    rb.gathered = tuple(got.values())


def add_tile(c, rb, w, t, ks):
    x = w["x"]
    buf, bi, got = w["rows", t]
    c.vec.need(w["got"], w["weights"])
    for k in ks:
        if k % (TOPK // 2) == 0:
            c.vec.need(got[k // (TOPK // 2)])
        a = c.vec.mark(c.nc.vector.scalar_tensor_tensor(x[:, t, :], buf[:, k, :], rb.weights[:, t, k:k + 1],
                                                        x[:, t, :], ALU.mult, ALU.add))
        c.vec.need(a)
    if ks[-1] == TOPK - 1:
        rb.rows.give(bi, a)
    rb.added = (a,)


def fused_experts(c, K, I, src, dst):
    nc = c.nc
    PS = 1.0 / 64.0
    with ExitStack() as ctx:
        sb = lambda n, s, d: ctx.enter_context(nc.sbuf_tensor(f"fe_{n}", s, d))
        port = lambda n: c.port(f"fe_{n}")
        ps = lambda n, s: ctx.enter_context(nc.psum_tensor(f"fe_{n}", s, F32))
        gen = Ring([ps(f"g{i}", [P, 512]) for i in range(2)])
        trio = Ring([ps(f"p{i}", [P, 3, 512]) for i in range(2)])
        nrm = NormBuffers(c, ctx, "fe", gen)
        NJ = 2 * KR // P
        left, right = ([sb(f"{n}{i}", [P, 2, KT, KR], F16) for i in range(2)] for n in ("lf", "rt"))
        router = [sb(f"ro{i}", [P, 2, KT, RH], F16) for i in range(2)]
        up = sb("up", [P, 2, NJ, D], F16)
        cz = Ring([sb(f"cz{i}", [P, KT, BLK], F32) for i in range(2)])
        czs = sb("czs", [P, 2, KT, BLK], F16)
        h32 = Ring([sb(f"h{i}", [P, KT, BLK], F32) for i in range(2)])
        prodT = sb("prodT", [P, 2, NJ, BLK], F16)
        t32, p32, c32 = (Ring([sb(f"{n}{i}", [P, BLK], F32) for i in range(2)]) for n in ("t", "pp", "c"))
        r2 = sb("r2", [P, KT, KE], F32)
        b1 = sb("b1", [P, KT], F32)
        b2, b2x, alpha = sb("b2", [P, KE], F32), sb("b2x", [P, KE], F32), sb("alpha", [P, 1], F32)
        bo = sb("bo", [2 * KE, 2, D], F16)
        sel32, sel = sb("sel32", [2 * KE, NJ, P], F32), sb("sel", [2 * KE, NJ, P], F16)
        lg, ex = sb("lg", [P, TPB, 2, KE], F32), sb("exr", [P, TPB, 2, KE], F32)
        mx, sm, rs = (sb(n, [P, TPB, 2], F32) for n in ("mx", "sm", "rs"))
        wr = sb("wr", [P, TPB, 2, KE], F32)
        wT = Ring([sb(f"wT{i}", [2 * KE, 2, BLK], F16) for i in range(2)])
        ni, nf = sb("ni", [P, SEQ // P], mybir.dt.int32), sb("nf", [P, SEQ // P], F32)
        pst = [port(f"st{i}") for i in range(3)]
        psm = port("small")

        view = lambda n: I["L1_ffn_" + n].rearrange("(k p) m -> p k m", p=P)
        stages = Ring(nrm.x.bufs)
        spare = [b[:, :, :].bitcast(F16).rearrange("p k (h n) -> p h k n", h=2) for b in h32.bufs]
        wq, wk, inv, inv_q, inv_k = *nrm.zT.bufs, czs, prodT[:, :, 0:KT, :], prodT[:, :, KT:NJ, :]
        factors_ = Ring(spare)

        def fetch(name, buf, dst_free=(), width=D):
            stage, i, free = stages.take()
            used = load_split(c, stage[:, :, 0:width], nrm.px[i], lambda h: buf[:, h, :, 0:width], view(name),
                              after=free, dst_free=dst_free)
            stages.give(i, *used)
            return used

        def factor(name, width=D):
            b, i, free = factors_.take()
            return b, i, fetch(name, b, free, width)

        inv_in, q_in = fetch("W_invT", inv), fetch("W_Q", wq)
        w1, w1i, w1_in = factor("router_w1T")
        k_in = fetch("W_K", wk)
        small = lambda d_, s_: psm.mark(nc.sync.dma_start(d_, s_))
        small(r2[:, :, :], I["L1_ffn_router_w2T"].rearrange("(k p) m -> p k m", p=P))
        with nc.allow_non_contiguous_dma(reason="a bias by feature, once"):
            small(b1[:, :], I["L1_ffn_router_b1"].rearrange("(k p) -> p k", p=P))
        row = lambda n, w: I["L1_ffn_" + n].rearrange("(a n) -> a n", a=1).broadcast_to([P, w])
        small(b2[:, :], row("router_b2", KE))
        small(b2x[:, :], row("expert_bias", KE))
        sm_in = small(alpha[:, :], row("alpha_bi", 1))

        def chain(lhs, lhs_in, rhs, rhs_in, out, after=()):
            c.pe.need(*lhs_in, *rhs_in)
            for m in range(KT):
                bank, bi, free = gen.take()
                c.pe.need(*free)
                tok = c.pe.mark(split3(c, bank[:, :], lambda h, k: lhs[:, h, k, m * P:(m + 1) * P],
                                       lambda h, k: rhs[:, h, k, :], range(KT)))
                c.act.need(tok, *after)
                hi = c.act.mark(nc.scalar.activation(out(0, m), bank[:, :], ACT.Copy, scale=1.0 / WS))
                c.vec.need(hi)
                lo = c.vec.mark(nc.vector.scalar_tensor_tensor(out(1, m), bank[:, :], 1.0 / WS, out(0, m),
                                                               ALU.mult, ALU.subtract))
                gen.give(bi, lo)
            return tok, (lo,)

        into = lambda buf: lambda h, m: buf[:, h, m, :]
        chain(wq, q_in, w1, w1_in, into(router[0]))
        _, inv_q_in = chain(inv, inv_in, wq, (), into(inv_q))
        inv_read, inv_k_in = chain(inv, (), wk, k_in, into(inv_k))
        ahead = factor("V_fwd")
        tok, _ = chain(inv_q, inv_q_in, w1, (), into(router[1]))
        factors_.give(w1i, tok)
        f_, fi, f_in = ahead
        for name, lhs, lhs_in, dst_ in (("W_fwd", wq, (), left[0]), ("W_inv_exp", wk, (), right[0]),
                                        ("V_inv", inv_q, (), left[1]), ("U_fwd", inv_k, inv_k_in, right[1])):
            ahead = factor(name)
            if name == "V_inv":
                wo, wo_in = inv, fetch("W_OT", inv, (inv_read,))
            tok, _ = chain(lhs, lhs_in, f_, f_in, into(dst_))
            factors_.give(fi, tok)
            f_, fi, f_in = ahead
        for i, (name, width) in enumerate((("U_inv", D), ("bT", P))):
            ahead = factor(name, width)
            tok, _ = chain(f_, f_in, wo, wo_in, lambda h, m: up[:, h, i * KT + m, :])
            factors_.give(fi, tok)
            f_, fi, f_in = ahead
        bT, bT_in = f_, f_in
        bank, bi, free = gen.take()
        c.pe.need(*bT_in, *free)
        tok = c.pe.mark(split3(c, bank[:, :], lambda h, k: bT[:, h, k, 0:P], lambda h, k: wo[:, h, k, :], range(KT)))
        c.act.need(tok)
        hi = c.act.mark(nc.scalar.activation(bo[:, 0, :], bank[0:2 * KE, :], ACT.Copy, scale=PS / WS))
        c.vec.need(hi)
        gen.give(bi, c.vec.mark(nc.vector.scalar_tensor_tensor(bo[:, 1, :], bank[0:2 * KE, :], PS / WS, bo[:, 0, :],
                                                               ALU.mult, ALU.subtract)))
        a = c.pool.mark(nc.gpsimd.memset(sel32[:, :, :], 1.0))
        c.pool.need(a)
        a = c.pool.mark(nc.gpsimd.affine_select(out=sel32[:, :, :], in_=sel32[:, :, :], compare_op=ALU.is_ge, fill=0.0,
                                                base=0, pattern=[[P, NJ], [1, P]], channel_multiplier=-RR))
        c.pool.need(a)
        a = c.pool.mark(nc.gpsimd.affine_select(out=sel32[:, :, :], in_=sel32[:, :, :], compare_op=ALU.is_ge, fill=0.0,
                                                base=RR - 1, pattern=[[-P, NJ], [-1, P]], channel_multiplier=RR))
        b_ = c.pool.mark(nc.gpsimd.iota(ni[:, :], pattern=[[P, SEQ // P]], base=1, channel_multiplier=1))
        c.vec.need(a, b_, sm_in)
        c.vec.mark(nc.vector.tensor_copy(sel[:, :, :], sel32[:, :, :]))
        c.vec.mark(nc.vector.tensor_tensor(b2[:, :], b2[:, :], b2x[:, :], ALU.add))
        a = c.vec.mark(nc.vector.tensor_copy(nf[:, :], ni[:, :]))
        c.vec.need(a)
        a = c.vec.mark(nc.vector.reciprocal(nf[:, :], nf[:, :]))
        c.vec.need(a)
        c.vec.mark(nc.vector.tensor_scalar(nf[:, :], nf[:, :], K.tgw[:, 3:4], 1.0 / PS, ALU.mult, ALU.mult))
        c.meet()

        with nc.Fori(0, BATCH) as g:
            for r in (gen, trio, cz, h32, t32, p32, c32, wT):
                r.reset()
            nrm.reset()
            blocks, held = {}, dict(czs=(), prod=(), lg=())

            def load(b):
                row_ = g * SEQ + b * BLK
                x, xi, got = load_tokens(c, nrm, src, row_)
                blocks[b] = dict(x=x, xi=xi, got=got, row=row_)

            def running(b):
                w = blocks[b]
                s_, w["ci"], free = cz.take()
                c.vec.need(*free, *w["turned"])
                before = blocks[b - 1] if b else None
                if b:
                    c.vec.need(before["scan"])
                for k in range(KT):
                    w["scan"] = c.vec.mark(nc.vector.tensor_tensor_scan(
                        s_[:, k, :], w["zT"][:, 0, k, :], w["zT"][:, 1, k, :],
                        before["cz"][:, k, BLK - 1:BLK] if b else 0.0, ALU.add, ALU.add))
                w["cz"] = s_
                if b:
                    cz.give(before["ci"], *before["cz_used"], w["scan"])
                w["cz_used"] = ()

            def halve(b):
                w = blocks[b]
                c.act.need(w["scan"], *held["czs"])
                for k in range(KT):
                    hi = c.act.mark(nc.scalar.copy(czs[:, 0, k, :], w["cz"][:, k, :]))
                    c.pool.need(hi)
                    w["czs"] = c.pool.mark(nc.gpsimd.tensor_tensor(czs[:, 1, k, :], w["cz"][:, k, :],
                                                                   czs[:, 0, k, :], ALU.subtract))
                w["cz_used"] = (w["czs"],)

            def route(b):
                w = blocks[b]
                c.pe.need(*w["turned"])
                v = nc.vector
                c.vec.need(*held["lg"])
                hidden = []
                for r in range(2):
                    h_, hi_, free = h32.take()
                    c.act.need(*free)
                    for m in range(KT):
                        bank, bi, free = gen.take()
                        c.pe.need(*free)
                        tok = c.pe.mark(split3(c, bank[:, :], lambda h, k: router[r][:, h, k, m * P:(m + 1) * P],
                                               lambda h, k: w["zT"][:, h, k, :], range(KT)))
                        c.act.need(tok)
                        a = c.act.mark(nc.scalar.activation(h_[:, m, :], bank[:, :], ACT.Gelu, bias=b1[:, m:m + 1],
                                                            scale=1.0 / WS))
                        gen.give(bi, a)
                    hidden.append((h_, hi_, a))
                for r, (h_, hi_, a) in enumerate(hidden):
                    bank, bi, free = gen.take()
                    c.pe.need(*free)
                    c.pe.need(a)
                    for t in range(TPB):
                        for k in range(KT):
                            mm = nc.tensor.matmul(bank[:, t * KE:(t + 1) * KE], h_[:, k, t * P:(t + 1) * P],
                                                  r2[:, k, :], start=(k == 0), stop=(k == KT - 1))
                    tok = c.pe.mark(mm)
                    h32.give(hi_, tok)
                    c.vec.need(tok)
                    a = c.vec.mark(v.tensor_tensor(
                        lg[:, :, r, :], bank[:, 0:TPB * KE].rearrange("p (t e) -> p t e", t=TPB),
                        b2[:, None, :].broadcast_to([P, TPB, KE]), ALU.add))
                    gen.give(bi, a)
                shape = [P, TPB, 2, KE]
                c.vec.need(a)
                a = c.vec.mark(v.tensor_reduce(mx[:, :, :], lg[:, :, :, :], AX.X, ALU.max))
                c.vec.need(a)
                a = c.vec.mark(v.tensor_tensor(lg[:, :, :, :], lg[:, :, :, :], mx[:, :, :, None].broadcast_to(shape),
                                               ALU.subtract))
                c.act.need(a)
                e = c.act.mark(nc.scalar.activation(ex[:, :, :, :], lg[:, :, :, :], ACT.Exp))
                c.vec.need(e)
                a = c.vec.mark(v.tensor_reduce(sm[:, :, :], ex[:, :, :, :], AX.X, ALU.add))
                c.vec.need(a)
                a = c.vec.mark(v.reciprocal(rs[:, :, :], sm[:, :, :]))
                c.vec.need(a)
                a = c.vec.mark(v.tensor_scalar(rs[:, :, 1], rs[:, :, 1], alpha[:, 0:1], None, ALU.mult))
                c.vec.need(a)
                w["wr"] = c.vec.mark(v.tensor_tensor(wr[:, :, :, :], ex[:, :, :, :],
                                                     rs[:, :, :, None].broadcast_to(shape), ALU.mult))

            def turn_weights(b):
                w = blocks[b]
                bank, bi, free = gen.take()
                c.pe.need(*free)
                c.pe.need(w["wr"])
                for t in range(TPB):
                    mm = nc.tensor.transpose(bank[0:2 * KE, t * P:(t + 1) * P],
                                             wr[:, t, :, :].rearrange("p r e -> p (r e)"), K.id32[:, :])
                tok = c.pe.mark(mm)
                held["lg"] = (tok,)
                o, w["wi"], free = wT.take()
                c.act.need(*free)
                c.vec.need(*wT.was[w["wi"]])
                c.act.need(tok)
                hi = c.act.mark(nc.scalar.copy(o[:, 0, :], bank[0:2 * KE, :]))
                c.vec.need(hi)
                w["wTr"] = c.vec.mark(nc.vector.tensor_tensor(o[:, 1, :], bank[0:2 * KE, :], o[:, 0, :], ALU.subtract))
                gen.give(bi, w["wTr"])
                w["wT"] = o

            def factors(b, j):
                w = blocks[b]
                br, m = divmod(j, KT)
                bank, bi, free = trio.take()
                c.pe.need(*free)
                ms = slice(m * P, (m + 1) * P)
                split3(c, bank[:, 0, :], lambda h, k: left[br][:, h, k, ms], lambda h, k: w["zT"][:, h, k, :], range(KT))
                c.pe.need(w["czs"])
                mm = split3(c, bank[:, 1, :], lambda h, k: right[br][:, h, k, ms], lambda h, k: czs[:, h, k, :],
                            range(KT))
                tok = c.pe.mark(mm)
                if j == NJ - 1:
                    nrm.zT.give(w["zi"], tok)
                    held["czs"] = (tok,)
                c_, ci, free = c32.take()
                c.act.need(*free)
                c.act.need(tok)
                cp = c.act.mark(nc.scalar.copy(c_[:, :], bank[:, 1, :]))
                t_, ti, free = t32.take()
                c.vec.need(*free)
                c.vec.need(tok, cp)
                pr = c.vec.mark(nc.vector.tensor_tensor(t_[:, :], bank[:, 0, :], c_[:, :], ALU.mult))
                c32.give(ci, pr)
                w[j] = (bank, bi, t_, ti, pr)

            def weigh(b, j):
                w = blocks[b]
                bank, bi, t_, ti, pr = w.pop(j)
                c.pe.need(w["wTr"])
                for h in range(2):
                    mm = nc.tensor.matmul(bank[:, 2, :], sel[:, j, :], w["wT"][:, h, :], start=(h == 0), stop=(h == 1))
                tok = c.pe.mark(mm)
                p_, pi, free = p32.take()
                c.vec.need(*free)
                c.vec.need(tok, pr)
                a = c.vec.mark(nc.vector.scalar_tensor_tensor(p_[:, :], t_[:, :], PS / WS / WS, bank[:, 2, :],
                                                              ALU.mult, ALU.mult))
                trio.give(bi, a)
                t32.give(ti, a)
                c.act.need(a, *held["prod"])
                hi = c.act.mark(nc.scalar.copy(prodT[:, 0, j, :], p_[:, :]))
                c.pool.need(hi)
                lo = c.pool.mark(nc.gpsimd.tensor_tensor(prodT[:, 1, j, :], p_[:, :], prodT[:, 0, j, :], ALU.subtract))
                p32.give(pi, lo)
                w["lo"] = lo

            def finish(b):
                w = blocks[b]
                x = w["x"]
                c.pe.need(w["lo"])
                for t in range(TPB):
                    ts_ = slice(t * P, (t + 1) * P)
                    bank, bi, free = gen.take()
                    c.pe.need(*free)
                    split3(c, bank[:, :], lambda h, j: prodT[:, h, j, ts_], lambda h, j: up[:, h, j, :], range(NJ),
                           stop=False)
                    mm = split3(c, bank[:, :], lambda h, k: w["wT"][:, h, ts_], lambda h, k: bo[:, h, :], [0],
                                start=False)
                    tok = c.pe.mark(mm)
                    c.vec.need(tok)
                    n_ = b * TPB + t
                    out = c.vec.mark(nc.vector.scalar_tensor_tensor(x[:, t, :], bank[:, :], nf[:, n_:n_ + 1],
                                                                    x[:, t, :], ALU.mult, ALU.add))
                    gen.give(bi, out)
                held["prod"] = (tok,)
                wT.give(w["wi"], tok)
                c.sp.need(out)
                st = pst[w["xi"]].mark(nc.sync.dma_start(
                    dst[bass.ds(w["row"], BLK), :].rearrange("(t p) d -> p t d", p=P), x[:, :, :]))
                nrm.x.give(w["xi"], st)

            load(0)
            statistics(c, K, nrm, blocks[0])
            for t in range(0, TPB, 2):
                for t_ in (t, t + 1):
                    high_half(c, nrm, blocks[0], t_)
                for t_ in (t, t + 1):
                    low_half(c, nrm, blocks[0], t_, c.vec)
                for t_ in (t, t + 1):
                    turn_tile(c, K, nrm, blocks[0], t_)
            running(0)
            halve(0)
            route(0)
            for b in range(NBB):
                nxt = b + 1 < NBB
                if nxt:
                    load(b + 1)
                factors(b, 0)
                turn_weights(b)
                weigh(b, 0)
                for j in range(1, NJ):
                    factors(b, j)
                    if nxt and j == 2:
                        statistics(c, K, nrm, blocks[b + 1])
                    if nxt and 3 <= j < 3 + TPB:
                        halves(c, nrm, blocks[b + 1], j - 3, c.vec)
                    weigh(b, j)
                    if nxt and j >= 4:
                        turn_tile(c, K, nrm, blocks[b + 1], j - 4)
                if nxt:
                    running(b + 1)
                    halve(b + 1)
                    route(b + 1)
                finish(b)
            c.meet()


def program(nc, I, out):
    scratch = lambda n, s, d: nc.dram_tensor(n, s, d, kind="Internal").ap()
    x1, xp, x3 = (scratch(n, (T, D), F32) for n in ("x1", "xp", "x3"))
    zrows, ids = scratch("zrows", (T, 2 * D), F16), scratch("ids", (SLOTS, 1), F32)
    oute = scratch("oute", (SLOTS, D), F32)
    with ExitStack() as ctx:
        c = Core(nc, ctx)
        K = constants(c, ctx, I)
        R = Routing(nc, ctx)
        attention(c, K, I, 0, I["x"], x1)
        shared_and_route(c, K, I, R, x1, xp, zrows, ids)
        experts(c, K, I, zrows, ids, oute)
        attention(c, K, I, 1, xp, x3, R=R, oute=oute)
        fused_experts(c, K, I, x3, out)


def layout(inputs):
    import numpy as np

    a = {n: np.asarray(v) for n, v in inputs.items()}
    out = {"x": a["x"].reshape(T, D), "mask": a["mask_Bx1xSxS2_ik1"].reshape(T, CTX)}
    ctxT = a["ctx_1024"].transpose(0, 2, 1)
    out["ctxT"] = ctxT
    rem = np.zeros((BATCH, D, HG, HD), ctxT.dtype)
    rem[:, :, :, 0:REM] = ctxT[:, :, None, P:CTX]
    out["ctxR"] = rem.reshape(BATCH, D, P)
    for n in ("g_xattn", "g_ffn", "L0_xattn_bq", "L0_xattn_bk", "L0_xattn_bv", "L0_xattn_bo"):
        out[n] = a[n]
    for n in ("L0_xattn_wq", "L0_xattn_wk", "L0_xattn_wv", "L0_xattn_wo",
              "L1_xattn_wq", "L1_xattn_wk", "L1_xattn_wv", "L1_ffn_W_O", "L1_ffn_W_inv", "L1_ffn_router_w1",
              "L1_ffn_router_w2"):
        out[n + "T"] = a[n].T
    out["gates65"] = np.concatenate([a["L0_ffn_gate_w"], a["L0_ffn_shared_gate_w"]], axis=1)
    for n in ("L0_ffn_shared_gate_up_w", "L0_ffn_shared_down_w", "L0_ffn_expert_gate_up_w", "L0_ffn_expert_down_w",
              "L1_ffn_W_Q", "L1_ffn_W_K", "L1_ffn_router_b1", "L1_ffn_router_b2",
              "L1_ffn_expert_bias"):
        out[n] = a[n]
    out["L1_ffn_alpha_bi"] = a["L1_ffn_alpha_bi"].reshape(1)
    for n in ("V_fwd", "W_fwd", "U_fwd", "V_inv", "W_inv_exp", "U_inv"):
        out["L1_ffn_" + n] = a["L1_ffn_" + n].transpose(1, 0, 2).reshape(D, KR)
    bT = np.zeros((D, P), a["L1_ffn_b_fwd"].dtype)
    bT[:, 0:KE], bT[:, KE:2 * KE] = a["L1_ffn_b_fwd"].T, a["L1_ffn_b_inv"].T
    out["L1_ffn_bT"] = bT
    return {n: np.ascontiguousarray(v) for n, v in out.items()}


def kernel(**inputs):
    import concourse.bacc as _bacc
    from concourse.bass_utils import run_bass_kernel_spmd as _run

    nc = _bacc.Bacc("TRN2", target_bir_lowering=False, num_devices=1)
    arrays = layout(inputs)
    I = {n: nc.dram_tensor(n, v.shape, mybir.dt.from_np(v.dtype), kind="ExternalInput").ap()
         for n, v in arrays.items()}
    out = nc.dram_tensor("out", (T, D), F32, kind="ExternalOutput").ap()
    program(nc, I, out)
    r = _run(nc, [arrays], core_ids=[0])
    return r.results[0]["out"].reshape(BATCH, SEQ, D)
```
